# Optimizing a Trainium2 kernel written in Bass

```python
import numpy as np
import jax
import jax.numpy as jnp

def _softmax(x, axis=-1):
    return jax.nn.softmax(x, axis=axis)

def _gelu(x):
    return jax.nn.gelu(x, approximate=True)

def _silu(x):
    return jax.nn.silu(x)

def _sigmoid(x):
    return jax.nn.sigmoid(x)

def _layernorm(x, axis=-1, eps=1e-05):
    m = jnp.mean(x, axis=axis, keepdims=True)
    v = jnp.var(x, axis=axis, keepdims=True)
    return (x - m) / jnp.sqrt(v + eps)

def _scatter_add(tgt, idx, src, axis=0):
    return tgt.at[idx].add(src)

def _segment_sum(src, seg, n):
    return jax.ops.segment_sum(src, seg, n)
kernel_name = 'mk_gnn_ffn_d1_gnn_r8_726913'

def setup_inputs(seed: int=0):
    np.random.seed(seed)
    _w = jnp.asarray

    def _rec_inputs():
        import jax
        import jax.numpy as jnp
        _gk = jax.random.key(seed)
        x = -0.0003713 + 1 * jax.random.normal(jax.random.fold_in(_gk, 1), (6250, 256), jnp.float32)
        src = jax.random.randint(jax.random.fold_in(_gk, 2), (100000,), 0, 6250, jnp.int32)
        dst = jax.random.randint(jax.random.fold_in(_gk, 3), (100000,), 0, 6250, jnp.int32)
        _o = jnp.argsort(dst, stable=True)
        src = src[_o]
        dst = dst[_o]
        return (x, src, dst)
    x, src, dst = _rec_inputs()

    def _L0_gnn_setup():
        import jax, jax.numpy as jnp
        import numpy as np
        N_NODES = 6250
        N_EDGES = 100000
        IN_CH = 256
        HID_CH = 256
        OUT_CH = 256
        N_LAYERS = 3
        key = jax.random.key(seed)
        ks = jax.random.split(key, 8)
        s_in = 1.0 / np.sqrt(IN_CH)
        s_h = 1.0 / np.sqrt(HID_CH)
        return {'x': jax.random.normal(ks[0], (N_NODES, IN_CH), dtype=jnp.float32), 'W_in': jax.random.normal(ks[1], (IN_CH, HID_CH), dtype=jnp.float32) * s_in, 'b_in': jnp.zeros((HID_CH,), dtype=jnp.float32), 'W_agg': jax.random.normal(ks[2], (N_LAYERS, HID_CH, HID_CH), dtype=jnp.float32) * s_h, 'W_self': jax.random.normal(ks[3], (N_LAYERS, HID_CH, HID_CH), dtype=jnp.float32) * s_h, 'b_hid': jnp.zeros((N_LAYERS, HID_CH), dtype=jnp.float32), 'W_out': jax.random.normal(ks[4], (HID_CH, OUT_CH), dtype=jnp.float32) * s_h, 'b_out': jnp.zeros((OUT_CH,), dtype=jnp.float32), 'edge_index': jax.random.randint(ks[5], (2, N_EDGES), 0, N_NODES, dtype=jnp.int64)}
    _L0_gnn_all = _L0_gnn_setup()
    _L0_gnn_in = {k: v for k, v in _L0_gnn_all.items() if k in ('W_in', 'b_in', 'W_agg', 'W_self', 'b_hid', 'W_out', 'b_out')}
    del _L0_gnn_all

    def _L0_ffn_setup():
        import jax, jax.numpy as jnp
        import numpy as np
        E, D, H, TOP_K = (6, 256, 256, 2)
        ROUTER_H = D // 2
        key = jax.random.key(seed)
        ks = jax.random.split(key, 12)
        s = 1.0 / np.sqrt(D)
        sh = 1.0 / np.sqrt(H)
        sr = 1.0 / np.sqrt(ROUTER_H)
        return {'features': jax.random.normal(ks[0], (8, 512, D), dtype=jnp.float32), 'router_w1': jax.random.uniform(ks[1], (D, ROUTER_H), jnp.float32, -s, s), 'router_b1': jnp.zeros((ROUTER_H,), jnp.float32), 'router_w2': jax.random.uniform(ks[2], (ROUTER_H, E), jnp.float32, -sr, sr), 'router_b2': jnp.zeros((E,), jnp.float32), 'expert_w1': jax.random.uniform(ks[3], (E, D, H), jnp.float32, -s, s), 'expert_b1': jnp.zeros((E, H), jnp.float32), 'expert_w2': jax.random.uniform(ks[4], (E, H, H), jnp.float32, -sh, sh), 'expert_b2': jnp.zeros((E, H), jnp.float32), 'expert_w3': jax.random.uniform(ks[5], (E, H, D), jnp.float32, -sh, sh), 'expert_b3': jnp.zeros((E, D), jnp.float32)}
    _L0_ffn_all = _L0_ffn_setup()
    _L0_ffn_in = {k: v for k, v in _L0_ffn_all.items() if k in ('router_w1', 'router_b1', 'router_w2', 'router_b2', 'expert_w1', 'expert_b1', 'expert_w2', 'expert_b2', 'expert_w3', 'expert_b3')}
    del _L0_ffn_all
    return {'x': x, 'src': src, 'dst': dst, 'L0_gnn_W_in': _L0_gnn_in['W_in'], 'L0_gnn_b_in': _L0_gnn_in['b_in'], 'L0_gnn_W_agg': _L0_gnn_in['W_agg'], 'L0_gnn_W_self': _L0_gnn_in['W_self'], 'L0_gnn_b_hid': _L0_gnn_in['b_hid'], 'L0_gnn_W_out': _L0_gnn_in['W_out'], 'L0_gnn_b_out': _L0_gnn_in['b_out'], 'L0_ffn_router_w1': _L0_ffn_in['router_w1'], 'L0_ffn_router_b1': _L0_ffn_in['router_b1'], 'L0_ffn_router_w2': _L0_ffn_in['router_w2'], 'L0_ffn_router_b2': _L0_ffn_in['router_b2'], 'L0_ffn_expert_w1': _L0_ffn_in['expert_w1'], 'L0_ffn_expert_b1': _L0_ffn_in['expert_b1'], 'L0_ffn_expert_w2': _L0_ffn_in['expert_w2'], 'L0_ffn_expert_b2': _L0_ffn_in['expert_b2'], 'L0_ffn_expert_w3': _L0_ffn_in['expert_w3'], 'L0_ffn_expert_b3': _L0_ffn_in['expert_b3']}

def reference(x, src, dst, L0_gnn_W_in, L0_gnn_b_in, L0_gnn_W_agg, L0_gnn_W_self, L0_gnn_b_hid, L0_gnn_W_out, L0_gnn_b_out, L0_ffn_router_w1, L0_ffn_router_b1, L0_ffn_router_w2, L0_ffn_router_b2, L0_ffn_expert_w1, L0_ffn_expert_b1, L0_ffn_expert_w2, L0_ffn_expert_b2, L0_ffn_expert_w3, L0_ffn_expert_b3):
    import jax
    import jax.numpy as jnp

    def _L0_gnn_ref(x, W_in, b_in, W_agg, W_self, b_hid, W_out, b_out, edge_index):
        import jax, jax.numpy as jnp
        import numpy as np
        N_NODES = 6250
        N_EDGES = 100000
        IN_CH = 256
        HID_CH = 256
        OUT_CH = 256
        N_LAYERS = 3
        n = x.shape[0]
        dst = edge_index[0]
        src = edge_index[1]
        n_layers = W_agg.shape[0]
        h = x @ W_in + b_in
        deg = jax.ops.segment_sum(jnp.ones_like(dst, dtype=h.dtype), dst, num_segments=n)
        deg = jnp.maximum(deg, 1.0)[:, None]
        for l in range(n_layers):
            agg = jax.ops.segment_sum(h[src], dst, num_segments=n) / deg
            h = jax.nn.relu(agg @ W_agg[l] + h @ W_self[l] + b_hid[l])
        return h @ W_out + b_out

    def _L0_ffn_ref(features, router_w1, router_b1, router_w2, router_b2, expert_w1, expert_b1, expert_w2, expert_b2, expert_w3, expert_b3):
        import jax, jax.numpy as jnp
        import numpy as np
        E, D, H, TOP_K = (6, 256, 256, 2)
        ROUTER_H = D // 2
        rh = jax.nn.relu(features @ router_w1 + router_b1)
        expert_logits = jax.nn.softmax(rh @ router_w2 + router_b2, axis=-1)
        top_w, top_i = jax.lax.top_k(expert_logits, TOP_K)
        routing_weights = jax.nn.softmax(top_w, axis=-1)
        h1 = jax.nn.relu(jnp.einsum('bsd,edh->bseh', features, expert_w1) + expert_b1)
        h2 = jax.nn.relu(jnp.einsum('bseh,ehf->bsef', h1, expert_w2) + expert_b2)
        expert_out = jnp.einsum('bsef,efo->bseo', h2, expert_w3) + expert_b3
        sel = jnp.take_along_axis(expert_out, top_i[:, :, :, None], axis=2)
        combined = jnp.sum(sel * routing_weights[..., None], axis=2)
        return combined
    edge_index = jnp.stack([src, dst])
    x = x + _L0_gnn_ref(_layernorm(x, axis=-1), L0_gnn_W_in, L0_gnn_b_in, L0_gnn_W_agg, L0_gnn_W_self, L0_gnn_b_hid, L0_gnn_W_out, L0_gnn_b_out, edge_index)
    x = x + _L0_ffn_ref(_layernorm(x, axis=-1)[None], L0_ffn_router_w1, L0_ffn_router_b1, L0_ffn_router_w2, L0_ffn_router_b2, L0_ffn_expert_w1, L0_ffn_expert_b1, L0_ffn_expert_w2, L0_ffn_expert_b2, L0_ffn_expert_w3, L0_ffn_expert_b3)[0]
    return x

_drawn_inputs = setup_inputs


def setup_inputs(seed=0):
    import zlib

    import numpy as np

    out = dict(_drawn_inputs(seed))
    spreads = {'L0_gnn_b_in': (0.0, 0.1),
     'L0_gnn_b_hid': (0.0, 0.1),
     'L0_gnn_b_out': (0.0, 0.1),
     'L0_ffn_router_b1': (0.0, 0.1),
     'L0_ffn_router_b2': (0.0, 0.1),
     'L0_ffn_expert_b1': (0.0, 0.783),
     'L0_ffn_expert_b2': (0.0, 0.337),
     'L0_ffn_expert_b3': (0.0, 0.1)}
    factors = {}
    for name, (base, spread) in spreads.items():
        noise = np.random.default_rng([zlib.crc32(name.encode()), seed]).standard_normal(out[name].shape)
        drawn = base * np.exp(spread * noise) if base else spread * noise
        out[name] = jnp.asarray(drawn.astype(out[name].dtype))
    for name, factor in factors.items():
        out[name] = (out[name] * factor).astype(out[name].dtype)
    return out
```

```python
from contextlib import ExitStack

import concourse.bass as bass
from concourse import mybir

ACT = mybir.ActivationFunctionType
ALU = mybir.AluOpType
AX = mybir.AxisListType
F32 = mybir.dt.float32
F16 = mybir.dt.float16
I32 = mybir.dt.int32

P = 128
NODES = 6250
EDGES = 100000
C = 256
KC = C // P
LAYERS = 3
EXPERTS = 6
TOP_K = 2
EPS = 1e-5

NT = -(-NODES // P)
BODY = 7
BODIES = NT // BODY
PAIRS = [(0, 2), (2, 4), (4, 6), (6, 7)]
NPAIR = len(PAIRS)

COLS = 784
SLOTS = EDGES // P + NT + 3
RING = 17
STEPS = SLOTS // RING
HALF = 9
HALVES = [(0, HALF), (HALF, RING)]
AW = C + 1
PERM = 8
PW = SLOTS + 1
CUT = 512
SORT_STEPS = 28
PE_COLS = 448
SC_COLS = COLS - PE_COLS
SC_RING = SC_COLS // SORT_STEPS
SC_HALF = SC_RING // 2
assert PE_COLS % PERM == 0 and SC_COLS == SORT_STEPS * 2 * SC_HALF
assert NT == BODIES * BODY == STEPS and SLOTS == STEPS * RING and COLS % PERM == 0

FH = BODY * P // 2


def bank_of(b):
    return b % 4 if b < RING - 1 else 4


def cum_of(b):
    return b % 2 if b < BODY - 1 else 2


T_BANK = [0, 1, 0, 1]
M_BANK = [2, 3, 4, 2]
G_BANK = [5, 6, 7, 5]


def t_freed(n, q):
    return n * NPAIR + (0 if q < 2 else q - 1)


def gnn_moe(nc, x, tgt, gat, w_in, b_in, w_agg, w_self, b_hid, w_out, b_out,
            r_w1, r_b1, r_w2, r_b2, e_w1, e_b1, e_w2, e_b2, e_w3, e_b3, out):
    g_dram = nc.dram_tensor("g_rows", [NT * P, C], F32, kind="Internal").ap()
    g_tiles = g_dram.rearrange("(t p) c -> p t c", p=P)
    rec_dram = nc.dram_tensor("records", [P * SLOTS + P * COLS, 1], I32, kind="Internal").ap()
    x_tiles = x.rearrange("(t p) c -> p t c", p=P)
    out_tiles = out.rearrange("(t p) c -> p t c", p=P)

    with ExitStack() as ctx:
        def sb(name, shape, dt=F32):
            return ctx.enter_context(nc.sbuf_tensor(name, shape, dt))

        def sem(name):
            return ctx.enter_context(nc.semaphore(name))

        banks = [ctx.enter_context(nc.psum_tensor(f"bank{k}", [P, CUT], F32)) for k in range(8)]

        acc = sb("acc", [P, NT * AW])
        selfp = sb("selfp", [P, NT * C])
        hT_all = sb("hT_all", [P, NT * C])
        gath = sb("gath", [P, RING * AW])
        onehot = sb("onehot", [P, RING * P])
        misc = sb("misc", [P, BODY * C])
        tables = sb("tables", [P, 2 * SLOTS])
        idx_ring = sb("idx_ring", [P, RING], I32)
        wg = sb("wg", [P, (LAYERS + 1) * KC * C])
        ws = sb("ws", [P, LAYERS * KC * C])
        win = sb("win", [P, KC * C])
        bias_in = sb("bias_in", [P, KC])
        bias_hid = sb("bias_hid", [P, LAYERS * KC])
        bias_e = sb("bias_e", [P, 2 * EXPERTS * KC])
        ident = sb("ident", [P, P])
        iota_f = sb("iota_f", [P, P])
        zeros = sb("zeros", [P, 1])
        eps_t = sb("eps_t", [P, 1])
        rdeg = sb("rdeg", [P, NT])
        mv = sb("mv", [P, NT * 2])
        rstd = sb("rstd", [P, NT])
        nmr = sb("nmr", [P, NT])
        cnt = sb("cnt", [P, NT])
        base = sb("base", [P, NT])
        run_i = sb("run_i", [NT, 1], I32)
        run_j = sb("run_j", [NT, 1], I32)
        run_tiles = sb("run_tiles", [NT, 1])
        run_end = sb("run_end", [NT, 1])
        w_body = sb("w_body", [P, BODY * EXPERTS])

        acc3 = acc[:, :].rearrange("p (t c) -> p t c", c=AW)
        gath3 = gath[:, :].rearrange("p (t c) -> p t c", c=AW)
        onehot3 = onehot[:, :].rearrange("p (t c) -> p t c", c=P)
        u_ring = gath[:, 0:BODY * C]
        g_ring = gath[:, BODY * C:2 * BODY * C]
        hT_ring = onehot[:, 0:BODY * C]
        u3 = u_ring.rearrange("p (t c) -> p t c", c=C)
        g3 = g_ring.rearrange("p (t c) -> p t c", c=C)
        hr4 = hT_ring.rearrange("p (t k c) -> p t k c", k=KC, c=P)
        hT_self = misc[:, 4 * C:5 * C]
        hs3 = hT_self.rearrange("p (k c) -> p k c", k=KC)
        win3 = win[:, :].rearrange("p (k c) -> p k c", k=KC)
        mv3 = mv[:, :].rearrange("p (t c) -> p t c", c=2)
        slot_src = tables[:, 0:SLOTS].bitcast(I32)
        slot_tgt = tables[:, SLOTS:2 * SLOTS]
        slot_node = misc[0:1, 0:SLOTS].bitcast(I32)

        stats = misc[:, BODY * C - NT * 6:BODY * C]

        xT_ring = misc[:, :]
        xr4 = xT_ring.rearrange("p (t k c) -> p t k c", k=KC, c=P)
        scratch = [selfp[:, r * COLS:(r + 1) * COLS] for r in range(11)]
        edge_t, edge_s, tile_i, temp_i = (scratch[r].bitcast(I32) for r in range(4))
        tile_h = scratch[4].bitcast(F16)[:, 0:COLS]
        cums = scratch[5:8]
        pos_sum = scratch[10]
        masks = [scratch[8 + r // 2].bitcast(F16)[:, (r % 2) * COLS:(r % 2 + 1) * COLS]
                 for r in range(3)]
        part_a = tables[:, 0:COLS]
        part_b = tables[:, COLS:2 * COLS]
        pos_hi = misc[:, 0:COLS]
        pos_lo = misc[:, COLS:2 * COLS]
        iota_h = gath[:, 2 * BODY * C:2 * BODY * C + PW // 2].bitcast(F16)
        run_wide = gath[0:NT, 2 * BODY * C + PW // 2:2 * BODY * C + PW // 2 + P]
        lower = onehot[:, BODY * C:BODY * C + P]
        lower_eq = onehot[:, BODY * C + P:BODY * C + P + NT]
        ones = onehot[:, BODY * C + P + NT:BODY * C + 2 * P + NT]
        RW = PW // 2
        p_hi = selfp[:, 0:PERM * RW].bitcast(F16).rearrange("p (r c) -> p r c", c=PW)
        p_lo = selfp[:, PERM * RW:PERM * RW + PERM * P].bitcast(F16)\
            .rearrange("p (r a c) -> p r a c", a=2, c=P)
        DEC0 = PERM * (RW + P)
        past, dec_a, dec_b, dec_c, dec_e = (
            selfp[:, DEC0 + r * SLOTS:DEC0 + (r + 1) * SLOTS] for r in range(5))
        dec_d = dec_a
        dec_bi, dec_ci, scattered_recs = (v.bitcast(I32) for v in (dec_b, dec_c, dec_e))
        AFTER = 11 * COLS
        sc_slot, sc_rec, sc_temp, sc_pad = (
            selfp[:, AFTER + r * SC_COLS:AFTER + (r + 1) * SC_COLS].bitcast(I32) for r in range(4))
        sc_ring = selfp[:, AFTER + 4 * SC_COLS:AFTER + 4 * SC_COLS + 2 * SC_RING].bitcast(I32)
        slot_ring, rec_ring = sc_ring[:, 0:SC_RING], sc_ring[:, SC_RING:2 * SC_RING]

        x2_all = selfp[:, :].rearrange("p (t c) -> p t c", c=C)
        fT_all = hT_all[:, :].rearrange("p (k n) -> p k n", k=KC)
        EW = KC * C
        ew = acc[:, 0:EXPERTS * 3 * EW].rearrange("p (w e k c) -> p w e k c", w=3, e=EXPERTS, k=KC)
        EXTRA = EXPERTS * 3 * EW
        f_ring = acc[:, EXTRA:EXTRA + BODY * C].rearrange("p (t c) -> p t c", c=C)
        rhT = acc[:, EXTRA + BODY * C:EXTRA + BODY * C + BODY * P]
        h1T = gath[:, 0:BODY * C].rearrange("p (k n) -> p k n", k=KC)
        h2T = gath[:, BODY * C:2 * BODY * C].rearrange("p (k n) -> p k n", k=KC)
        x_in, y_in = u3, g3
        be4 = bias_e[:, :].rearrange("p (w e k) -> p w e k", w=2, e=EXPERTS)
        bout_t = onehot[:, 0:C]
        rw1 = onehot[:, C:C + KC * P].rearrange("p (k c) -> p k c", k=KC)
        rw2 = onehot[:, 2 * C:2 * C + EXPERTS]
        rb2 = onehot[:, 2 * C + EXPERTS:2 * C + 2 * EXPERTS]
        rb1 = onehot[:, 2 * C + 2 * EXPERTS:2 * C + 2 * EXPERTS + 1]
        wT = onehot[0:EXPERTS, 3 * C:3 * C + BODY * P]
        b3_t = onehot[0:EXPERTS, 3 * C + BODY * P:4 * C + BODY * P]
        NE = NT * EXPERTS
        logits, gates, rank, beat = (misc[:, r * NE:(r + 1) * NE] for r in range(4))
        topv = misc[:, 4 * NE:4 * NE + NT]
        lg3, gt3, rk3, bt3 = (v.rearrange("p (t e) -> p t e", e=EXPERTS)
                              for v in (logits, gates, rank, beat))
        top3 = topv.unsqueeze(2)

        weights_in = sem("weights_in")
        edges_in = sem("edges_in")
        x_loaded = sem("x_loaded")
        consts = sem("consts")
        dve_step = sem("dve_step")
        var_ready = sem("var_ready")
        std_ready = sem("std_ready")
        stats_ready = sem("stats_ready")
        cnt_ready = sem("cnt_ready")
        runs_counted = sem("runs_counted")
        run_sizes = sem("run_sizes")
        base_sum = sem("base_sum")
        mask_ready = sem("mask_ready")
        cum_ready = sem("cum_ready")
        msk_ready = sem("msk_ready")
        pos_added = sem("pos_added")
        p_ready = sem("p_ready")
        table_cleared = sem("table_cleared")
        sc_base = sem("sc_base")
        sc_tables = sem("sc_tables")
        sc_filled = sem("sc_filled")
        scattered = [sem(f"scattered{h}") for h in range(2)]
        table_in = sem("table_in")
        p_used = sem("p_used")
        slots_summed = sem("slots_summed")
        past_ready = sem("past_ready")
        node_sum = sem("node_sum")
        slots_ready = sem("slots_ready")
        u_ready = sem("u_ready")
        t_done = sem("t_done")
        t_evac = sem("t_evac")
        m_done = sem("m_done")
        m_evac = sem("m_evac")
        g_done = sem("g_done")
        g_evac = sem("g_evac")
        g_stored = sem("g_stored")
        g_free = sem("g_free")
        h_kept = sem("h_kept")
        acc_zeroed = sem("acc_zeroed")
        ones_ready = sem("ones_ready")
        idx_ready = sem("idx_ready")
        gathered = [sem(f"gathered{b}") for b in range(RING)]
        ticks = {eng: sem(f"ticks_{name}")
                 for name, eng in (("act", nc.scalar), ("dve", nc.vector), ("pool", nc.gpsimd))}
        onehot_ready = sem("onehot_ready")
        summed = sem("summed")
        drained = sem("drained")
        selfT_ready = sem("selfT_ready")
        self_done = sem("self_done")
        self_evac = sem("self_evac")
        deg_step = sem("deg_step")
        ffn_weights = sem("ffn_weights")
        x_reloaded = sem("x_reloaded")
        y_loaded = sem("y_loaded")
        xy_used = sem("xy_used")
        x2_ready = sem("x2_ready")
        rh_done = sem("rh_done")
        rh_ready = sem("rh_ready")
        lg_done = sem("lg_done")
        lg_evac = sem("lg_evac")
        soft_in = sem("soft_in")
        soft_exp = sem("soft_exp")
        w_ready = sem("w_ready")
        wT_done = sem("wT_done")
        wT_ready = sem("wT_ready")
        h_done = sem("h_done")
        h_evac = sem("h_evac")
        y_done = sem("y_done")
        y_added = sem("y_added")
        out_stored = sem("out_stored")

        CREDIT = 1
        credited = (pos_added, xy_used, t_done, t_evac, h_kept, g_free, self_done, lg_done, g_evac,
                    m_evac, self_evac, rh_ready, lg_evac, h_evac, wT_done)

        N_CONSTS = 9
        FFN_EARLY = 3
        FFN_LOADS = FFN_EARLY + 3 * EXPERTS + 5
        SPLIT = ((0, CUT), (CUT, SLOTS))
        WT_PARTS = ((0, 4), (4, BODY))
        block = ctx.enter_context(nc.Block())

        def go(eng, semaphore, value):
            eng.wait_ge(semaphore, value)
            eng.sem_inc(ticks[eng], 1)

        @block.sync
        def _(sp):
            sp.dma_start(edge_t, tgt.rearrange("(p c) -> p c", p=P)).then_inc(edges_in, 16)
            sp.dma_start(edge_s, gat.rearrange("(p c) -> p c", p=P)).then_inc(edges_in, 16)
            for i in range(BODIES):
                sp.dma_start(acc3[:, i * BODY:(i + 1) * BODY, 0:C],
                             x_tiles[:, i * BODY:(i + 1) * BODY, :]).then_inc(x_loaded, 16)
            sp.dma_start(win3, w_in.rearrange("(k p) c -> p k c", p=P)).then_inc(weights_in, 16)
            wg4 = wg[:, :].rearrange("p (l k c) -> p l k c", k=KC, c=C)
            ws4 = ws[:, :].rearrange("p (l k c) -> p l k c", k=KC, c=C)
            for l in range(LAYERS):
                sp.dma_start(wg4[:, l], w_agg[l].rearrange("(k p) c -> p k c", p=P))\
                    .then_inc(weights_in, 16)
                sp.dma_start(ws4[:, l], w_self[l].rearrange("(k p) c -> p k c", p=P))\
                    .then_inc(weights_in, 16)
            sp.dma_start(wg4[:, LAYERS], w_out.rearrange("(k p) c -> p k c", p=P))\
                .then_inc(weights_in, 16)
            with nc.allow_non_contiguous_dma(reason="biases, one per partition"):
                sp.dma_start(bias_in[:, :], b_in.rearrange("(k p) -> p k", p=P))\
                    .then_inc(weights_in, 16)
                sp.dma_start(bias_hid[:, :], b_hid.rearrange("l (k p) -> p (l k)", p=P))\
                    .then_inc(weights_in, 16)
                for w, b in enumerate((e_b1, e_b2)):
                    sp.dma_start(bias_e[:, w * EXPERTS * KC:(w + 1) * EXPERTS * KC],
                                 b.rearrange("e (k p) -> p (e k)", p=P)).then_inc(ffn_weights, 16)

            def store_g(i, n):
                sp.wait_ge(g_evac, CREDIT + NPAIR * n + NPAIR)
                sp.dma_start(g_tiles[:, bass.ds(i * BODY, BODY), :], g3).then_inc(g_stored, 16)
                sp.wait_ge(g_stored, n * 16 + 16)
                sp.sem_inc(g_free, 1)

            sp.wait_ge(acc_zeroed, 1)
            by_slot = rec_dram[0:P * SLOTS, :].rearrange("(p c) a -> p (c a)", p=P)
            sp.dma_start(by_slot, acc[:, 0:SLOTS].bitcast(I32)).then_inc(table_cleared, 16)
            with sp.Fori(0, BODIES) as i:
                store_g(i, i)
            for h in range(2):
                sp.wait_ge(scattered[h], 16 * SC_HALF * SORT_STEPS)
            sp.wait_ge(sc_filled, 2 * SORT_STEPS)
            sp.dma_start(scattered_recs, by_slot).then_inc(table_in, 16)
            with sp.Fori(0, LAYERS) as l:
                with sp.Fori(0, BODIES) as i:
                    store_g(i, l * BODIES + i + BODIES)

            sp.wait_ge(acc_zeroed, BODIES * (LAYERS + 1))
            for w, src in enumerate((e_w1, e_w2, e_w3)):
                for e in range(EXPERTS):
                    sp.dma_start(ew[:, w, e], src[e].rearrange("(k p) c -> p k c", p=P))\
                        .then_inc(ffn_weights, 16)
            sp.wait_ge(g_stored, 16 * BODIES * (LAYERS + 1))
            sp.wait_ge(h_kept, CREDIT + BODIES * (LAYERS + 1))
            sp.dma_start(rw1, r_w1.rearrange("(k p) c -> p k c", p=P)).then_inc(ffn_weights, 16)
            with nc.allow_non_contiguous_dma(reason="a bias, one per partition"):
                sp.dma_start(rb1, r_b1.rearrange("(p a) -> p a", a=1)).then_inc(ffn_weights, 16)
            sp.dma_start(b3_t, e_b3).then_inc(ffn_weights, 16)
            sp.dma_start(rw2, r_w2).then_inc(ffn_weights, 16)
            sp.dma_start(rb2, r_b2.unsqueeze(0).to_broadcast([P, EXPERTS])).then_inc(ffn_weights, 16)
            sp.dma_start(bout_t, b_out.unsqueeze(0).to_broadcast([P, C])).then_inc(ffn_weights, 16)
            with sp.Fori(0, BODIES) as i:
                sp.wait_ge(xy_used, CREDIT + i)
                sp.dma_start(x_in, x_tiles[:, bass.ds(i * BODY, BODY), :]).then_inc(x_reloaded, 16)
                sp.dma_start(y_in, g_tiles[:, bass.ds(i * BODY, BODY), :]).then_inc(y_loaded, 16)
            with sp.Fori(0, BODIES) as i:
                sp.wait_ge(y_added, (i + 1) * (NPAIR * (EXPERTS + 1)) + NPAIR)
                sp.dma_start(out_tiles[:, bass.ds(i * BODY, BODY), :],
                             x2_all[:, bass.ds(i * BODY, BODY), :]).then_inc(out_stored, 16)
            sp.wait_ge(out_stored, 16 * BODIES)

        @block.gpsimd
        def _(pool):
            pool.iota(iota_f[:, :], [[1, P]], base=0, channel_multiplier=0,
                      allow_small_or_imprecise_dtypes=True).then_inc(consts, 1)
            pool.iota(iota_h, [[1, PW]], base=0, channel_multiplier=0,
                      allow_small_or_imprecise_dtypes=True).then_inc(consts, 1)
            pool.memset(zeros[:, :], 0.0).then_inc(consts, 1)
            pool.memset(eps_t[:, :], EPS).then_inc(consts, 1)
            pool.memset(ones, 1.0).then_inc(consts, 1)
            pool.memset(ident[:, :], 0.0).then_inc(consts, 1)
            pool.wait_ge(consts, 6)
            pool.affine_select(out=ident[:, :], in_=ident[:, :], compare_op=ALU.not_equal, fill=1.0,
                               base=0, pattern=[[-1, P]], channel_multiplier=1).then_inc(consts, 1)
            pool.affine_select(out=lower, in_=ones, compare_op=ALU.is_gt, fill=0.0,
                               base=0, pattern=[[1, P]], channel_multiplier=-1).then_inc(consts, 1)
            pool.affine_select(out=lower_eq, in_=ones[:, 0:NT], compare_op=ALU.is_ge, fill=0.0,
                               base=0, pattern=[[1, NT]], channel_multiplier=-1).then_inc(consts, 1)

            def zero_sums(i, n):
                pool.wait_ge(u_ready, n * BODY + BODY)
                pool.tensor_copy(acc[:, bass.ds(i * (BODY * AW), BODY * AW)],
                                 zeros[:, 0:1].to_broadcast([P, BODY * AW])).then_inc(acc_zeroed, 1)

            with pool.Fori(0, BODIES) as i:
                for b in range(BODY):
                    pool.wait_ge(cum_ready, i * BODY + b + 1)
                    cum = cums[cum_of(b)]
                    pool.tensor_tensor(cum, cum, masks[cum_of(b)], ALU.mult).then_inc(msk_ready, 1)
                zero_sums(i, i)

            pool.iota(sc_pad, [[1, SC_COLS]], base=P * SLOTS + PE_COLS, channel_multiplier=COLS)\
                .then_inc(sc_base, 1)
            pool.wait_ge(table_cleared, 16)
            with pool.Fori(0, SORT_STEPS) as i:
                for b in range(SC_RING):
                    h = b // SC_HALF
                    if b % SC_HALF == 0:
                        go(pool, sc_filled, i * 2 + (h + 1))
                    pool.indirect_dma_start(
                        rec_dram, bass.IndirectOffsetOnAxis(ap=slot_ring[:, b:b + 1], axis=0),
                        rec_ring[:, b:b + 1], None).then_inc(scattered[h], 16)

            pool.wait_ge(slots_ready, 1)
            with pool.Fori(0, LAYERS) as l:
                go(pool, g_stored, l * (16 * BODIES) + 16 * BODIES)
                pool.memset(gath3[:, :, C:AW], 1.0).then_inc(ones_ready, 1)
                go(pool, ones_ready, l + 1)
                with pool.Fori(0, STEPS) as i:
                    n = l * STEPS + i
                    for b in range(RING):
                        if b == 0:
                            pool.wait_ge(idx_ready, n * 2 + 1)
                        if b == HALF:
                            pool.wait_ge(idx_ready, n * 2 + 2)
                        go(pool, summed, n * RING + (b + 1))
                        pool.indirect_dma_start(
                            gath3[:, b, 0:C], None, g_dram,
                            bass.IndirectOffsetOnAxis(ap=idx_ring[:, b:b + 1], axis=0))\
                            .then_inc(gathered[b], 16)
                with pool.Fori(0, BODIES) as i:
                    zero_sums(i, l * BODIES + i + BODIES)

        @block.scalar
        def _(act):
            act.wait_ge(consts, N_CONSTS)
            act.wait_ge(var_ready, 1)
            act.activation(rstd[:, :], mv3[:, :, 1], ACT.Sqrt, bias=eps_t[:, 0:1])\
                .then_inc(std_ready, 1)
            act.wait_ge(weights_in, 16 * (2 + 2 * LAYERS + 2))

            def evac_g(n):
                act.wait_ge(g_free, CREDIT + n)
                for q, (a, z) in enumerate(PAIRS):
                    act.wait_ge(g_done, NPAIR * n + (q + 1))
                    act.copy(g_ring[:, a * C:z * C], banks[G_BANK[q]][:, 0:(z - a) * C])\
                        .then_inc(g_evac, 1)

            def keep_h(i, n, ready):
                go(act, ready, CREDIT + NPAIR * n + NPAIR)
                act.copy(hT_all[:, bass.ds(i * (BODY * C), BODY * C)], hT_ring).then_inc(h_kept, 1)

            def by_tile(bank, n):
                return bank[:, 0:n * C].rearrange("p (t k c) -> p t k c", k=KC, c=P)

            act.wait_ge(stats_ready, 1)
            with act.Fori(0, BODIES) as i:
                act.wait_ge(t_done, CREDIT + i * NPAIR)
                for b in range(BODY):
                    act.activation(u3[:, b], acc[:, bass.ds(i * (BODY * AW) + b * AW, C)],
                                   ACT.Identity, bias=nmr[:, bass.ds(i * BODY + b, 1)],
                                   scale=rstd[:, bass.ds(i * BODY + b, 1)]).then_inc(u_ready, 1)
                for q, (a, z) in enumerate(PAIRS):
                    act.wait_ge(t_done, CREDIT + i * NPAIR + (q + 1))
                    act.copy(xT_ring[:, a * C:z * C], banks[T_BANK[q]][:, 0:(z - a) * C])\
                        .then_inc(t_evac, 1)
                act.wait_ge(h_kept, CREDIT + i)
                for q, (a, z) in enumerate(PAIRS):
                    act.wait_ge(m_done, i * NPAIR + (q + 1))
                    for k in range(KC):
                        ins = act.activation(hr4[:, a:z, k], by_tile(banks[M_BANK[q]], z - a)[:, :, k],
                                             ACT.Identity, bias=bias_in[:, k:k + 1])
                    ins.then_inc(m_evac, 1)
                keep_h(i, i, m_evac)
                evac_g(i)

            def fill_half(h, step):
                ring = slice(h * SC_HALF, (h + 1) * SC_HALF)
                at = bass.ds(step * SC_RING + h * SC_HALF, SC_HALF)
                act.copy(slot_ring[:, ring], sc_slot[:, at])
                act.copy(rec_ring[:, ring], sc_rec[:, at]).then_inc(sc_filled, 1)

            act.wait_ge(sc_tables, 1)
            for h in range(2):
                fill_half(h, 0)
            with act.Fori(0, SORT_STEPS - 1) as i:
                for h in range(2):
                    go(act, scattered[h], (i + 1) * (16 * SC_HALF))
                    fill_half(h, i + 1)

            act.wait_ge(slots_ready, 1)
            with act.Fori(0, LAYERS) as l:
                act.wait_ge(h_kept, CREDIT + l * BODIES + BODIES)
                with act.Fori(0, STEPS) as i:
                    n = l * STEPS + i
                    act.wait_ge(summed, n * RING + HALF)
                    act.copy(idx_ring[:, 0:HALF], slot_src[:, bass.ds(i * RING, HALF)])\
                        .then_inc(idx_ready, 1)
                    act.wait_ge(self_done, CREDIT + n)
                    act.copy(hT_self, hT_all[:, bass.ds(i * C, C)]).then_inc(selfT_ready, 1)
                    act.wait_ge(summed, n * RING + RING)
                    act.copy(idx_ring[:, HALF:RING], slot_src[:, bass.ds(i * RING + HALF, RING - HALF)])\
                        .then_inc(idx_ready, 1)
                    act.wait_ge(self_done, CREDIT + n + 1)
                    act.copy(selfp[:, bass.ds(i * C, C)], banks[5][:, 0:C]).then_inc(self_evac, 1)
                with act.Fori(0, BODIES) as i:
                    n = l * BODIES + i + BODIES
                    act.wait_ge(h_kept, CREDIT + n)
                    for q, (a, z) in enumerate(PAIRS):
                        go(act, t_done, CREDIT + n * NPAIR + (q + 1))
                        for k in range(KC):
                            ins = act.activation(hr4[:, a:z, k],
                                                 by_tile(banks[T_BANK[q]], z - a)[:, :, k],
                                                 ACT.Relu, bias=bias_hid[:, bass.ds(l * KC + k, 1)])
                        ins.then_inc(t_evac, 1)
                    keep_h(i, n, t_evac)
                    evac_g(n)

            act.wait_ge(var_ready, 2)
            act.activation(rstd[:, :], mv3[:, :, 1], ACT.Sqrt, bias=eps_t[:, 0:1])\
                .then_inc(std_ready, 1)
            act.wait_ge(ffn_weights, 16 * FFN_LOADS)
            with act.Fori(0, BODIES) as i:
                n = i + (LAYERS + 1) * BODIES
                for q, (a, z) in enumerate(PAIRS):
                    act.wait_ge(t_done, CREDIT + n * NPAIR + (q + 1))
                    act.copy(fT_all[:, :, bass.ds(i * (BODY * P) + a * P, (z - a) * P)],
                             banks[T_BANK[q]][:, 0:(z - a) * C].rearrange("p (k n) -> p k n", k=KC))\
                        .then_inc(t_evac, 1)
                act.wait_ge(lg_done, CREDIT + i)
                for h in range(2):
                    act.wait_ge(rh_done, i * 2 + (h + 1))
                    act.activation(rhT[:, h * FH:(h + 1) * FH], banks[5 + h][:, 0:FH], ACT.Relu,
                                   bias=rb1).then_inc(rh_ready, 1)
            for k in range(2):
                act.wait_ge(soft_in, k + 1)
                act.activation(gates, gates, ACT.Exp).then_inc(soft_exp, 1)

            with act.Fori(0, BODIES) as i:
                for h, (a, z) in enumerate(WT_PARTS):
                    act.wait_ge(wT_done, CREDIT + i * 2 + (h + 1))
                    act.copy(wT[:, a * P:z * P], banks[h][0:EXPERTS, 0:(z - a) * P])\
                        .then_inc(wT_ready, 1)
                for e in range(EXPERTS):
                    for w, dst in enumerate((h1T, h2T)):
                        for k in range(4):
                            h, m = k // 2, k % 2
                            act.wait_ge(h_done, i * (EXPERTS * 8) + (8 * e + 4 * w + k + 1))
                            act.activation(dst[:, m, h * FH:(h + 1) * FH], banks[k][:, 0:FH],
                                           ACT.Relu, bias=be4[:, w, e, m:m + 1])\
                                .then_inc(h_evac, 1)

        @block.tensor
        def _(pe):
            pe.wait_ge(consts, N_CONSTS)
            pe.sem_inc(summed, RING)
            for semaphore in credited:
                pe.sem_inc(semaphore, CREDIT)

            pe.wait_ge(cnt_ready, 1)
            pe.matmul(banks[0][0:NT, 0:1], cnt[:, :], ones[:, 0:1], start=True, stop=True)\
                .then_inc(runs_counted, 1)
            pe.wait_ge(run_sizes, 1)
            pe.matmul(banks[1][:, 0:NT], run_wide, lower[0:NT, 0:NT], start=True, stop=False)
            pe.matmul(banks[1][:, 0:NT], lower, cnt[:, :], start=False, stop=True)
            pe.matmul(banks[2][0:NT, 0:1], lower_eq[0:NT, 0:NT], run_tiles[:, :],
                      start=True, stop=True).then_inc(base_sum, 1)

            def transposes(n):
                for q, (a, z) in enumerate(PAIRS):
                    pe.wait_ge(u_ready, n * BODY + z)
                    pe.wait_ge(t_evac, CREDIT + t_freed(n, q))
                    for t in range(a, z):
                        for k in range(KC):
                            at = ((t - a) * KC + k) * P
                            ins = pe.transpose(banks[T_BANK[q]][:, at:at + P],
                                               u3[:, t, k * P:(k + 1) * P], ident[:, :])
                    ins.then_inc(t_done, 1)

            def g_products(n, w, ready):
                for q, (a, z) in enumerate(PAIRS):
                    pe.wait_ge(ready, CREDIT + n * NPAIR + (q + 1))
                    pe.wait_ge(g_evac, CREDIT + n * NPAIR + (1 if q == 3 else 0))
                    for t in range(a, z):
                        for k in range(KC):
                            ins = pe.matmul(banks[G_BANK[q]][:, (t - a) * C:(t - a + 1) * C],
                                            hr4[:, t, k], wg[:, bass.ds(w * (KC * C) + k * C, C)],
                                            start=(k == 0), stop=(k == KC - 1))
                    ins.then_inc(g_done, 1)

            def with_zeros(bank, width, opens):
                return pe.matmul(banks[bank][:, 0:width], ident[:, :],
                                 zeros[:, :].to_broadcast([P, width]), start=opens,
                                 stop=not opens, skip_group_check=True)

            pe.wait_ge(weights_in, 16 * (2 + 2 * LAYERS + 2))
            with pe.Fori(0, BODIES) as i:
                transposes(i)
                for q, (a, z) in enumerate(PAIRS):
                    pe.wait_ge(t_evac, CREDIT + i * NPAIR + (q + 1))
                    pe.wait_ge(m_evac, CREDIT + i * NPAIR + (1 if q == 3 else 0))
                    for t in range(a, z):
                        for m in range(KC):
                            at = ((t - a) * KC + m) * P
                            for k in range(KC):
                                ins = pe.matmul(banks[M_BANK[q]][:, at:at + P],
                                                win3[:, k, m * P:(m + 1) * P], xr4[:, t, k],
                                                start=(k == 0), stop=(k == KC - 1))
                    ins.then_inc(m_done, 1)
                g_products(i, 0, m_evac)

            pe.wait_ge(g_evac, CREDIT + NPAIR * BODIES)
            for part in range(2):
                for k, (a, z) in enumerate(SPLIT):
                    with_zeros(2 * part + k, z - a, True)
            pe.sem_inc(p_used, PERM)
            with pe.Fori(0, PE_COLS // PERM) as i:
                for b in range(PERM):
                    pe.wait_ge(p_ready, i * PERM + (b + 2))
                    for part in range(2):
                        for k, (a, z) in enumerate(SPLIT):
                            ins = pe.matmul(banks[2 * part + k][:, 0:z - a], p_lo[:, b, part],
                                            p_hi[:, b, a:z], start=False, stop=False,
                                            skip_group_check=True)
                    ins.then_inc(p_used, 1)
            for part in range(2):
                for k, (a, z) in enumerate(SPLIT):
                    ins = with_zeros(2 * part + k, z - a, False)
            ins.then_inc(p_used, 1)
            pe.wait_ge(past_ready, 1)
            for k, (a, z) in enumerate(SPLIT):
                ins = pe.matmul(banks[6 + k][:, 0:z - a], ones[0:NT, :], past[0:NT, a:z],
                                start=True, stop=True)
            ins.then_inc(node_sum, 1)

            with pe.Fori(0, LAYERS) as l:
                with pe.Fori(0, STEPS) as i:
                    n = l * STEPS + i
                    for b in range(RING):
                        pe.wait_ge(gathered[b], n * 16 + 16)
                        if b == 0:
                            pe.wait_ge(onehot_ready, n * 2 + 1)
                        if b == HALF:
                            pe.wait_ge(onehot_ready, n * 2 + 2)
                        pe.wait_ge(drained, n * RING + (b + 1))
                        pe.matmul(banks[bank_of(b)][:, 0:AW], onehot3[:, b], gath3[:, b],
                                  start=True, stop=True).then_inc(summed, 1)
                        if b == RING // 2:
                            pe.wait_ge(selfT_ready, n + 1)
                            pe.wait_ge(self_evac, CREDIT + n)
                            for k in range(KC):
                                ins = pe.matmul(banks[5][:, 0:C], hs3[:, k],
                                                ws[:, bass.ds(l * (KC * C) + k * C, C)],
                                                start=(k == 0), stop=(k == KC - 1))
                            ins.then_inc(self_done, 1)
                with pe.Fori(0, BODIES) as i:
                    n = l * BODIES + i + BODIES
                    transposes(n)
                    g_products(n, l + 1, t_evac)

            pe.wait_ge(ffn_weights, 16 * FFN_LOADS)
            pe.wait_ge(g_evac, CREDIT + NPAIR * BODIES * (LAYERS + 1))
            with pe.Fori(0, BODIES) as i:
                n = i + (LAYERS + 1) * BODIES
                for q, (a, z) in enumerate(PAIRS):
                    pe.wait_ge(u_ready, n * BODY + z)
                    pe.wait_ge(t_evac, CREDIT + t_freed(n, q))
                    for t in range(a, z):
                        for k in range(KC):
                            at = (k * (z - a) + t - a) * P
                            ins = pe.transpose(banks[T_BANK[q]][:, at:at + P],
                                               f_ring[:, t, k * P:(k + 1) * P], ident[:, :])
                    ins.then_inc(t_done, 1)
                pe.wait_ge(t_evac, CREDIT + n * NPAIR + NPAIR)
                pe.wait_ge(rh_ready, CREDIT + i * 2)
                for h in range(2):
                    for k in range(KC):
                        ins = pe.matmul(banks[5 + h][:, 0:FH], rw1[:, k],
                                        fT_all[:, k, bass.ds(i * (BODY * P) + h * FH, FH)],
                                        start=(k == 0), stop=(k == KC - 1))
                    ins.then_inc(rh_done, 1)
                pe.wait_ge(rh_ready, CREDIT + i * 2 + 2)
                pe.wait_ge(lg_evac, CREDIT + i)
                for t in range(BODY):
                    ins = pe.matmul(banks[7][:, t * EXPERTS:(t + 1) * EXPERTS],
                                    rhT[:, t * P:(t + 1) * P], rw2, start=True, stop=True)
                ins.then_inc(lg_done, 1)

            pe.sem_inc(y_added, NPAIR)
            with pe.Fori(0, BODIES) as i:
                pe.wait_ge(w_ready, i + 1)
                pe.wait_ge(h_evac, CREDIT + i * (EXPERTS * 8))
                for h, (a, z) in enumerate(WT_PARTS):
                    for t in range(a, z):
                        ins = pe.transpose(banks[h][0:EXPERTS, (t - a) * P:(t - a + 1) * P],
                                           w_body[:, t * EXPERTS:(t + 1) * EXPERTS], ident[:, :])
                    ins.then_inc(wT_done, 1)
                pe.wait_ge(wT_ready, i * 2 + 2)
                for q, (a, z) in enumerate(PAIRS):
                    pe.wait_ge(y_added, i * (NPAIR * (EXPERTS + 1)) + (q + 1))
                    for t in range(a, z):
                        ins = pe.matmul(banks[4 + q][:, (t - a) * C:(t - a + 1) * C],
                                        wT[:, t * P:(t + 1) * P], b3_t, start=True, stop=True)
                    ins.then_inc(y_done, 1)
                for e in range(EXPERTS):
                    for w in range(2):
                        for k in range(4):
                            h, m = k // 2, k % 2
                            pe.wait_ge(h_evac, CREDIT + i * (EXPERTS * 8) + (8 * e + (2 * h + 2) * w))
                            for kk in range(KC):
                                rhs = (fT_all[:, kk, bass.ds(i * (BODY * P) + h * FH, FH)]
                                       if w == 0 else h1T[:, kk, h * FH:(h + 1) * FH])
                                ins = pe.matmul(banks[k][:, 0:FH],
                                                ew[:, w, e, kk, m * P:(m + 1) * P], rhs,
                                                start=(kk == 0), stop=(kk == KC - 1))
                            ins.then_inc(h_done, 1)
                    for q, (a, z) in enumerate(PAIRS):
                        pe.wait_ge(h_evac, CREDIT + i * (EXPERTS * 8) + (8 * e + (6 if z * P <= FH else 8)))
                        pe.wait_ge(y_added, i * (NPAIR * (EXPERTS + 1)) + ((e + 1) * NPAIR + q + 1))
                        for t in range(a, z):
                            for kk in range(KC):
                                ins = pe.matmul(banks[4 + q][:, (t - a) * C:(t - a + 1) * C],
                                                h2T[:, kk, t * P:(t + 1) * P], ew[:, 2, e, kk],
                                                start=(kk == 0), stop=(kk == KC - 1))
                        ins.then_inc(y_done, 1)

        @block.vector
        def _(dve):
            steps = [0]

            def link(ins):
                steps[0] += 1
                ins.then_inc(dve_step, 1)
                dve.wait_ge(dve_step, steps[0])

            dve.wait_ge(edges_in, 32)
            link(nc.vector.tensor_scalar(tile_i, edge_t, 7, None, ALU.arith_shift_right))
            link(nc.vector.tensor_copy(tile_h, tile_i))
            for b in range(NT):
                ins = nc.vector.tensor_scalar(masks[0], tile_h, float(b), 0.0,
                                              ALU.is_equal, ALU.add, accum_out=cnt[:, b:b + 1])
                if b < NT - 1:
                    link(ins)
            ins.then_inc(cnt_ready, 1)
            link(nc.vector.tensor_scalar(tile_i, edge_s, 3, None, ALU.arith_shift_right))
            link(nc.vector.tensor_copy(part_a, tile_i))
            link(nc.vector.tensor_scalar(temp_i, edge_s, 7, 7, ALU.bitwise_and,
                                         ALU.logical_shift_left))
            link(nc.vector.tensor_scalar(edge_t, edge_t, P - 1, None, ALU.bitwise_and))
            link(nc.vector.tensor_tensor(temp_i, temp_i, edge_t, ALU.add))
            link(nc.vector.tensor_scalar(part_b, temp_i, 1.0, None, ALU.add))

            dve.wait_ge(runs_counted, 1)
            link(nc.vector.tensor_scalar(run_i[:, :], banks[0][0:NT, 0:1], float(P - 1), None, ALU.add))
            link(nc.vector.tensor_scalar(run_j[:, :], run_i[:, :], 7, None, ALU.arith_shift_right))
            link(nc.vector.tensor_copy(run_tiles[:, :], run_j[:, :]))
            dve.wait_ge(consts, N_CONSTS)
            nc.vector.tensor_scalar(run_wide, ones[0:NT, :], run_tiles[:, 0:1], float(P),
                                    ALU.mult, ALU.mult).then_inc(run_sizes, 1)
            dve.wait_ge(base_sum, 1)
            link(nc.vector.tensor_copy(base[:, :], banks[1][:, 0:NT]))
            link(nc.vector.tensor_copy(run_end[:, :], banks[2][0:NT, 0:1]))

            def row_stats(rows):
                for t in range(NT):
                    ins = nc.vector.bn_stats(stats[:, t * 6:(t + 1) * 6], rows(t))
                link(ins)
                for t in range(NT):
                    ins = nc.vector.bn_aggr(mv[:, 2 * t:2 * t + 2], stats[:, t * 6:(t + 1) * 6])
                ins.then_inc(var_ready, 1)

            def row_scales(n):
                dve.wait_ge(std_ready, n)
                link(nc.vector.reciprocal(rstd[:, :], rstd[:, :]))
                return nc.vector.scalar_tensor_tensor(nmr[:, :], mv3[:, :, 0], -1.0, rstd[:, :],
                                                      ALU.mult, ALU.mult)

            dve.wait_ge(x_loaded, 16 * BODIES)
            row_stats(lambda t: acc3[:, t, 0:C])
            row_scales(1).then_inc(stats_ready, 1)

            link(nc.vector.memset(pos_sum, 0.0))
            link(nc.vector.memset(cums[2], 0.0))
            dve.sem_inc(msk_ready, 1)

            def add_counts(b):
                return nc.vector.tensor_tensor(pos_sum, pos_sum, cums[cum_of(b)], ALU.add)

            with dve.Fori(0, BODIES) as i:
                for b in range(BODY):
                    n = i * BODY + b
                    go(dve, pos_added, CREDIT + n)
                    mask = masks[cum_of(b)]
                    nc.vector.tensor_scalar(mask, tile_h, iota_f[:, bass.ds(i * BODY + b, 1)], None,
                                            ALU.is_equal).then_inc(mask_ready, 1)
                    dve.wait_ge(mask_ready, n + 1)
                    nc.vector.tensor_tensor_scan(cums[cum_of(b)], mask, mask,
                                                 base[:, bass.ds(i * BODY + b, 1)],
                                                 ALU.add, ALU.bypass).then_inc(cum_ready, 1)
                    dve.wait_ge(msk_ready, n + 1)
                    add_counts((b - 1) % BODY).then_inc(pos_added, 1)

            dve.wait_ge(pos_added, CREDIT + NT)
            dve.wait_ge(msk_ready, NT + 1)
            link(add_counts(BODY - 1))
            dve.wait_ge(m_done, NPAIR * BODIES)
            slot_i, temp_j = (cums[r].bitcast(I32) for r in range(2))
            link(nc.vector.tensor_scalar(slot_i, pos_sum, -1.0, None, ALU.add))
            link(nc.vector.tensor_scalar(temp_j, slot_i, 7, None, ALU.arith_shift_right))
            link(nc.vector.tensor_copy(pos_hi, temp_j))
            link(nc.vector.tensor_scalar(temp_j, slot_i, P - 1, None, ALU.bitwise_and))
            link(nc.vector.tensor_copy(pos_lo, temp_j))
            tail = slice(PE_COLS, COLS)
            link(nc.vector.tensor_scalar(sc_rec, part_a[:, tail], 1024.0, None, ALU.mult))
            link(nc.vector.tensor_tensor(sc_rec, sc_rec, part_b[:, tail], ALU.add))
            link(nc.vector.tensor_scalar(sc_slot, pos_lo[:, tail], float(SLOTS), None, ALU.mult))
            link(nc.vector.tensor_tensor(sc_slot, sc_slot, pos_hi[:, tail], ALU.add))
            link(nc.vector.tensor_scalar(sc_temp, pos_hi[:, tail], 0.0, None, ALU.is_lt))
            dve.wait_ge(sc_base, 1)
            link(nc.vector.tensor_tensor(sc_pad, sc_pad, sc_slot, ALU.subtract))
            link(nc.vector.tensor_tensor(sc_pad, sc_pad, sc_temp, ALU.mult))
            nc.vector.tensor_tensor(sc_slot, sc_slot, sc_pad, ALU.add).then_inc(sc_tables, 1)
            dve.sem_inc(p_ready, 1)
            with dve.Fori(0, PE_COLS // PERM) as i:
                for b in range(PERM):
                    dve.wait_ge(p_used, i * PERM + (b + 1))
                    at = bass.ds(i * PERM + b, 1)
                    for part, value in enumerate((part_a, part_b)):
                        nc.vector.tensor_scalar(p_lo[:, b, part], iota_h[:, 0:P], pos_lo[:, at],
                                                value[:, at], ALU.is_equal, ALU.mult)
                    nc.vector.tensor_scalar(p_hi[:, b], iota_h, pos_hi[:, at], None,
                                            ALU.is_equal).then_inc(p_ready, 1)

            nc.vector.tensor_scalar(past[0:NT, :], iota_h[0:NT, 0:SLOTS], run_end[:, 0:1], None,
                                    ALU.is_ge).then_inc(past_ready, 1)
            dve.wait_ge(p_used, PE_COLS + PERM + 1)
            for k, (a, z) in enumerate(SPLIT):
                link(nc.vector.tensor_scalar(dec_a[:, a:z], banks[k][:, 0:z - a], 1024.0, None,
                                             ALU.mult))
                link(nc.vector.tensor_tensor(dec_a[:, a:z], dec_a[:, a:z], banks[2 + k][:, 0:z - a],
                                             ALU.add))
            dve.wait_ge(table_in, 16)
            link(nc.vector.tensor_tensor(dec_a, dec_a, scattered_recs, ALU.add))
            link(nc.vector.tensor_scalar(dec_bi, dec_a, -1.0, None, ALU.add))
            link(nc.vector.tensor_scalar(dec_ci, dec_bi, 7, None, ALU.arith_shift_right))
            link(nc.vector.tensor_scalar(slot_src, dec_ci, 0.0, None, ALU.max))
            link(nc.vector.tensor_scalar(dec_d, dec_bi, 0.0, 1000.0, ALU.is_lt, ALU.mult))
            link(nc.vector.tensor_scalar(dec_ci, dec_bi, P - 1, None, ALU.bitwise_and))
            link(nc.vector.tensor_tensor(slot_tgt, dec_d, dec_ci, ALU.add))
            dve.wait_ge(node_sum, 1)
            for k, (a, z) in enumerate(SPLIT):
                link(nc.vector.tensor_scalar(slot_node[:, a:z], banks[6 + k][0:1, 0:z - a],
                                             float(NT - 1), None, ALU.min))
            dve.sem_inc(drained, 4)
            dve.sem_inc(slots_ready, 1)

            with dve.Fori(0, LAYERS) as l:
                dve.wait_ge(acc_zeroed, l * BODIES + BODIES)
                dve.wait_ge(h_kept, CREDIT + l * BODIES + BODIES)
                go(dve, g_evac, CREDIT + l * (BODIES * NPAIR) + BODIES * NPAIR)
                with dve.Fori(0, STEPS) as i:
                    n = l * STEPS + i
                    _, nodes = nc.values_load_multi_w_load_instructions(
                        slot_node[:, bass.ds(i * RING, RING)], engines=(mybir.EngineType.DVE,),
                        min_val=0, max_val=NT - 1,
                        skip_runtime_bounds_check_because="the table was cut to this range")
                    for a, z in HALVES:
                        dve.wait_ge(summed, n * RING + z)
                        nc.vector.tensor_tensor(
                            onehot3[:, a:z],
                            iota_f[:, :].unsqueeze(1).to_broadcast([P, z - a, P]),
                            slot_tgt[:, bass.ds(i * RING + a, z - a)].unsqueeze(2)
                            .to_broadcast([P, z - a, P]), ALU.is_equal).then_inc(onehot_ready, 1)
                    for b in range(RING):
                        dve.wait_ge(drained, n * RING + (b + 4))
                        dve.wait_ge(summed, n * RING + (b + 1 + RING))
                        row = bass.ds(nodes[b] * AW, AW)
                        nc.vector.tensor_tensor(acc[:, row], acc[:, row],
                                                banks[bank_of(b)][:, 0:AW], ALU.add)\
                            .then_inc(drained, 1)
                dve.wait_ge(drained, l * SLOTS + (SLOTS + 4))
                dve.wait_ge(self_evac, CREDIT + l * STEPS + STEPS)
                nc.vector.tensor_scalar(rdeg[:, :], acc3[:, :, C], 1.0, None, ALU.max)\
                    .then_inc(deg_step, 1)
                dve.wait_ge(deg_step, l * 2 + 1)
                nc.vector.reciprocal(rdeg[:, :], rdeg[:, :]).then_inc(deg_step, 1)
                go(dve, deg_step, l * 2 + 2)
                with dve.Fori(0, BODIES) as i:
                    n = l * BODIES + i + BODIES
                    dve.wait_ge(t_done, CREDIT + n * NPAIR)
                    for b in range(BODY):
                        nc.vector.scalar_tensor_tensor(
                            u3[:, b], acc[:, bass.ds(i * (BODY * AW) + b * AW, C)],
                            rdeg[:, bass.ds(i * BODY + b, 1)],
                            selfp[:, bass.ds(i * (BODY * C) + b * C, C)],
                            ALU.mult, ALU.add).then_inc(u_ready, 1)

            dve.wait_ge(ffn_weights, 16 * FFN_LOADS)
            with dve.Fori(0, BODIES) as i:
                here = x2_all[:, bass.ds(i * BODY, BODY), :]
                dve.wait_ge(x_reloaded, i * 16 + 16)
                dve.wait_ge(y_loaded, i * 16 + 16)
                nc.vector.tensor_tensor(here, x_in, y_in, ALU.add).then_inc(xy_used, 1)
                dve.wait_ge(xy_used, CREDIT + i + 1)
                nc.vector.tensor_tensor(here, here,
                                        bout_t.unsqueeze(1).to_broadcast([P, BODY, C]), ALU.add)\
                    .then_inc(x2_ready, 1)
            dve.wait_ge(x2_ready, BODIES)
            row_stats(lambda t: x2_all[:, t])
            link(row_scales(2))
            with dve.Fori(0, BODIES) as i:
                n = i + (LAYERS + 1) * BODIES
                dve.wait_ge(t_done, CREDIT + n * NPAIR)
                for b in range(BODY):
                    nc.vector.tensor_scalar(f_ring[:, b], selfp[:, bass.ds(i * (BODY * C) + b * C, C)],
                                            rstd[:, bass.ds(i * BODY + b, 1)],
                                            nmr[:, bass.ds(i * BODY + b, 1)],
                                            ALU.mult, ALU.add).then_inc(u_ready, 1)
                dve.wait_ge(lg_done, CREDIT + i + 1)
                nc.vector.tensor_tensor(lg3[:, bass.ds(i * BODY, BODY), :],
                                        banks[7][:, 0:BODY * EXPERTS]
                                        .rearrange("p (t e) -> p t e", e=EXPERTS),
                                        rb2.unsqueeze(1).to_broadcast([P, BODY, EXPERTS]),
                                        ALU.add).then_inc(lg_evac, 1)

            wide = top3.to_broadcast([P, NT, EXPERTS])
            dve.wait_ge(lg_evac, CREDIT + BODIES)
            link(nc.vector.tensor_reduce(topv, lg3, AX.X, ALU.max))
            nc.vector.tensor_tensor(gt3, lg3, wide, ALU.subtract).then_inc(soft_in, 1)
            dve.wait_ge(soft_exp, 1)
            link(nc.vector.tensor_reduce(topv, gt3, AX.X, ALU.add))
            link(nc.vector.reciprocal(topv, topv))
            link(nc.vector.tensor_tensor(gt3, gt3, wide, ALU.mult))
            link(nc.vector.memset(rank, 0.0))
            for o in range(EXPERTS):
                if o > 0:
                    link(nc.vector.tensor_tensor(bt3[:, :, 0:o],
                                                 gt3[:, :, o:o + 1].to_broadcast([P, NT, o]),
                                                 gt3[:, :, 0:o], ALU.is_gt))
                    link(nc.vector.tensor_tensor(rk3[:, :, 0:o], rk3[:, :, 0:o], bt3[:, :, 0:o],
                                                 ALU.add))
                if o < EXPERTS - 1:
                    r = EXPERTS - 1 - o
                    link(nc.vector.tensor_tensor(bt3[:, :, o + 1:],
                                                 gt3[:, :, o:o + 1].to_broadcast([P, NT, r]),
                                                 gt3[:, :, o + 1:], ALU.is_ge))
                    link(nc.vector.tensor_tensor(rk3[:, :, o + 1:], rk3[:, :, o + 1:],
                                                 bt3[:, :, o + 1:], ALU.add))
            link(nc.vector.tensor_scalar(rank, rank, float(TOP_K), None, ALU.is_lt))
            link(nc.vector.tensor_reduce(topv, gt3, AX.X, ALU.max))
            nc.vector.tensor_tensor(gt3, gt3, wide, ALU.subtract).then_inc(soft_in, 1)
            dve.wait_ge(soft_exp, 2)
            link(nc.vector.tensor_tensor(gates, gates, rank, ALU.mult))
            link(nc.vector.tensor_reduce(topv, gt3, AX.X, ALU.add))
            link(nc.vector.reciprocal(topv, topv))
            link(nc.vector.tensor_tensor(gt3, gt3, wide, ALU.mult))

            with dve.Fori(0, BODIES) as i:
                dve.wait_ge(wT_done, CREDIT + i * 2)
                nc.vector.tensor_copy(w_body[:, :], gates[:, bass.ds(i * (BODY * EXPERTS),
                                                                     BODY * EXPERTS)])\
                    .then_inc(w_ready, 1)
                for e in range(EXPERTS + 1):
                    for q, (a, z) in enumerate(PAIRS):
                        done = i * (NPAIR * (EXPERTS + 1)) + (e * NPAIR + q + 1)
                        dve.wait_ge(y_done, done)
                        dve.wait_ge(y_added, done)
                        for t in range(a, z):
                            here = selfp[:, bass.ds(i * (BODY * C) + t * C, C)]
                            part = banks[4 + q][:, (t - a) * C:(t - a + 1) * C]
                            if e == 0:
                                ins = nc.vector.tensor_tensor(here, here, part, ALU.add)
                            else:
                                gate = gates[:, bass.ds(i * (BODY * EXPERTS)
                                                        + (t * EXPERTS + e - 1), 1)]
                                ins = nc.vector.scalar_tensor_tensor(here, part, gate, here,
                                                                     ALU.mult, ALU.add)
                        ins.then_inc(y_added, 1)


def kernel(x, src, dst, L0_gnn_W_in, L0_gnn_b_in, L0_gnn_W_agg, L0_gnn_W_self, L0_gnn_b_hid,
           L0_gnn_W_out, L0_gnn_b_out, L0_ffn_router_w1, L0_ffn_router_b1, L0_ffn_router_w2,
           L0_ffn_router_b2, L0_ffn_expert_w1, L0_ffn_expert_b1, L0_ffn_expert_w2,
           L0_ffn_expert_b2, L0_ffn_expert_w3, L0_ffn_expert_b3):
    import numpy as np
    import concourse.bacc as bacc
    from concourse.bass_utils import run_bass_kernel_spmd

    def padded(a, rows, fill):
        a = np.asarray(a)
        out = np.full((rows,) + a.shape[1:], fill, a.dtype)
        out[:a.shape[0]] = a
        return out

    arrays = {
        "in_x": padded(x, NT * P, 0),
        "in_tgt": padded(src, P * COLS, -1),
        "in_gat": padded(dst, P * COLS, 0),
    }
    for name, a in (("w_in", L0_gnn_W_in), ("b_in", L0_gnn_b_in), ("w_agg", L0_gnn_W_agg),
                    ("w_self", L0_gnn_W_self), ("b_hid", L0_gnn_b_hid), ("w_out", L0_gnn_W_out),
                    ("b_out", L0_gnn_b_out), ("r_w1", L0_ffn_router_w1),
                    ("r_b1", L0_ffn_router_b1), ("r_w2", L0_ffn_router_w2),
                    ("r_b2", L0_ffn_router_b2), ("e_w1", L0_ffn_expert_w1),
                    ("e_b1", L0_ffn_expert_b1), ("e_w2", L0_ffn_expert_w2),
                    ("e_b2", L0_ffn_expert_b2), ("e_w3", L0_ffn_expert_w3),
                    ("e_b3", L0_ffn_expert_b3)):
        arrays["in_" + name] = np.ascontiguousarray(np.asarray(a))

    nc = bacc.Bacc("TRN2", target_bir_lowering=False, num_devices=1)
    args = [nc.dram_tensor(n, a.shape, mybir.dt.from_np(a.dtype), kind="ExternalInput").ap()
            for n, a in arrays.items()]
    out = nc.dram_tensor("out_rows", (NT * P, C), F32, kind="ExternalOutput").ap()
    gnn_moe(nc, *args, out)
    r = run_bass_kernel_spmd(nc, [arrays], core_ids=[0])
    return r.results[0]["out_rows"][:NODES]
```

```python
from contextlib import ExitStack

import concourse.bass as bass
from concourse import mybir

ACT = mybir.ActivationFunctionType
ALU = mybir.AluOpType
AX = mybir.AxisListType
F32 = mybir.dt.float32
F16 = mybir.dt.float16
I32 = mybir.dt.int32

P = 128
NODES = 6250
EDGES = 100000
C = 256
KC = C // P
LAYERS = 3
EXPERTS = 6
TOP_K = 2
EPS = 1e-5

NT = -(-NODES // P)
BODY = 7
BODIES = NT // BODY
PAIRS = [(0, 2), (2, 4), (4, 6), (6, 7)]
NPAIR = len(PAIRS)

COLS = 784
SLOTS = EDGES // P + NT + 3
RING = 17
STEPS = SLOTS // RING
HALF = 9
HALVES = [(0, HALF), (HALF, RING)]
AW = C + 1
PERM = 8
PW = SLOTS + 1
CUT = 512
SORT_STEPS = 28
PE_COLS = 448
SC_COLS = COLS - PE_COLS
SC_RING = SC_COLS // SORT_STEPS
SC_HALF = SC_RING // 2
assert PE_COLS % PERM == 0 and SC_COLS == SORT_STEPS * 2 * SC_HALF
assert NT == BODIES * BODY == STEPS and SLOTS == STEPS * RING and COLS % PERM == 0

FH = BODY * P // 2

ITEMS = TOP_K * NT
UNROLL = 8
EHALF = UNROLL // 2
ETILES = -(-(ITEMS + EXPERTS - 1) // UNROLL) * UNROLL
ESTEPS = ETILES // UNROLL
ROWS = TOP_K * NT * P
EROW = 7
WEXP = 3 * KC * C + 2 * KC + C
WBUFS = 4


def bank_of(b):
    return b % 4 if b < RING - 1 else 4


def cum_of(b):
    return b % 2 if b < BODY - 1 else 2


T_BANK = [0, 1, 0, 1]
M_BANK = [2, 3, 4, 2]
G_BANK = [5, 6, 7, 5]


def t_freed(n, q):
    return n * NPAIR + (0 if q < 2 else q - 1)


def gnn_moe(nc, x, tgt, gat, w_in, b_in, w_agg, w_self, b_hid, w_out, b_out,
            r_w1, r_b1, r_w2, r_b2, e_w1, e_b1, e_w2, e_b2, e_w3, e_b3, out):
    g_dram = nc.dram_tensor("g_rows", [NT * P, C], F32, kind="Internal").ap()
    g_tiles = g_dram.rearrange("(t p) c -> p t c", p=P)
    rec_dram = nc.dram_tensor("records", [P * SLOTS + P * COLS, 1], I32, kind="Internal").ap()
    f_dram = nc.dram_tensor("features", [NT * P, C], F32, kind="Internal").ap()
    f_tiles = f_dram.rearrange("(t p) c -> p t c", p=P)
    y_dram = nc.dram_tensor("expert_rows", [ROWS + ETILES * P, C], F32, kind="Internal").ap()
    y_tiles = y_dram[0:ROWS, :].rearrange("(k t p) c -> p k t c", k=TOP_K, p=P)
    x_tiles = x.rearrange("(t p) c -> p t c", p=P)
    out_tiles = out.rearrange("(t p) c -> p t c", p=P)

    with ExitStack() as ctx:
        def sb(name, shape, dt=F32):
            return ctx.enter_context(nc.sbuf_tensor(name, shape, dt))

        def sem(name):
            return ctx.enter_context(nc.semaphore(name))

        banks = [ctx.enter_context(nc.psum_tensor(f"bank{k}", [P, CUT], F32)) for k in range(8)]

        acc = sb("acc", [P, NT * AW])
        selfp = sb("selfp", [P, NT * C])
        hT_all = sb("hT_all", [P, NT * C])
        gath = sb("gath", [P, RING * AW])
        onehot = sb("onehot", [P, RING * P])
        misc = sb("misc", [P, BODY * C])
        tables = sb("tables", [P, 2 * SLOTS])
        idx_ring = sb("idx_ring", [P, RING], I32)
        wg = sb("wg", [P, (LAYERS + 1) * KC * C])
        ws = sb("ws", [P, LAYERS * KC * C])
        win = sb("win", [P, KC * C])
        bias_in = sb("bias_in", [P, KC])
        bias_hid = sb("bias_hid", [P, LAYERS * KC])
        ident = sb("ident", [P, P])
        iota_f = sb("iota_f", [P, P])
        zeros = sb("zeros", [P, 1])
        eps_t = sb("eps_t", [P, 1])
        rdeg = sb("rdeg", [P, NT])
        mv = sb("mv", [P, NT * 2])
        rstd = sb("rstd", [P, NT])
        nmr = sb("nmr", [P, NT])
        cnt = sb("cnt", [P, NT])
        base = sb("base", [P, NT])
        run_i = sb("run_i", [NT, 1], I32)
        run_j = sb("run_j", [NT, 1], I32)
        run_tiles = sb("run_tiles", [NT, 1])
        run_end = sb("run_end", [NT, 1])

        acc3 = acc[:, :].rearrange("p (t c) -> p t c", c=AW)
        gath3 = gath[:, :].rearrange("p (t c) -> p t c", c=AW)
        onehot3 = onehot[:, :].rearrange("p (t c) -> p t c", c=P)
        u_ring = gath[:, 0:BODY * C]
        g_ring = gath[:, BODY * C:2 * BODY * C]
        hT_ring = onehot[:, 0:BODY * C]
        u3 = u_ring.rearrange("p (t c) -> p t c", c=C)
        g3 = g_ring.rearrange("p (t c) -> p t c", c=C)
        hr4 = hT_ring.rearrange("p (t k c) -> p t k c", k=KC, c=P)
        hT_self = misc[:, 4 * C:5 * C]
        hs3 = hT_self.rearrange("p (k c) -> p k c", k=KC)
        win3 = win[:, :].rearrange("p (k c) -> p k c", k=KC)
        mv3 = mv[:, :].rearrange("p (t c) -> p t c", c=2)
        slot_src = tables[:, 0:SLOTS].bitcast(I32)
        slot_tgt = tables[:, SLOTS:2 * SLOTS]
        slot_node = misc[0:1, 0:SLOTS].bitcast(I32)

        stats = misc[:, BODY * C - NT * 6:BODY * C]

        xT_ring = misc[:, :]
        xr4 = xT_ring.rearrange("p (t k c) -> p t k c", k=KC, c=P)
        scratch = [selfp[:, r * COLS:(r + 1) * COLS] for r in range(11)]
        edge_t, edge_s, tile_i, temp_i = (scratch[r].bitcast(I32) for r in range(4))
        tile_h = scratch[4].bitcast(F16)[:, 0:COLS]
        cums = scratch[5:8]
        pos_sum = scratch[10]
        masks = [scratch[8 + r // 2].bitcast(F16)[:, (r % 2) * COLS:(r % 2 + 1) * COLS]
                 for r in range(3)]
        part_a = tables[:, 0:COLS]
        part_b = tables[:, COLS:2 * COLS]
        pos_hi = misc[:, 0:COLS]
        pos_lo = misc[:, COLS:2 * COLS]
        iota_h = gath[:, 2 * BODY * C:2 * BODY * C + PW // 2].bitcast(F16)
        run_wide = gath[0:NT, 2 * BODY * C + PW // 2:2 * BODY * C + PW // 2 + P]
        lower = onehot[:, BODY * C:BODY * C + P]
        lower_eq = onehot[:, BODY * C + P:BODY * C + P + NT]
        ones = onehot[:, BODY * C + P + NT:BODY * C + 2 * P + NT]
        RW = PW // 2
        p_hi = selfp[:, 0:PERM * RW].bitcast(F16).rearrange("p (r c) -> p r c", c=PW)
        p_lo = selfp[:, PERM * RW:PERM * RW + PERM * P].bitcast(F16)\
            .rearrange("p (r a c) -> p r a c", a=2, c=P)
        DEC0 = PERM * (RW + P)
        past, dec_a, dec_b, dec_c, dec_e = (
            selfp[:, DEC0 + r * SLOTS:DEC0 + (r + 1) * SLOTS] for r in range(5))
        dec_d = dec_a
        dec_bi, dec_ci, scattered_recs = (v.bitcast(I32) for v in (dec_b, dec_c, dec_e))
        AFTER = 11 * COLS
        sc_slot, sc_rec, sc_temp, sc_pad = (
            selfp[:, AFTER + r * SC_COLS:AFTER + (r + 1) * SC_COLS].bitcast(I32) for r in range(4))
        sc_ring = selfp[:, AFTER + 4 * SC_COLS:AFTER + 4 * SC_COLS + 2 * SC_RING].bitcast(I32)
        slot_ring, rec_ring = sc_ring[:, 0:SC_RING], sc_ring[:, SC_RING:2 * SC_RING]

        x2_all = selfp[:, :].rearrange("p (t c) -> p t c", c=C)
        experts = acc[:, 0:EXPERTS * WEXP]
        ex3 = experts.rearrange("p (e c) -> p e c", e=EXPERTS)
        f_ring = acc[:, EXPERTS * WEXP:EXPERTS * WEXP + BODY * C].rearrange("p (t c) -> p t c", c=C)
        x_in, y_in = u3, g3
        rhT = gath[:, 0:BODY * P]
        f_in = [gath[:, b * C:(b + 1) * C] for b in range(UNROLL)]
        y_out = [gath[:, (UNROLL + b) * C:(UNROLL + b + 1) * C] for b in range(UNROLL)]

        taken = [0]

        def room(words, parts=P):
            a = taken[0]
            taken[0] += words
            assert taken[0] <= NT * C
            return hT_all[0:parts, a:a + words]

        fT_ring = hT_all[:, 0:BODY * C]
        wbuf = [room(WEXP) for _ in range(WBUFS)]
        fT, h1T, h2T = ([room(KC * P) for _ in range(2)] for _ in range(3))
        item_lo = [room(P) for _ in range(EROW)]
        item_hi = [room(ETILES) for _ in range(EROW)]
        chosen, ranked = (room(EXPERTS * ITEMS) for _ in range(2))
        ch3, ra3 = (v.rearrange("p (e j) -> p e j", e=EXPERTS) for v in (chosen, ranked))
        item_no, eslot_lo, eslot_hi = (room(ITEMS) for _ in range(3))
        eslot_i, etemp_i = (room(ITEMS).bitcast(I32) for _ in range(2))
        gate = [room(NT) for _ in range(TOP_K)]
        item_i, node_i, pad_i, etest_i = (room(ETILES).bitcast(I32) for _ in range(4))
        pairs_in = hT_all[:, 0:4 * BODY * C].rearrange("p (b k t c) -> p b k t c", b=2, k=TOP_K, c=C)
        bout_t = onehot[:, 0:C]
        rw1 = onehot[:, C:C + KC * P].rearrange("p (k c) -> p k c", k=KC)
        rw2 = onehot[:, 2 * C:2 * C + EXPERTS]
        rb2 = onehot[:, 2 * C + EXPERTS:2 * C + 2 * EXPERTS]
        rb1 = onehot[:, 2 * C + 2 * EXPERTS:2 * C + 2 * EXPERTS + 1]
        e_lower = onehot[:, 3 * C:3 * C + P]
        e_ones = onehot[:, 3 * C + P:3 * C + 2 * P]
        e_at = 3 * C + 2 * P
        e_lower_eq, ecnt, ebase = (onehot[:, e_at + r * EXPERTS:e_at + (r + 1) * EXPERTS]
                                   for r in range(3))
        e_at += 3 * EXPERTS
        node_ring, item_ring = (onehot[:, e_at + r * UNROLL:e_at + (r + 1) * UNROLL].bitcast(I32)
                                for r in range(2))
        e_at += 2 * UNROLL
        e_past = onehot[0:EXPERTS, e_at:e_at + ETILES]
        tile_expert = onehot[0:1, e_at + ETILES:e_at + 2 * ETILES].bitcast(I32)
        e_wide = onehot[0:EXPERTS, e_at + 2 * ETILES:e_at + 2 * ETILES + P]
        NE = NT * EXPERTS
        logits, gates, rank, beat = (misc[:, r * NE:(r + 1) * NE] for r in range(4))
        topv = misc[:, 4 * NE:4 * NE + NT]
        lg3, gt3, rk3, bt3 = (v.rearrange("p (t e) -> p t e", e=EXPERTS)
                              for v in (logits, gates, rank, beat))
        top3 = topv.unsqueeze(2)

        weights_in = sem("weights_in")
        edges_in = sem("edges_in")
        x_loaded = sem("x_loaded")
        consts = sem("consts")
        dve_step = sem("dve_step")
        var_ready = sem("var_ready")
        std_ready = sem("std_ready")
        stats_ready = sem("stats_ready")
        cnt_ready = sem("cnt_ready")
        runs_counted = sem("runs_counted")
        run_sizes = sem("run_sizes")
        base_sum = sem("base_sum")
        mask_ready = sem("mask_ready")
        cum_ready = sem("cum_ready")
        msk_ready = sem("msk_ready")
        pos_added = sem("pos_added")
        p_ready = sem("p_ready")
        table_cleared = sem("table_cleared")
        sc_base = sem("sc_base")
        sc_tables = sem("sc_tables")
        sc_filled = sem("sc_filled")
        scattered = [sem(f"scattered{h}") for h in range(2)]
        table_in = sem("table_in")
        p_used = sem("p_used")
        slots_summed = sem("slots_summed")
        past_ready = sem("past_ready")
        node_sum = sem("node_sum")
        slots_ready = sem("slots_ready")
        u_ready = sem("u_ready")
        t_done = sem("t_done")
        t_evac = sem("t_evac")
        m_done = sem("m_done")
        m_evac = sem("m_evac")
        g_done = sem("g_done")
        g_evac = sem("g_evac")
        g_stored = sem("g_stored")
        g_free = sem("g_free")
        h_kept = sem("h_kept")
        acc_zeroed = sem("acc_zeroed")
        ones_ready = sem("ones_ready")
        idx_ready = sem("idx_ready")
        gathered = [sem(f"gathered{b}") for b in range(RING)]
        ticks = {eng: sem(f"ticks_{name}")
                 for name, eng in (("act", nc.scalar), ("dve", nc.vector), ("pool", nc.gpsimd))}
        onehot_ready = sem("onehot_ready")
        summed = sem("summed")
        drained = sem("drained")
        selfT_ready = sem("selfT_ready")
        self_done = sem("self_done")
        self_evac = sem("self_evac")
        deg_step = sem("deg_step")
        ffn_weights = sem("ffn_weights")
        x_reloaded = sem("x_reloaded")
        y_loaded = sem("y_loaded")
        xy_used = sem("xy_used")
        x2_ready = sem("x2_ready")
        rh_done = sem("rh_done")
        rh_ready = sem("rh_ready")
        lg_done = sem("lg_done")
        lg_evac = sem("lg_evac")
        soft_in = sem("soft_in")
        soft_exp = sem("soft_exp")
        f_stored = sem("f_stored")
        f_free = sem("f_free")
        e_consts = sem("e_consts")
        ecnt_ready = sem("ecnt_ready")
        experts_counted = sem("experts_counted")
        e_sizes = sem("e_sizes")
        ebase_sum = sem("ebase_sum")
        item_ready = sem("item_ready")
        item_used = sem("item_used")
        tables_ready = sem("tables_ready")
        rows_copied = sem("rows_copied")
        items_copied = sem("items_copied")
        fx_done = sem("fx_done")
        fx_ready = sem("fx_ready")
        words_ready = sem("words_ready")
        h1_done = sem("h1_done")
        h1_ready = sem("h1_ready")
        h2_done = sem("h2_done")
        h2_ready = sem("h2_ready")
        y_done = sem("y_done")
        y_ready = sem("y_ready")
        y_scattered = [sem(f"y_scattered{h}") for h in range(2)]
        y_free = [sem(f"y_free{h}") for h in range(2)]
        pairs_loaded = [sem(f"pairs_loaded{b}") for b in range(2)]
        first_added = sem("first_added")
        body_done = sem("body_done")
        out_stored = sem("out_stored")

        CREDIT = 1
        credited = (pos_added, f_free, y_free[0], y_free[1], xy_used, t_done, t_evac, h_kept, g_free, self_done, lg_done, g_evac,
                    m_evac, self_evac, rh_ready, lg_evac, first_added, body_done)

        N_CONSTS = 9
        FFN_LOADS = 5 * EXPERTS + 1 + 5
        SPLIT = ((0, CUT), (CUT, SLOTS))
        block = ctx.enter_context(nc.Block())

        def go(eng, semaphore, value):
            eng.wait_ge(semaphore, value)
            eng.sem_inc(ticks[eng], 1)

        def after(eng, semaphore, value):
            if not isinstance(value, int) or value > 0:
                eng.wait_ge(semaphore, value)

        @block.sync
        def _(sp):
            sp.dma_start(edge_t, tgt.rearrange("(p c) -> p c", p=P)).then_inc(edges_in, 16)
            sp.dma_start(edge_s, gat.rearrange("(p c) -> p c", p=P)).then_inc(edges_in, 16)
            for i in range(BODIES):
                sp.dma_start(acc3[:, i * BODY:(i + 1) * BODY, 0:C],
                             x_tiles[:, i * BODY:(i + 1) * BODY, :]).then_inc(x_loaded, 16)
            sp.dma_start(win3, w_in.rearrange("(k p) c -> p k c", p=P)).then_inc(weights_in, 16)
            wg4 = wg[:, :].rearrange("p (l k c) -> p l k c", k=KC, c=C)
            ws4 = ws[:, :].rearrange("p (l k c) -> p l k c", k=KC, c=C)
            for l in range(LAYERS):
                sp.dma_start(wg4[:, l], w_agg[l].rearrange("(k p) c -> p k c", p=P))\
                    .then_inc(weights_in, 16)
                sp.dma_start(ws4[:, l], w_self[l].rearrange("(k p) c -> p k c", p=P))\
                    .then_inc(weights_in, 16)
            sp.dma_start(wg4[:, LAYERS], w_out.rearrange("(k p) c -> p k c", p=P))\
                .then_inc(weights_in, 16)
            with nc.allow_non_contiguous_dma(reason="biases, one per partition"):
                sp.dma_start(bias_in[:, :], b_in.rearrange("(k p) -> p k", p=P))\
                    .then_inc(weights_in, 16)
                sp.dma_start(bias_hid[:, :], b_hid.rearrange("l (k p) -> p (l k)", p=P))\
                    .then_inc(weights_in, 16)

            def store_g(i, n):
                sp.wait_ge(g_evac, CREDIT + NPAIR * n + NPAIR)
                sp.dma_start(g_tiles[:, bass.ds(i * BODY, BODY), :], g3).then_inc(g_stored, 16)
                sp.wait_ge(g_stored, n * 16 + 16)
                sp.sem_inc(g_free, 1)

            sp.wait_ge(acc_zeroed, 1)
            by_slot = rec_dram[0:P * SLOTS, :].rearrange("(p c) a -> p (c a)", p=P)
            sp.dma_start(by_slot, acc[:, 0:SLOTS].bitcast(I32)).then_inc(table_cleared, 16)
            with sp.Fori(0, BODIES) as i:
                store_g(i, i)
            for h in range(2):
                sp.wait_ge(scattered[h], 16 * SC_HALF * SORT_STEPS)
            sp.wait_ge(sc_filled, 2 * SORT_STEPS)
            sp.dma_start(scattered_recs, by_slot).then_inc(table_in, 16)
            with sp.Fori(0, LAYERS) as l:
                with sp.Fori(0, BODIES) as i:
                    store_g(i, l * BODIES + i + BODIES)

            sp.wait_ge(acc_zeroed, BODIES * (LAYERS + 1))
            for w, src in enumerate((e_w1, e_w2, e_w3)):
                for e in range(EXPERTS):
                    sp.dma_start(ex3[:, e, w * KC * C:(w + 1) * KC * C]
                                 .rearrange("p (k c) -> p k c", k=KC),
                                 src[e].rearrange("(k p) c -> p k c", p=P)).then_inc(ffn_weights, 16)
            with nc.allow_non_contiguous_dma(reason="biases, one per partition"):
                for w, b in enumerate((e_b1, e_b2)):
                    at = 3 * KC * C + w * KC
                    for e in range(EXPERTS):
                        sp.dma_start(ex3[:, e, at:at + KC], b[e].rearrange("(k p) -> p k", p=P))\
                            .then_inc(ffn_weights, 16)
            sp.dma_start(ex3[:, :, WEXP - C:WEXP], e_b3.unsqueeze(0).to_broadcast([P, EXPERTS, C]))\
                .then_inc(ffn_weights, 16)
            sp.wait_ge(g_stored, 16 * BODIES * (LAYERS + 1))
            sp.wait_ge(h_kept, CREDIT + BODIES * (LAYERS + 1))
            sp.dma_start(rw1, r_w1.rearrange("(k p) c -> p k c", p=P)).then_inc(ffn_weights, 16)
            with nc.allow_non_contiguous_dma(reason="a bias, one per partition"):
                sp.dma_start(rb1, r_b1.rearrange("(p a) -> p a", a=1)).then_inc(ffn_weights, 16)
            sp.dma_start(rw2, r_w2).then_inc(ffn_weights, 16)
            sp.dma_start(rb2, r_b2.unsqueeze(0).to_broadcast([P, EXPERTS])).then_inc(ffn_weights, 16)
            sp.dma_start(bout_t, b_out.unsqueeze(0).to_broadcast([P, C])).then_inc(ffn_weights, 16)
            with sp.Fori(0, BODIES) as i:
                sp.wait_ge(xy_used, CREDIT + i)
                sp.dma_start(x_in, x_tiles[:, bass.ds(i * BODY, BODY), :]).then_inc(x_reloaded, 16)
                sp.dma_start(y_in, g_tiles[:, bass.ds(i * BODY, BODY), :]).then_inc(y_loaded, 16)
            with sp.Fori(0, BODIES) as i:
                sp.wait_ge(u_ready, (i + (LAYERS + 1) * BODIES) * BODY + BODY)
                sp.dma_start(f_tiles[:, bass.ds(i * BODY, BODY), :], f_ring).then_inc(f_stored, 16)
                sp.wait_ge(f_stored, i * 16 + 16)
                sp.sem_inc(f_free, 1)

            with sp.Fori(0, ESTEPS) as i:
                for h in range(2):
                    sp.wait_ge(y_scattered[h], i * (16 * EHALF) + 16 * EHALF)
                    sp.sem_inc(y_free[h], 1)

            def load_pairs(i, b):
                for k in range(TOP_K):
                    sp.dma_start(pairs_in[:, b, k], y_tiles[:, k, i * BODY:(i + 1) * BODY, :])\
                        .then_inc(pairs_loaded[b], 16)

            sp.wait_ge(y_ready, ETILES)
            for i in range(BODIES):
                if i >= 2:
                    sp.wait_ge(body_done, CREDIT + i - 1)
                load_pairs(i, i % 2)
                if i >= 1:
                    sp.wait_ge(body_done, CREDIT + i)
                    sp.dma_start(out_tiles[:, (i - 1) * BODY:i * BODY, :],
                                 x2_all[:, (i - 1) * BODY:i * BODY, :]).then_inc(out_stored, 16)
            sp.wait_ge(body_done, CREDIT + BODIES)
            sp.dma_start(out_tiles[:, (BODIES - 1) * BODY:, :], x2_all[:, (BODIES - 1) * BODY:, :])\
                .then_inc(out_stored, 16)
            sp.wait_ge(out_stored, 16 * BODIES)

        @block.gpsimd
        def _(pool):
            pool.iota(iota_f[:, :], [[1, P]], base=0, channel_multiplier=0,
                      allow_small_or_imprecise_dtypes=True).then_inc(consts, 1)
            pool.iota(iota_h, [[1, PW]], base=0, channel_multiplier=0,
                      allow_small_or_imprecise_dtypes=True).then_inc(consts, 1)
            pool.memset(zeros[:, :], 0.0).then_inc(consts, 1)
            pool.memset(eps_t[:, :], EPS).then_inc(consts, 1)
            pool.memset(ones, 1.0).then_inc(consts, 1)
            pool.memset(ident[:, :], 0.0).then_inc(consts, 1)
            pool.wait_ge(consts, 6)
            pool.affine_select(out=ident[:, :], in_=ident[:, :], compare_op=ALU.not_equal, fill=1.0,
                               base=0, pattern=[[-1, P]], channel_multiplier=1).then_inc(consts, 1)
            pool.affine_select(out=lower, in_=ones, compare_op=ALU.is_gt, fill=0.0,
                               base=0, pattern=[[1, P]], channel_multiplier=-1).then_inc(consts, 1)
            pool.affine_select(out=lower_eq, in_=ones[:, 0:NT], compare_op=ALU.is_ge, fill=0.0,
                               base=0, pattern=[[1, NT]], channel_multiplier=-1).then_inc(consts, 1)

            def zero_sums(i, n):
                pool.wait_ge(u_ready, n * BODY + BODY)
                pool.tensor_copy(acc[:, bass.ds(i * (BODY * AW), BODY * AW)],
                                 zeros[:, 0:1].to_broadcast([P, BODY * AW])).then_inc(acc_zeroed, 1)

            with pool.Fori(0, BODIES) as i:
                for b in range(BODY):
                    pool.wait_ge(cum_ready, i * BODY + b + 1)
                    cum = cums[cum_of(b)]
                    pool.tensor_tensor(cum, cum, masks[cum_of(b)], ALU.mult).then_inc(msk_ready, 1)
                zero_sums(i, i)

            pool.iota(sc_pad, [[1, SC_COLS]], base=P * SLOTS + PE_COLS, channel_multiplier=COLS)\
                .then_inc(sc_base, 1)
            pool.wait_ge(table_cleared, 16)
            with pool.Fori(0, SORT_STEPS) as i:
                for b in range(SC_RING):
                    h = b // SC_HALF
                    if b % SC_HALF == 0:
                        go(pool, sc_filled, i * 2 + (h + 1))
                    pool.indirect_dma_start(
                        rec_dram, bass.IndirectOffsetOnAxis(ap=slot_ring[:, b:b + 1], axis=0),
                        rec_ring[:, b:b + 1], None).then_inc(scattered[h], 16)

            pool.wait_ge(slots_ready, 1)
            with pool.Fori(0, LAYERS) as l:
                go(pool, g_stored, l * (16 * BODIES) + 16 * BODIES)
                pool.memset(gath3[:, :, C:AW], 1.0).then_inc(ones_ready, 1)
                go(pool, ones_ready, l + 1)
                with pool.Fori(0, STEPS) as i:
                    n = l * STEPS + i
                    for b in range(RING):
                        if b == 0:
                            pool.wait_ge(idx_ready, n * 2 + 1)
                        if b == HALF:
                            pool.wait_ge(idx_ready, n * 2 + 2)
                        go(pool, summed, n * RING + (b + 1))
                        pool.indirect_dma_start(
                            gath3[:, b, 0:C], None, g_dram,
                            bass.IndirectOffsetOnAxis(ap=idx_ring[:, b:b + 1], axis=0))\
                            .then_inc(gathered[b], 16)
                with pool.Fori(0, BODIES) as i:
                    zero_sums(i, l * BODIES + i + BODIES)

            pool.wait_ge(g_evac, CREDIT + NPAIR * BODIES * (LAYERS + 1))
            pool.wait_ge(h_kept, CREDIT + BODIES * (LAYERS + 1))
            pool.memset(e_ones, 1.0).then_inc(e_consts, 1)
            pool.iota(item_no, [[P, ITEMS]], base=1, channel_multiplier=1,
                      allow_small_or_imprecise_dtypes=True).then_inc(e_consts, 1)
            pool.iota(pad_i, [[P, ETILES]], base=ROWS, channel_multiplier=1).then_inc(e_consts, 1)
            pool.wait_ge(e_consts, 3)
            pool.affine_select(out=e_lower, in_=e_ones, compare_op=ALU.is_gt, fill=0.0,
                               base=0, pattern=[[1, P]], channel_multiplier=-1).then_inc(e_consts, 1)
            pool.affine_select(out=e_lower_eq, in_=e_ones[:, 0:EXPERTS], compare_op=ALU.is_ge,
                               fill=0.0, base=0, pattern=[[1, EXPERTS]],
                               channel_multiplier=-1).then_inc(e_consts, 1)

            def gather_tile(b):
                pool.indirect_dma_start(
                    f_in[b], None, f_dram,
                    bass.IndirectOffsetOnAxis(ap=node_ring[:, b:b + 1], axis=0))\
                    .then_inc(gathered[b], 16)

            def copy_rows(i):
                for b in range(UNROLL):
                    go(pool, gathered[b], (i + LAYERS * STEPS) * 16)
                pool.tensor_copy(node_ring, node_i[:, bass.ds(i * UNROLL, UNROLL)])\
                    .then_inc(rows_copied, 1)
                go(pool, rows_copied, i + 1)

            def copy_items(i):
                if not isinstance(i, int):
                    for h in range(2):
                        go(pool, y_scattered[h], i * (16 * EHALF))
                pool.tensor_copy(item_ring, item_i[:, bass.ds(i * UNROLL, UNROLL)])\
                    .then_inc(items_copied, 1)
                go(pool, items_copied, i + 1)

            def scatter_tile(i, b):
                go(pool, y_ready, i * UNROLL + (b + 1))
                pool.indirect_dma_start(
                    y_dram, bass.IndirectOffsetOnAxis(ap=item_ring[:, b:b + 1], axis=0),
                    y_out[b], None).then_inc(y_scattered[b // EHALF], 16)

            def expert_step(i):
                copy_rows(i + 1)
                copy_items(i)
                for b in range(UNROLL):
                    go(pool, fx_done, i * UNROLL + (b + 1))
                    gather_tile(b)
                    scatter_tile(i, b)

            pool.wait_ge(f_stored, 16 * BODIES)
            pool.wait_ge(tables_ready, 1)
            copy_rows(0)
            for b in range(UNROLL):
                gather_tile(b)
            expert_step(0)
            with pool.Fori(0, ESTEPS - 2) as i:
                expert_step(i + 1)
            pool.wait_ge(items_copied, ESTEPS - 1)
            for h in range(2):
                pool.wait_ge(y_scattered[h], (ESTEPS - 1) * (16 * EHALF))
            pool.tensor_copy(item_ring, item_i[:, ETILES - UNROLL:]).then_inc(items_copied, 1)
            pool.wait_ge(items_copied, ESTEPS)
            for b in range(UNROLL):
                scatter_tile(ESTEPS - 1, b)

        @block.scalar
        def _(act):
            act.wait_ge(consts, N_CONSTS)
            act.wait_ge(var_ready, 1)
            act.activation(rstd[:, :], mv3[:, :, 1], ACT.Sqrt, bias=eps_t[:, 0:1])\
                .then_inc(std_ready, 1)
            act.wait_ge(weights_in, 16 * (2 + 2 * LAYERS + 2))

            def evac_g(n):
                act.wait_ge(g_free, CREDIT + n)
                for q, (a, z) in enumerate(PAIRS):
                    act.wait_ge(g_done, NPAIR * n + (q + 1))
                    act.copy(g_ring[:, a * C:z * C], banks[G_BANK[q]][:, 0:(z - a) * C])\
                        .then_inc(g_evac, 1)

            def keep_h(i, n, ready):
                go(act, ready, CREDIT + NPAIR * n + NPAIR)
                act.copy(hT_all[:, bass.ds(i * (BODY * C), BODY * C)], hT_ring).then_inc(h_kept, 1)

            def by_tile(bank, n):
                return bank[:, 0:n * C].rearrange("p (t k c) -> p t k c", k=KC, c=P)

            act.wait_ge(stats_ready, 1)
            with act.Fori(0, BODIES) as i:
                act.wait_ge(t_done, CREDIT + i * NPAIR)
                for b in range(BODY):
                    act.activation(u3[:, b], acc[:, bass.ds(i * (BODY * AW) + b * AW, C)],
                                   ACT.Identity, bias=nmr[:, bass.ds(i * BODY + b, 1)],
                                   scale=rstd[:, bass.ds(i * BODY + b, 1)]).then_inc(u_ready, 1)
                for q, (a, z) in enumerate(PAIRS):
                    act.wait_ge(t_done, CREDIT + i * NPAIR + (q + 1))
                    act.copy(xT_ring[:, a * C:z * C], banks[T_BANK[q]][:, 0:(z - a) * C])\
                        .then_inc(t_evac, 1)
                act.wait_ge(h_kept, CREDIT + i)
                for q, (a, z) in enumerate(PAIRS):
                    act.wait_ge(m_done, i * NPAIR + (q + 1))
                    for k in range(KC):
                        ins = act.activation(hr4[:, a:z, k], by_tile(banks[M_BANK[q]], z - a)[:, :, k],
                                             ACT.Identity, bias=bias_in[:, k:k + 1])
                    ins.then_inc(m_evac, 1)
                keep_h(i, i, m_evac)
                evac_g(i)

            def fill_half(h, step):
                ring = slice(h * SC_HALF, (h + 1) * SC_HALF)
                at = bass.ds(step * SC_RING + h * SC_HALF, SC_HALF)
                act.copy(slot_ring[:, ring], sc_slot[:, at])
                act.copy(rec_ring[:, ring], sc_rec[:, at]).then_inc(sc_filled, 1)

            act.wait_ge(sc_tables, 1)
            for h in range(2):
                fill_half(h, 0)
            with act.Fori(0, SORT_STEPS - 1) as i:
                for h in range(2):
                    go(act, scattered[h], (i + 1) * (16 * SC_HALF))
                    fill_half(h, i + 1)

            act.wait_ge(slots_ready, 1)
            with act.Fori(0, LAYERS) as l:
                act.wait_ge(h_kept, CREDIT + l * BODIES + BODIES)
                with act.Fori(0, STEPS) as i:
                    n = l * STEPS + i
                    act.wait_ge(summed, n * RING + HALF)
                    act.copy(idx_ring[:, 0:HALF], slot_src[:, bass.ds(i * RING, HALF)])\
                        .then_inc(idx_ready, 1)
                    act.wait_ge(self_done, CREDIT + n)
                    act.copy(hT_self, hT_all[:, bass.ds(i * C, C)]).then_inc(selfT_ready, 1)
                    act.wait_ge(summed, n * RING + RING)
                    act.copy(idx_ring[:, HALF:RING], slot_src[:, bass.ds(i * RING + HALF, RING - HALF)])\
                        .then_inc(idx_ready, 1)
                    act.wait_ge(self_done, CREDIT + n + 1)
                    act.copy(selfp[:, bass.ds(i * C, C)], banks[5][:, 0:C]).then_inc(self_evac, 1)
                with act.Fori(0, BODIES) as i:
                    n = l * BODIES + i + BODIES
                    act.wait_ge(h_kept, CREDIT + n)
                    for q, (a, z) in enumerate(PAIRS):
                        go(act, t_done, CREDIT + n * NPAIR + (q + 1))
                        for k in range(KC):
                            ins = act.activation(hr4[:, a:z, k],
                                                 by_tile(banks[T_BANK[q]], z - a)[:, :, k],
                                                 ACT.Relu, bias=bias_hid[:, bass.ds(l * KC + k, 1)])
                        ins.then_inc(t_evac, 1)
                    keep_h(i, n, t_evac)
                    evac_g(n)

            act.wait_ge(var_ready, 2)
            act.activation(rstd[:, :], mv3[:, :, 1], ACT.Sqrt, bias=eps_t[:, 0:1])\
                .then_inc(std_ready, 1)
            act.wait_ge(ffn_weights, 16 * FFN_LOADS)
            fT3 = fT_ring.rearrange("p (k n) -> p k n", k=KC)
            with act.Fori(0, BODIES) as i:
                n = i + (LAYERS + 1) * BODIES
                act.wait_ge(rh_ready, CREDIT + i * 2)
                for q, (a, z) in enumerate(PAIRS):
                    act.wait_ge(t_done, CREDIT + n * NPAIR + (q + 1))
                    act.copy(fT3[:, :, a * P:z * P],
                             banks[T_BANK[q]][:, 0:(z - a) * C].rearrange("p (k n) -> p k n", k=KC))\
                        .then_inc(t_evac, 1)
                act.wait_ge(lg_done, CREDIT + i)
                for h in range(2):
                    act.wait_ge(rh_done, i * 2 + (h + 1))
                    act.activation(rhT[:, h * FH:(h + 1) * FH], banks[5 + h][:, 0:FH], ACT.Relu,
                                   bias=rb1).then_inc(rh_ready, 1)
            for k in range(2):
                act.wait_ge(soft_in, k + 1)
                act.activation(gates, gates, ACT.Exp).then_inc(soft_exp, 1)

            def features_out(n, b):
                after(act, fx_done, n + 1)
                after(act, h1_done, n - 1)
                act.copy(fT[b % 2], banks[b % 2][:, 0:C]).then_inc(fx_ready, 1)

            def hidden_out(n, b, w, dst, done, ready, used):
                after(act, done, n + 1)
                after(act, used, n - 1)
                for m in range(KC):
                    at = 3 * KC * C + w * KC + m
                    ins = act.activation(dst[b % 2][:, m * P:(m + 1) * P],
                                         banks[2 + 2 * w + b % 2][:, m * P:(m + 1) * P], ACT.Relu,
                                         bias=wbuf[b % WBUFS][:, at:at + 1])
                ins.then_inc(ready, 1)

            def act_slot(n, b, first=0, last=WBUFS):
                if first <= 0 < last:
                    features_out(n, b)
                if first <= 1 < last:
                    hidden_out(n - 1, b - 1, 0, h1T, h1_done, h1_ready, h2_done)
                if first <= 2 < last:
                    hidden_out(n - 2, b - 2, 1, h2T, h2_done, h2_ready, y_done)

            for b in range(UNROLL):
                act_slot(b, b, last=b + 1)
            with act.Fori(0, ESTEPS - 1) as i:
                for b in range(UNROLL):
                    act_slot((i + 1) * UNROLL + b, b)
            for b in range(2):
                act_slot(ETILES + b, b, first=b + 1)

        @block.tensor
        def _(pe):
            pe.wait_ge(consts, N_CONSTS)
            pe.sem_inc(summed, RING)
            for semaphore in credited:
                pe.sem_inc(semaphore, CREDIT)

            pe.wait_ge(cnt_ready, 1)
            pe.matmul(banks[0][0:NT, 0:1], cnt[:, :], ones[:, 0:1], start=True, stop=True)\
                .then_inc(runs_counted, 1)
            pe.wait_ge(run_sizes, 1)
            pe.matmul(banks[1][:, 0:NT], run_wide, lower[0:NT, 0:NT], start=True, stop=False)
            pe.matmul(banks[1][:, 0:NT], lower, cnt[:, :], start=False, stop=True)
            pe.matmul(banks[2][0:NT, 0:1], lower_eq[0:NT, 0:NT], run_tiles[:, :],
                      start=True, stop=True).then_inc(base_sum, 1)

            def transposes(n):
                for q, (a, z) in enumerate(PAIRS):
                    pe.wait_ge(u_ready, n * BODY + z)
                    pe.wait_ge(t_evac, CREDIT + t_freed(n, q))
                    for t in range(a, z):
                        for k in range(KC):
                            at = ((t - a) * KC + k) * P
                            ins = pe.transpose(banks[T_BANK[q]][:, at:at + P],
                                               u3[:, t, k * P:(k + 1) * P], ident[:, :])
                    ins.then_inc(t_done, 1)

            def g_products(n, w, ready):
                for q, (a, z) in enumerate(PAIRS):
                    pe.wait_ge(ready, CREDIT + n * NPAIR + (q + 1))
                    pe.wait_ge(g_evac, CREDIT + n * NPAIR + (1 if q == 3 else 0))
                    for t in range(a, z):
                        for k in range(KC):
                            ins = pe.matmul(banks[G_BANK[q]][:, (t - a) * C:(t - a + 1) * C],
                                            hr4[:, t, k], wg[:, bass.ds(w * (KC * C) + k * C, C)],
                                            start=(k == 0), stop=(k == KC - 1))
                    ins.then_inc(g_done, 1)

            def with_zeros(bank, width, opens):
                return pe.matmul(banks[bank][:, 0:width], ident[:, :],
                                 zeros[:, :].to_broadcast([P, width]), start=opens,
                                 stop=not opens, skip_group_check=True)

            pe.wait_ge(weights_in, 16 * (2 + 2 * LAYERS + 2))
            with pe.Fori(0, BODIES) as i:
                transposes(i)
                for q, (a, z) in enumerate(PAIRS):
                    pe.wait_ge(t_evac, CREDIT + i * NPAIR + (q + 1))
                    pe.wait_ge(m_evac, CREDIT + i * NPAIR + (1 if q == 3 else 0))
                    for t in range(a, z):
                        for m in range(KC):
                            at = ((t - a) * KC + m) * P
                            for k in range(KC):
                                ins = pe.matmul(banks[M_BANK[q]][:, at:at + P],
                                                win3[:, k, m * P:(m + 1) * P], xr4[:, t, k],
                                                start=(k == 0), stop=(k == KC - 1))
                    ins.then_inc(m_done, 1)
                g_products(i, 0, m_evac)

            pe.wait_ge(g_evac, CREDIT + NPAIR * BODIES)
            for part in range(2):
                for k, (a, z) in enumerate(SPLIT):
                    with_zeros(2 * part + k, z - a, True)
            pe.sem_inc(p_used, PERM)
            with pe.Fori(0, PE_COLS // PERM) as i:
                for b in range(PERM):
                    pe.wait_ge(p_ready, i * PERM + (b + 2))
                    for part in range(2):
                        for k, (a, z) in enumerate(SPLIT):
                            ins = pe.matmul(banks[2 * part + k][:, 0:z - a], p_lo[:, b, part],
                                            p_hi[:, b, a:z], start=False, stop=False,
                                            skip_group_check=True)
                    ins.then_inc(p_used, 1)
            for part in range(2):
                for k, (a, z) in enumerate(SPLIT):
                    ins = with_zeros(2 * part + k, z - a, False)
            ins.then_inc(p_used, 1)
            pe.wait_ge(past_ready, 1)
            for k, (a, z) in enumerate(SPLIT):
                ins = pe.matmul(banks[6 + k][:, 0:z - a], ones[0:NT, :], past[0:NT, a:z],
                                start=True, stop=True)
            ins.then_inc(node_sum, 1)

            with pe.Fori(0, LAYERS) as l:
                with pe.Fori(0, STEPS) as i:
                    n = l * STEPS + i
                    for b in range(RING):
                        pe.wait_ge(gathered[b], n * 16 + 16)
                        if b == 0:
                            pe.wait_ge(onehot_ready, n * 2 + 1)
                        if b == HALF:
                            pe.wait_ge(onehot_ready, n * 2 + 2)
                        pe.wait_ge(drained, n * RING + (b + 1))
                        pe.matmul(banks[bank_of(b)][:, 0:AW], onehot3[:, b], gath3[:, b],
                                  start=True, stop=True).then_inc(summed, 1)
                        if b == RING // 2:
                            pe.wait_ge(selfT_ready, n + 1)
                            pe.wait_ge(self_evac, CREDIT + n)
                            for k in range(KC):
                                ins = pe.matmul(banks[5][:, 0:C], hs3[:, k],
                                                ws[:, bass.ds(l * (KC * C) + k * C, C)],
                                                start=(k == 0), stop=(k == KC - 1))
                            ins.then_inc(self_done, 1)
                with pe.Fori(0, BODIES) as i:
                    n = l * BODIES + i + BODIES
                    transposes(n)
                    g_products(n, l + 1, t_evac)

            pe.wait_ge(ffn_weights, 16 * FFN_LOADS)
            pe.wait_ge(g_evac, CREDIT + NPAIR * BODIES * (LAYERS + 1))
            with pe.Fori(0, BODIES) as i:
                n = i + (LAYERS + 1) * BODIES
                for q, (a, z) in enumerate(PAIRS):
                    pe.wait_ge(u_ready, n * BODY + z)
                    pe.wait_ge(t_evac, CREDIT + t_freed(n, q))
                    for t in range(a, z):
                        for k in range(KC):
                            at = (k * (z - a) + t - a) * P
                            ins = pe.transpose(banks[T_BANK[q]][:, at:at + P],
                                               f_ring[:, t, k * P:(k + 1) * P], ident[:, :])
                    ins.then_inc(t_done, 1)
                pe.wait_ge(t_evac, CREDIT + n * NPAIR + NPAIR)
                pe.wait_ge(rh_ready, CREDIT + i * 2)
                for h in range(2):
                    for k in range(KC):
                        ins = pe.matmul(banks[5 + h][:, 0:FH], rw1[:, k],
                                        fT_ring[:, k * 2 * FH + h * FH:k * 2 * FH + (h + 1) * FH],
                                        start=(k == 0), stop=(k == KC - 1))
                    ins.then_inc(rh_done, 1)
                pe.wait_ge(rh_ready, CREDIT + i * 2 + 2)
                pe.wait_ge(lg_evac, CREDIT + i)
                for t in range(BODY):
                    ins = pe.matmul(banks[7][:, t * EXPERTS:(t + 1) * EXPERTS],
                                    rhT[:, t * P:(t + 1) * P], rw2, start=True, stop=True)
                ins.then_inc(lg_done, 1)

            pe.wait_ge(e_consts, 5)
            pe.wait_ge(ecnt_ready, 1)
            pe.matmul(banks[0][0:EXPERTS, 0:1], ecnt, e_ones[:, 0:1], start=True, stop=True)\
                .then_inc(experts_counted, 1)
            pe.wait_ge(e_sizes, 1)
            pe.matmul(banks[1][:, 0:EXPERTS], e_wide, e_lower[0:EXPERTS, 0:EXPERTS],
                      start=True, stop=False)
            pe.matmul(banks[1][:, 0:EXPERTS], e_lower, ecnt, start=False, stop=True)
            pe.matmul(banks[2][0:EXPERTS, 0:1], e_lower_eq[0:EXPERTS, 0:EXPERTS],
                      run_tiles[0:EXPERTS, :], start=True, stop=True).then_inc(ebase_sum, 1)
            pe.matmul(banks[3][:, 0:ETILES], ident[:, :], zeros[:, :].to_broadcast([P, ETILES]),
                      start=True, stop=False, skip_group_check=True)
            pe.sem_inc(item_used, EROW)
            with pe.Fori(0, ITEMS // EROW) as i:
                for b in range(EROW):
                    pe.wait_ge(item_ready, i * EROW + (b + 1))
                    pe.matmul(banks[3][:, 0:ETILES], item_lo[b], item_hi[b], start=False, stop=False,
                              skip_group_check=True).then_inc(item_used, 1)
            pe.matmul(banks[3][:, 0:ETILES], ident[:, :], zeros[:, :].to_broadcast([P, ETILES]),
                      start=False, stop=True, skip_group_check=True)
            pe.matmul(banks[4][:, 0:ETILES], e_ones[0:EXPERTS, :], e_past, start=True, stop=True)\
                .then_inc(item_used, 1)

            def turn(n, b, step):
                pe.wait_ge(gathered[b], (step + LAYERS * STEPS + 1) * 16)
                after(pe, fx_ready, n - 1)
                for k in range(KC):
                    ins = pe.transpose(banks[b % 2][:, k * P:(k + 1) * P],
                                       f_in[b][:, k * P:(k + 1) * P], ident[:, :])
                ins.then_inc(fx_done, 1)

            def hidden(n, b, w, src, src_ready, done, bank_read):
                after(pe, src_ready, n + 1)
                if w == 0:
                    after(pe, words_ready, n + 1)
                after(pe, bank_read, n - 1)
                for m in range(KC):
                    for k in range(KC):
                        at = w * KC * C + k * C + m * P
                        ins = pe.matmul(banks[2 + 2 * w + b % 2][:, m * P:(m + 1) * P],
                                        wbuf[b % WBUFS][:, at:at + P],
                                        src[b % 2][:, k * P:(k + 1) * P],
                                        start=(k == 0), stop=(k == KC - 1))
                ins.then_inc(done, 1)

            def rows_out(n, b):
                after(pe, h2_ready, n + 1)
                after(pe, y_ready, n - 1)
                for k in range(KC):
                    at = 2 * KC * C + k * C
                    ins = pe.matmul(banks[6 + b % 2][:, 0:C], h2T[b % 2][:, k * P:(k + 1) * P],
                                    wbuf[b % WBUFS][:, at:at + C], start=(k == 0), stop=(k == KC - 1))
                ins.then_inc(y_done, 1)

            def pe_slot(n, b, step, first=0, last=WBUFS):
                if first <= 0 < last:
                    turn(n, b, step)
                if first <= 1 < last:
                    hidden(n - 1, b - 1, 0, fT, fx_ready, h1_done, h1_ready)
                if first <= 2 < last:
                    hidden(n - 2, b - 2, 1, h1T, h1_ready, h2_done, h2_ready)
                if first <= 3 < last:
                    rows_out(n - 3, b - 3)

            pe.wait_ge(tables_ready, 1)
            for b in range(UNROLL):
                pe_slot(b, b, 0, last=b + 1)
            with pe.Fori(0, ESTEPS - 1) as i:
                for b in range(UNROLL):
                    pe_slot((i + 1) * UNROLL + b, b, i + 1)
            for b in range(3):
                pe_slot(ETILES + b, b, 0, first=b + 1)

        @block.vector
        def _(dve):
            steps = [0]

            def link(ins):
                steps[0] += 1
                ins.then_inc(dve_step, 1)
                dve.wait_ge(dve_step, steps[0])

            dve.wait_ge(edges_in, 32)
            link(nc.vector.tensor_scalar(tile_i, edge_t, 7, None, ALU.arith_shift_right))
            link(nc.vector.tensor_copy(tile_h, tile_i))
            for b in range(NT):
                ins = nc.vector.tensor_scalar(masks[0], tile_h, float(b), 0.0,
                                              ALU.is_equal, ALU.add, accum_out=cnt[:, b:b + 1])
                if b < NT - 1:
                    link(ins)
            ins.then_inc(cnt_ready, 1)
            link(nc.vector.tensor_scalar(tile_i, edge_s, 3, None, ALU.arith_shift_right))
            link(nc.vector.tensor_copy(part_a, tile_i))
            link(nc.vector.tensor_scalar(temp_i, edge_s, 7, 7, ALU.bitwise_and,
                                         ALU.logical_shift_left))
            link(nc.vector.tensor_scalar(edge_t, edge_t, P - 1, None, ALU.bitwise_and))
            link(nc.vector.tensor_tensor(temp_i, temp_i, edge_t, ALU.add))
            link(nc.vector.tensor_scalar(part_b, temp_i, 1.0, None, ALU.add))

            dve.wait_ge(runs_counted, 1)
            link(nc.vector.tensor_scalar(run_i[:, :], banks[0][0:NT, 0:1], float(P - 1), None, ALU.add))
            link(nc.vector.tensor_scalar(run_j[:, :], run_i[:, :], 7, None, ALU.arith_shift_right))
            link(nc.vector.tensor_copy(run_tiles[:, :], run_j[:, :]))
            dve.wait_ge(consts, N_CONSTS)
            nc.vector.tensor_scalar(run_wide, ones[0:NT, :], run_tiles[:, 0:1], float(P),
                                    ALU.mult, ALU.mult).then_inc(run_sizes, 1)
            dve.wait_ge(base_sum, 1)
            link(nc.vector.tensor_copy(base[:, :], banks[1][:, 0:NT]))
            link(nc.vector.tensor_copy(run_end[:, :], banks[2][0:NT, 0:1]))

            def row_stats(rows):
                for t in range(NT):
                    ins = nc.vector.bn_stats(stats[:, t * 6:(t + 1) * 6], rows(t))
                link(ins)
                for t in range(NT):
                    ins = nc.vector.bn_aggr(mv[:, 2 * t:2 * t + 2], stats[:, t * 6:(t + 1) * 6])
                ins.then_inc(var_ready, 1)

            def row_scales(n):
                dve.wait_ge(std_ready, n)
                link(nc.vector.reciprocal(rstd[:, :], rstd[:, :]))
                return nc.vector.scalar_tensor_tensor(nmr[:, :], mv3[:, :, 0], -1.0, rstd[:, :],
                                                      ALU.mult, ALU.mult)

            dve.wait_ge(x_loaded, 16 * BODIES)
            row_stats(lambda t: acc3[:, t, 0:C])
            row_scales(1).then_inc(stats_ready, 1)

            link(nc.vector.memset(pos_sum, 0.0))
            link(nc.vector.memset(cums[2], 0.0))
            dve.sem_inc(msk_ready, 1)

            def add_counts(b):
                return nc.vector.tensor_tensor(pos_sum, pos_sum, cums[cum_of(b)], ALU.add)

            with dve.Fori(0, BODIES) as i:
                for b in range(BODY):
                    n = i * BODY + b
                    go(dve, pos_added, CREDIT + n)
                    mask = masks[cum_of(b)]
                    nc.vector.tensor_scalar(mask, tile_h, iota_f[:, bass.ds(i * BODY + b, 1)], None,
                                            ALU.is_equal).then_inc(mask_ready, 1)
                    dve.wait_ge(mask_ready, n + 1)
                    nc.vector.tensor_tensor_scan(cums[cum_of(b)], mask, mask,
                                                 base[:, bass.ds(i * BODY + b, 1)],
                                                 ALU.add, ALU.bypass).then_inc(cum_ready, 1)
                    dve.wait_ge(msk_ready, n + 1)
                    add_counts((b - 1) % BODY).then_inc(pos_added, 1)

            dve.wait_ge(pos_added, CREDIT + NT)
            dve.wait_ge(msk_ready, NT + 1)
            link(add_counts(BODY - 1))
            dve.wait_ge(m_done, NPAIR * BODIES)
            slot_i, temp_j = (cums[r].bitcast(I32) for r in range(2))
            link(nc.vector.tensor_scalar(slot_i, pos_sum, -1.0, None, ALU.add))
            link(nc.vector.tensor_scalar(temp_j, slot_i, 7, None, ALU.arith_shift_right))
            link(nc.vector.tensor_copy(pos_hi, temp_j))
            link(nc.vector.tensor_scalar(temp_j, slot_i, P - 1, None, ALU.bitwise_and))
            link(nc.vector.tensor_copy(pos_lo, temp_j))
            tail = slice(PE_COLS, COLS)
            link(nc.vector.tensor_scalar(sc_rec, part_a[:, tail], 1024.0, None, ALU.mult))
            link(nc.vector.tensor_tensor(sc_rec, sc_rec, part_b[:, tail], ALU.add))
            link(nc.vector.tensor_scalar(sc_slot, pos_lo[:, tail], float(SLOTS), None, ALU.mult))
            link(nc.vector.tensor_tensor(sc_slot, sc_slot, pos_hi[:, tail], ALU.add))
            link(nc.vector.tensor_scalar(sc_temp, pos_hi[:, tail], 0.0, None, ALU.is_lt))
            dve.wait_ge(sc_base, 1)
            link(nc.vector.tensor_tensor(sc_pad, sc_pad, sc_slot, ALU.subtract))
            link(nc.vector.tensor_tensor(sc_pad, sc_pad, sc_temp, ALU.mult))
            nc.vector.tensor_tensor(sc_slot, sc_slot, sc_pad, ALU.add).then_inc(sc_tables, 1)
            dve.sem_inc(p_ready, 1)
            with dve.Fori(0, PE_COLS // PERM) as i:
                for b in range(PERM):
                    dve.wait_ge(p_used, i * PERM + (b + 1))
                    at = bass.ds(i * PERM + b, 1)
                    for part, value in enumerate((part_a, part_b)):
                        nc.vector.tensor_scalar(p_lo[:, b, part], iota_h[:, 0:P], pos_lo[:, at],
                                                value[:, at], ALU.is_equal, ALU.mult)
                    nc.vector.tensor_scalar(p_hi[:, b], iota_h, pos_hi[:, at], None,
                                            ALU.is_equal).then_inc(p_ready, 1)

            nc.vector.tensor_scalar(past[0:NT, :], iota_h[0:NT, 0:SLOTS], run_end[:, 0:1], None,
                                    ALU.is_ge).then_inc(past_ready, 1)
            dve.wait_ge(p_used, PE_COLS + PERM + 1)
            for k, (a, z) in enumerate(SPLIT):
                link(nc.vector.tensor_scalar(dec_a[:, a:z], banks[k][:, 0:z - a], 1024.0, None,
                                             ALU.mult))
                link(nc.vector.tensor_tensor(dec_a[:, a:z], dec_a[:, a:z], banks[2 + k][:, 0:z - a],
                                             ALU.add))
            dve.wait_ge(table_in, 16)
            link(nc.vector.tensor_tensor(dec_a, dec_a, scattered_recs, ALU.add))
            link(nc.vector.tensor_scalar(dec_bi, dec_a, -1.0, None, ALU.add))
            link(nc.vector.tensor_scalar(dec_ci, dec_bi, 7, None, ALU.arith_shift_right))
            link(nc.vector.tensor_scalar(slot_src, dec_ci, 0.0, None, ALU.max))
            link(nc.vector.tensor_scalar(dec_d, dec_bi, 0.0, 1000.0, ALU.is_lt, ALU.mult))
            link(nc.vector.tensor_scalar(dec_ci, dec_bi, P - 1, None, ALU.bitwise_and))
            link(nc.vector.tensor_tensor(slot_tgt, dec_d, dec_ci, ALU.add))
            dve.wait_ge(node_sum, 1)
            for k, (a, z) in enumerate(SPLIT):
                link(nc.vector.tensor_scalar(slot_node[:, a:z], banks[6 + k][0:1, 0:z - a],
                                             float(NT - 1), None, ALU.min))
            dve.sem_inc(drained, 4)
            dve.sem_inc(slots_ready, 1)

            with dve.Fori(0, LAYERS) as l:
                dve.wait_ge(acc_zeroed, l * BODIES + BODIES)
                dve.wait_ge(h_kept, CREDIT + l * BODIES + BODIES)
                go(dve, g_evac, CREDIT + l * (BODIES * NPAIR) + BODIES * NPAIR)
                with dve.Fori(0, STEPS) as i:
                    n = l * STEPS + i
                    _, nodes = nc.values_load_multi_w_load_instructions(
                        slot_node[:, bass.ds(i * RING, RING)], engines=(mybir.EngineType.DVE,),
                        min_val=0, max_val=NT - 1,
                        skip_runtime_bounds_check_because="the table was cut to this range")
                    for a, z in HALVES:
                        dve.wait_ge(summed, n * RING + z)
                        nc.vector.tensor_tensor(
                            onehot3[:, a:z],
                            iota_f[:, :].unsqueeze(1).to_broadcast([P, z - a, P]),
                            slot_tgt[:, bass.ds(i * RING + a, z - a)].unsqueeze(2)
                            .to_broadcast([P, z - a, P]), ALU.is_equal).then_inc(onehot_ready, 1)
                    for b in range(RING):
                        dve.wait_ge(drained, n * RING + (b + 4))
                        dve.wait_ge(summed, n * RING + (b + 1 + RING))
                        row = bass.ds(nodes[b] * AW, AW)
                        nc.vector.tensor_tensor(acc[:, row], acc[:, row],
                                                banks[bank_of(b)][:, 0:AW], ALU.add)\
                            .then_inc(drained, 1)
                dve.wait_ge(drained, l * SLOTS + (SLOTS + 4))
                dve.wait_ge(self_evac, CREDIT + l * STEPS + STEPS)
                nc.vector.tensor_scalar(rdeg[:, :], acc3[:, :, C], 1.0, None, ALU.max)\
                    .then_inc(deg_step, 1)
                dve.wait_ge(deg_step, l * 2 + 1)
                nc.vector.reciprocal(rdeg[:, :], rdeg[:, :]).then_inc(deg_step, 1)
                go(dve, deg_step, l * 2 + 2)
                with dve.Fori(0, BODIES) as i:
                    n = l * BODIES + i + BODIES
                    dve.wait_ge(t_done, CREDIT + n * NPAIR)
                    for b in range(BODY):
                        nc.vector.scalar_tensor_tensor(
                            u3[:, b], acc[:, bass.ds(i * (BODY * AW) + b * AW, C)],
                            rdeg[:, bass.ds(i * BODY + b, 1)],
                            selfp[:, bass.ds(i * (BODY * C) + b * C, C)],
                            ALU.mult, ALU.add).then_inc(u_ready, 1)

            dve.wait_ge(ffn_weights, 16 * FFN_LOADS)
            with dve.Fori(0, BODIES) as i:
                here = x2_all[:, bass.ds(i * BODY, BODY), :]
                dve.wait_ge(x_reloaded, i * 16 + 16)
                dve.wait_ge(y_loaded, i * 16 + 16)
                nc.vector.tensor_tensor(here, x_in, y_in, ALU.add).then_inc(xy_used, 1)
                dve.wait_ge(xy_used, CREDIT + i + 1)
                nc.vector.tensor_tensor(here, here,
                                        bout_t.unsqueeze(1).to_broadcast([P, BODY, C]), ALU.add)\
                    .then_inc(x2_ready, 1)
            dve.wait_ge(x2_ready, BODIES)
            row_stats(lambda t: x2_all[:, t])
            link(row_scales(2))
            with dve.Fori(0, BODIES) as i:
                n = i + (LAYERS + 1) * BODIES
                dve.wait_ge(t_done, CREDIT + n * NPAIR)
                go(dve, f_free, CREDIT + i)
                for b in range(BODY):
                    nc.vector.tensor_scalar(f_ring[:, b], selfp[:, bass.ds(i * (BODY * C) + b * C, C)],
                                            rstd[:, bass.ds(i * BODY + b, 1)],
                                            nmr[:, bass.ds(i * BODY + b, 1)],
                                            ALU.mult, ALU.add).then_inc(u_ready, 1)
                dve.wait_ge(lg_done, CREDIT + i + 1)
                nc.vector.tensor_tensor(lg3[:, bass.ds(i * BODY, BODY), :],
                                        banks[7][:, 0:BODY * EXPERTS]
                                        .rearrange("p (t e) -> p t e", e=EXPERTS),
                                        rb2.unsqueeze(1).to_broadcast([P, BODY, EXPERTS]),
                                        ALU.add).then_inc(lg_evac, 1)

            wide = top3.to_broadcast([P, NT, EXPERTS])
            dve.wait_ge(lg_evac, CREDIT + BODIES)
            link(nc.vector.tensor_reduce(topv, lg3, AX.X, ALU.max))
            nc.vector.tensor_tensor(gt3, lg3, wide, ALU.subtract).then_inc(soft_in, 1)
            dve.wait_ge(soft_exp, 1)
            link(nc.vector.tensor_reduce(topv, gt3, AX.X, ALU.add))
            link(nc.vector.reciprocal(topv, topv))
            link(nc.vector.tensor_tensor(gt3, gt3, wide, ALU.mult))
            link(nc.vector.memset(rank, 0.0))
            for o in range(EXPERTS):
                if o > 0:
                    link(nc.vector.tensor_tensor(bt3[:, :, 0:o],
                                                 gt3[:, :, o:o + 1].to_broadcast([P, NT, o]),
                                                 gt3[:, :, 0:o], ALU.is_gt))
                    link(nc.vector.tensor_tensor(rk3[:, :, 0:o], rk3[:, :, 0:o], bt3[:, :, 0:o],
                                                 ALU.add))
                if o < EXPERTS - 1:
                    r = EXPERTS - 1 - o
                    link(nc.vector.tensor_tensor(bt3[:, :, o + 1:],
                                                 gt3[:, :, o:o + 1].to_broadcast([P, NT, r]),
                                                 gt3[:, :, o + 1:], ALU.is_ge))
                    link(nc.vector.tensor_tensor(rk3[:, :, o + 1:], rk3[:, :, o + 1:],
                                                 bt3[:, :, o + 1:], ALU.add))
            by_expert = rk3.rearrange("p t e -> p e t")
            for k in range(TOP_K):
                link(nc.vector.tensor_scalar(ch3[:, :, k * NT:(k + 1) * NT], by_expert, float(k), None,
                                             ALU.is_equal))
            nc.vector.tensor_reduce(ecnt, ch3, AX.X, ALU.add).then_inc(ecnt_ready, 1)
            link(nc.vector.tensor_scalar(rank, rank, float(TOP_K), None, ALU.is_lt))
            link(nc.vector.tensor_reduce(topv, gt3, AX.X, ALU.max))
            nc.vector.tensor_tensor(gt3, gt3, wide, ALU.subtract).then_inc(soft_in, 1)
            dve.wait_ge(soft_exp, 2)
            link(nc.vector.tensor_tensor(gates, gates, rank, ALU.mult))
            link(nc.vector.tensor_reduce(topv, gt3, AX.X, ALU.add))
            link(nc.vector.reciprocal(topv, topv))
            link(nc.vector.tensor_tensor(gt3, gt3, wide, ALU.mult))

            for k in range(TOP_K):
                picked = ch3[:, :, k * NT:(k + 1) * NT].rearrange("p e t -> p t e")
                link(nc.vector.tensor_tensor(bt3, gt3, picked, ALU.mult))
                link(nc.vector.tensor_reduce(gate[k], bt3, AX.X, ALU.add))

            dve.wait_ge(experts_counted, 1)
            link(nc.vector.tensor_scalar(run_i[0:EXPERTS, :], banks[0][0:EXPERTS, 0:1], float(P - 1),
                                         None, ALU.add))
            link(nc.vector.tensor_scalar(run_j[0:EXPERTS, :], run_i[0:EXPERTS, :], 7, None,
                                         ALU.arith_shift_right))
            link(nc.vector.tensor_copy(run_tiles[0:EXPERTS, :], run_j[0:EXPERTS, :]))
            nc.vector.tensor_scalar(e_wide, e_ones[0:EXPERTS, :], run_tiles[0:EXPERTS, 0:1], float(P),
                                    ALU.mult, ALU.mult).then_inc(e_sizes, 1)
            dve.wait_ge(ebase_sum, 1)
            link(nc.vector.tensor_copy(ebase, banks[1][:, 0:EXPERTS]))
            link(nc.vector.tensor_copy(run_end[0:EXPERTS, :], banks[2][0:EXPERTS, 0:1]))
            for e in range(EXPERTS):
                ins = nc.vector.tensor_tensor_scan(ra3[:, e], ch3[:, e], ch3[:, e], ebase[:, e:e + 1],
                                                   ALU.add, ALU.bypass)
            link(ins)
            link(nc.vector.tensor_tensor(ranked, ranked, chosen, ALU.mult))
            link(nc.vector.tensor_reduce(eslot_lo, ra3.rearrange("p e j -> p j e"), AX.X, ALU.add))
            link(nc.vector.tensor_scalar(eslot_i, eslot_lo, -1.0, None, ALU.add))
            link(nc.vector.tensor_scalar(etemp_i, eslot_i, 7, None, ALU.arith_shift_right))
            link(nc.vector.tensor_copy(eslot_hi, etemp_i))
            link(nc.vector.tensor_scalar(etemp_i, eslot_i, P - 1, None, ALU.bitwise_and))
            link(nc.vector.tensor_copy(eslot_lo, etemp_i))
            link(nc.vector.tensor_scalar(e_past, iota_f[0:EXPERTS, 0:ETILES],
                                         run_end[0:EXPERTS, 0:1], None, ALU.is_ge))
            with dve.Fori(0, ITEMS // EROW) as i:
                for b in range(EROW):
                    dve.wait_ge(item_used, i * EROW + (b + 1))
                    at = bass.ds(i * EROW + b, 1)
                    nc.vector.tensor_scalar(item_lo[b], iota_f[:, :], eslot_lo[:, at],
                                            item_no[:, at], ALU.is_equal, ALU.mult)
                    nc.vector.tensor_scalar(item_hi[b], iota_f[:, 0:ETILES], eslot_hi[:, at], None,
                                            ALU.is_equal).then_inc(item_ready, 1)
            dve.wait_ge(item_used, ITEMS + EROW + 1)
            link(nc.vector.tensor_scalar(item_i, banks[3][:, 0:ETILES], -1.0, None, ALU.add))
            link(nc.vector.tensor_scalar(etest_i, item_i, float(NT * P), float(-NT * P),
                                         ALU.is_ge, ALU.mult))
            link(nc.vector.tensor_tensor(node_i, item_i, etest_i, ALU.add))
            link(nc.vector.tensor_scalar(node_i, node_i, 0.0, None, ALU.max))
            link(nc.vector.tensor_scalar(etest_i, item_i, 0.0, None, ALU.is_lt))
            link(nc.vector.tensor_scalar(pad_i, pad_i, 1.0, None, ALU.add))
            link(nc.vector.tensor_tensor(pad_i, pad_i, etest_i, ALU.mult))
            link(nc.vector.tensor_tensor(item_i, item_i, pad_i, ALU.add))
            link(nc.vector.tensor_scalar(tile_expert, banks[4][0:1, 0:ETILES], float(EXPERTS - 1),
                                         None, ALU.min))
            dve.sem_inc(tables_ready, 1)

            def words_in(n, b, expert):
                after(dve, y_done, n - 3)
                after(dve, y_ready, n - 3)
                nc.vector.tensor_copy(wbuf[b % WBUFS], experts[:, bass.ds(expert * WEXP, WEXP)])\
                    .then_inc(words_ready, 1)

            def rows_in(n, b, step):
                after(dve, y_done, n + 1)
                dve.wait_ge(y_free[b // EHALF], CREDIT + step)
                nc.vector.tensor_tensor(y_out[b], banks[6 + b % 2][:, 0:C],
                                        wbuf[b % WBUFS][:, WEXP - C:WEXP], ALU.add)\
                    .then_inc(y_ready, 1)

            def load_experts(step):
                _, which = nc.values_load_multi_w_load_instructions(
                    tile_expert[:, bass.ds(step * UNROLL, UNROLL)],
                    engines=(mybir.EngineType.DVE,), min_val=0, max_val=EXPERTS - 1,
                    skip_runtime_bounds_check_because="the table was cut to this range")
                return which

            which = load_experts(0)
            for b in range(UNROLL):
                words_in(b, b, which[b])
                if b >= 3:
                    rows_in(b - 3, b - 3, 0)
            with dve.Fori(0, ESTEPS - 1) as i:
                which = load_experts(i + 1)
                for b in range(UNROLL):
                    words_in((i + 1) * UNROLL + b, b, which[b])
                    rows_in((i + 1) * UNROLL + b - 3, (b - 3) % UNROLL, i + 1 if b >= 3 else i)
            for b in range(3):
                rows_in(ETILES + b - 3, UNROLL + b - 3, ESTEPS - 1)

            for i in range(BODIES):
                dve.wait_ge(pairs_loaded[i % 2], 16 * TOP_K * (i // 2 + 1))
                for k in range(TOP_K):
                    for t in range(i * BODY, (i + 1) * BODY):
                        ins = nc.vector.scalar_tensor_tensor(
                            x2_all[:, t], pairs_in[:, i % 2, k, t - i * BODY], gate[k][:, t:t + 1],
                            x2_all[:, t], ALU.mult, ALU.add)
                    ins.then_inc(first_added if k == 0 else body_done, 1)
                    if k == 0:
                        dve.wait_ge(first_added, CREDIT + i + 1)


def kernel(x, src, dst, L0_gnn_W_in, L0_gnn_b_in, L0_gnn_W_agg, L0_gnn_W_self, L0_gnn_b_hid,
           L0_gnn_W_out, L0_gnn_b_out, L0_ffn_router_w1, L0_ffn_router_b1, L0_ffn_router_w2,
           L0_ffn_router_b2, L0_ffn_expert_w1, L0_ffn_expert_b1, L0_ffn_expert_w2,
           L0_ffn_expert_b2, L0_ffn_expert_w3, L0_ffn_expert_b3):
    import numpy as np
    import concourse.bacc as bacc
    from concourse.bass_utils import run_bass_kernel_spmd

    def padded(a, rows, fill):
        a = np.asarray(a)
        out = np.full((rows,) + a.shape[1:], fill, a.dtype)
        out[:a.shape[0]] = a
        return out

    arrays = {
        "in_x": padded(x, NT * P, 0),
        "in_tgt": padded(src, P * COLS, -1),
        "in_gat": padded(dst, P * COLS, 0),
    }
    for name, a in (("w_in", L0_gnn_W_in), ("b_in", L0_gnn_b_in), ("w_agg", L0_gnn_W_agg),
                    ("w_self", L0_gnn_W_self), ("b_hid", L0_gnn_b_hid), ("w_out", L0_gnn_W_out),
                    ("b_out", L0_gnn_b_out), ("r_w1", L0_ffn_router_w1),
                    ("r_b1", L0_ffn_router_b1), ("r_w2", L0_ffn_router_w2),
                    ("r_b2", L0_ffn_router_b2), ("e_w1", L0_ffn_expert_w1),
                    ("e_b1", L0_ffn_expert_b1), ("e_w2", L0_ffn_expert_w2),
                    ("e_b2", L0_ffn_expert_b2), ("e_w3", L0_ffn_expert_w3),
                    ("e_b3", L0_ffn_expert_b3)):
        arrays["in_" + name] = np.ascontiguousarray(np.asarray(a))

    nc = bacc.Bacc("TRN2", target_bir_lowering=False, num_devices=1)
    args = [nc.dram_tensor(n, a.shape, mybir.dt.from_np(a.dtype), kind="ExternalInput").ap()
            for n, a in arrays.items()]
    out = nc.dram_tensor("out_rows", (NT * P, C), F32, kind="ExternalOutput").ap()
    gnn_moe(nc, *args, out)
    r = run_bass_kernel_spmd(nc, [arrays], core_ids=[0])
    return r.results[0]["out_rows"][:NODES]
```

```python
from contextlib import ExitStack

import concourse.bass as bass
from concourse import mybir

ACT = mybir.ActivationFunctionType
ALU = mybir.AluOpType
AX = mybir.AxisListType
F32 = mybir.dt.float32
F16 = mybir.dt.float16
I32 = mybir.dt.int32

P = 128
NODES = 6250
EDGES = 100000
C = 256
KC = C // P
LAYERS = 3
EXPERTS = 6
TOP_K = 2
EPS = 1e-5

NT = -(-NODES // P)
BODY = 7
BODIES = NT // BODY
PAIRS = [(0, 2), (2, 4), (4, 6), (6, 7)]
NPAIR = len(PAIRS)

COLS = 784
SLOTS = EDGES // P + NT + 3
RING = 17
STEPS = SLOTS // RING
HALF = 9
HALVES = [(0, HALF), (HALF, RING)]
AW = C + 1
PERM = 8
PW = SLOTS + 1
CUT = 512
SORT_STEPS = 28
PE_COLS = 448
SC_COLS = COLS - PE_COLS
SC_RING = SC_COLS // SORT_STEPS
SC_HALF = SC_RING // 2
assert PE_COLS % PERM == 0 and SC_COLS == SORT_STEPS * 2 * SC_HALF
assert NT == BODIES * BODY == STEPS and SLOTS == STEPS * RING and COLS % PERM == 0

FH = BODY * P // 2

ITEMS = TOP_K * NT
UNROLL = 8
EHALF = UNROLL // 2
ETILES = -(-(ITEMS + EXPERTS - 1) // UNROLL) * UNROLL
ESTEPS = ETILES // UNROLL
ROWS = TOP_K * NT * P
EROW = 7
WEXP = 3 * KC * C + 2 * KC + C
PBUFS = 3
WBUFS = 4


def bank_of(b):
    return b % 4 if b < RING - 1 else 4


def cum_of(b):
    return b % 2 if b < BODY - 1 else 2


def mask_of(b):
    return b % 3 if b < BODY - 1 else 3


IN_BANK = [0, 1, 0, 1]
T_BANK = [0, 1, 2, 3]
M_BANK = [2, 3, 4, 2]
G_BANK = [5, 6, 7, 5]


def t_freed(n, q, t_bank=T_BANK):
    return n * NPAIR + (q - 1 if t_bank[q] in t_bank[:q] else 0)


def gnn_moe(nc, x, tgt, gat, w_in, b_in, w_agg, w_self, b_hid, w_out, b_out,
            r_w1, r_b1, r_w2, r_b2, e_w1, e_b1, e_w2, e_b2, e_w3, e_b3, out):
    g_dram = nc.dram_tensor("g_rows", [NT * P, C], F32, kind="Internal").ap()
    g_tiles = g_dram.rearrange("(t p) c -> p t c", p=P)
    rec_dram = nc.dram_tensor("records", [P * SLOTS + P * COLS, 1], I32, kind="Internal").ap()
    f_dram = nc.dram_tensor("features", [NT * P, C], F32, kind="Internal").ap()
    f_tiles = f_dram.rearrange("(t p) c -> p t c", p=P)
    y_dram = nc.dram_tensor("expert_rows", [ROWS + ETILES * P, C], F32, kind="Internal").ap()
    y_tiles = y_dram[0:ROWS, :].rearrange("(k t p) c -> p k t c", k=TOP_K, p=P)
    x_tiles = x.rearrange("(t p) c -> p t c", p=P)
    out_tiles = out.rearrange("(t p) c -> p t c", p=P)

    with ExitStack() as ctx:
        def sb(name, shape, dt=F32):
            return ctx.enter_context(nc.sbuf_tensor(name, shape, dt))

        def sem(name):
            return ctx.enter_context(nc.semaphore(name))

        banks = [ctx.enter_context(nc.psum_tensor(f"bank{k}", [P, CUT], F32)) for k in range(8)]

        acc = sb("acc", [P, NT * AW])
        selfp = sb("selfp", [P, NT * C])
        hT_all = sb("hT_all", [P, NT * C])
        gath = sb("gath", [P, RING * AW])
        onehot = sb("onehot", [P, RING * P])
        misc = sb("misc", [P, BODY * C])
        tables = sb("tables", [P, 2 * SLOTS])
        idx_ring = sb("idx_ring", [P, RING], I32)
        wg = sb("wg", [P, (LAYERS + 1) * KC * C])
        ws = sb("ws", [P, LAYERS * KC * C])
        win = sb("win", [P, KC * C])
        bias_in = sb("bias_in", [P, KC])
        bias_hid = sb("bias_hid", [P, LAYERS * KC])
        bias_now = sb("bias_now", [P, KC])
        ident = sb("ident", [P, P])
        iota_f = sb("iota_f", [P, P])
        zeros = sb("zeros", [P, 1])
        eps_t = sb("eps_t", [P, 1])
        rdeg = sb("rdeg", [P, NT])
        mv = sb("mv", [P, NT * 2])
        rstd = sb("rstd", [P, NT])
        nmr = sb("nmr", [P, NT])
        cnt = sb("cnt", [P, NT])
        base = sb("base", [P, NT])
        run_i = sb("run_i", [NT, 1], I32)
        run_j = sb("run_j", [NT, 1], I32)
        run_tiles = sb("run_tiles", [NT, 1])
        run_end = sb("run_end", [NT, 1])

        acc3 = acc[:, :].rearrange("p (t c) -> p t c", c=AW)
        gath3 = gath[:, :].rearrange("p (t c) -> p t c", c=AW)
        onehot3 = onehot[:, :].rearrange("p (t c) -> p t c", c=P)
        u_ring = gath[:, 0:BODY * C]
        g_ring = gath[:, BODY * C:2 * BODY * C]
        hT_ring = onehot[:, 0:BODY * C]
        u3 = u_ring.rearrange("p (t c) -> p t c", c=C)
        g3 = g_ring.rearrange("p (t c) -> p t c", c=C)
        hr4 = hT_ring.rearrange("p (t k c) -> p t k c", k=KC, c=P)
        hT_self = misc[:, 4 * C:5 * C]
        hs3 = hT_self.rearrange("p (k c) -> p k c", k=KC)
        win3 = win[:, :].rearrange("p (k c) -> p k c", k=KC)
        mv3 = mv[:, :].rearrange("p (t c) -> p t c", c=2)
        slot_src = tables[:, 0:SLOTS].bitcast(I32)
        slot_tgt = tables[:, SLOTS:2 * SLOTS]
        slot_node = misc[0:1, 0:SLOTS].bitcast(I32)

        stats = misc[:, BODY * C - NT * 6:BODY * C]

        xT_ring = misc[:, :]
        xr4 = xT_ring.rearrange("p (t k c) -> p t k c", k=KC, c=P)
        scratch = [selfp[:, r * COLS:(r + 1) * COLS] for r in range(11)]
        edge_t, edge_s, tile_i, temp_i = (scratch[r].bitcast(I32) for r in range(4))
        tile_h = scratch[4].bitcast(F16)[:, 0:COLS]
        cums = scratch[5:8]
        pos_sum = scratch[10]
        masks = [scratch[8 + r // 2].bitcast(F16)[:, (r % 2) * COLS:(r % 2 + 1) * COLS]
                 for r in range(4)]
        part_a = tables[:, 0:COLS]
        part_b = tables[:, COLS:2 * COLS]
        pos_hi = misc[:, 0:COLS]
        pos_lo = misc[:, COLS:2 * COLS]
        iota_h = gath[:, 2 * BODY * C:2 * BODY * C + PW // 2].bitcast(F16)
        run_wide = gath[0:NT, 2 * BODY * C + PW // 2:2 * BODY * C + PW // 2 + P]
        lower = onehot[:, BODY * C:BODY * C + P]
        lower_eq = onehot[:, BODY * C + P:BODY * C + P + NT]
        ones = onehot[:, BODY * C + P + NT:BODY * C + 2 * P + NT]
        RW = PW // 2
        p_hi = selfp[:, 0:PERM * RW].bitcast(F16).rearrange("p (r c) -> p r c", c=PW)
        p_lo = selfp[:, PERM * RW:PERM * RW + PERM * P].bitcast(F16)\
            .rearrange("p (r a c) -> p r a c", a=2, c=P)
        DEC0 = PERM * (RW + P)
        past, dec_a, dec_b, dec_c, dec_e = (
            selfp[:, DEC0 + r * SLOTS:DEC0 + (r + 1) * SLOTS] for r in range(5))
        dec_d = dec_a
        dec_bi, dec_ci, scattered_recs = (v.bitcast(I32) for v in (dec_b, dec_c, dec_e))
        AFTER = 11 * COLS
        sc_slot, sc_rec, sc_temp, sc_pad = (
            selfp[:, AFTER + r * SC_COLS:AFTER + (r + 1) * SC_COLS].bitcast(I32) for r in range(4))
        sc_ring = selfp[:, AFTER + 4 * SC_COLS:AFTER + 4 * SC_COLS + 2 * SC_RING].bitcast(I32)
        clear = selfp[:, NT * C - SLOTS:NT * C].bitcast(I32)
        assert AFTER + 4 * SC_COLS + 2 * SC_RING <= NT * C - SLOTS
        slot_ring, rec_ring = sc_ring[:, 0:SC_RING], sc_ring[:, SC_RING:2 * SC_RING]

        x2_all = selfp[:, :].rearrange("p (t c) -> p t c", c=C)
        experts = hT_all[:, 0:EXPERTS * WEXP]
        ex3 = experts.rearrange("p (e c) -> p e c", e=EXPERTS)
        f_rings = (g3, u3)
        x_in = misc
        e_stats = tables[:, 0:NT * 6]
        rhT = acc[:, BODY * C:BODY * C + BODY * P]
        f_in = [gath[:, b * C:(b + 1) * C] for b in range(UNROLL)]
        y_out = [gath[:, (UNROLL + b) * C:(UNROLL + b + 1) * C] for b in range(UNROLL)]

        taken = [0]

        def room(words, parts=P):
            a = taken[0]
            taken[0] += words
            assert taken[0] <= NT * AW
            return acc[0:parts, a:a + words]

        fT_ring = acc[:, 0:BODY * C]
        wbuf = [room(WEXP) for _ in range(WBUFS)]
        fT, h1T, h2T = ([room(KC * P) for _ in range(2)] for _ in range(3))
        item_lo, item_hi = ([acc[:, (2 * w + r) * EROW * P:(2 * w + r) * EROW * P + EROW * width]
                             .rearrange("p (b c) -> p b c", b=EROW) for r in range(2)]
                            for w, width in enumerate((P, ETILES)))
        chosen, ranked = (room(EXPERTS * ITEMS) for _ in range(2))
        ch3, ra3 = (v.rearrange("p (e j) -> p e j", e=EXPERTS) for v in (chosen, ranked))
        item_no, eslot_lo, eslot_hi = (room(ITEMS) for _ in range(3))
        eslot_i, etemp_i = (room(ITEMS).bitcast(I32) for _ in range(2))
        gate = [room(NT) for _ in range(TOP_K)]
        item_i, node_i, pad_i, etest_i = (room(ETILES).bitcast(I32) for _ in range(4))
        pairs_in = hT_all[:, 0:PBUFS * TOP_K * BODY * C]\
            .rearrange("p (b k t c) -> p b k t c", b=PBUFS, k=TOP_K, c=C)
        small = hT_all[:, EXPERTS * WEXP:]
        bout_t = small[:, 0:C]
        rw1 = small[:, C:C + KC * P].rearrange("p (k c) -> p k c", k=KC)
        rw2 = small[:, 2 * C:2 * C + EXPERTS]
        rb2 = small[:, 2 * C + EXPERTS:2 * C + 2 * EXPERTS]
        rb1 = small[:, 2 * C + 2 * EXPERTS:2 * C + 2 * EXPERTS + 1]
        e_lower = onehot[:, 3 * C:3 * C + P]
        e_ones = onehot[:, 3 * C + P:3 * C + 2 * P]
        e_at = 3 * C + 2 * P
        e_lower_eq, ecnt, ebase = (onehot[:, e_at + r * EXPERTS:e_at + (r + 1) * EXPERTS]
                                   for r in range(3))
        e_at += 3 * EXPERTS
        node_ring, item_ring = (onehot[:, e_at + r * UNROLL:e_at + (r + 1) * UNROLL].bitcast(I32)
                                for r in range(2))
        e_at += 2 * UNROLL
        e_past = onehot[0:EXPERTS, e_at:e_at + ETILES]
        tile_expert = onehot[0:1, e_at + ETILES:e_at + 2 * ETILES].bitcast(I32)
        e_wide = onehot[0:EXPERTS, e_at + 2 * ETILES:e_at + 2 * ETILES + P]
        NE = NT * EXPERTS
        logits, gates, rank, beat = (misc[:, r * NE:(r + 1) * NE] for r in range(4))
        topv = misc[:, 4 * NE:4 * NE + NT]
        lg3, gt3, rk3, bt3 = (v.rearrange("p (t e) -> p t e", e=EXPERTS)
                              for v in (logits, gates, rank, beat))
        top3 = topv.unsqueeze(2)

        weights_in = sem("weights_in")
        edges_in = sem("edges_in")
        x_loaded = sem("x_loaded")
        consts = sem("consts")
        dve_step = sem("dve_step")
        var_ready = sem("var_ready")
        std_ready = sem("std_ready")
        stats_ready = sem("stats_ready")
        cnt_ready = sem("cnt_ready")
        runs_counted = sem("runs_counted")
        run_sizes = sem("run_sizes")
        base_sum = sem("base_sum")
        mask_ready = sem("mask_ready")
        cum_ready = sem("cum_ready")
        msk_ready = sem("msk_ready")
        pos_added = sem("pos_added")
        p_ready = sem("p_ready")
        table_cleared = sem("table_cleared")
        sc_base = sem("sc_base")
        sc_tables = sem("sc_tables")
        sc_filled = sem("sc_filled")
        scattered = [sem(f"scattered{h}") for h in range(2)]
        table_in = sem("table_in")
        p_used = sem("p_used")
        past_ready = sem("past_ready")
        node_sum = sem("node_sum")
        slots_ready = sem("slots_ready")
        u_ready = sem("u_ready")
        t_done = sem("t_done")
        t_evac = sem("t_evac")
        m_done = sem("m_done")
        m_evac = sem("m_evac")
        g_done = sem("g_done")
        g_evac = sem("g_evac")
        g_stored = sem("g_stored")
        g_free = sem("g_free")
        h_kept = sem("h_kept")
        acc_zeroed = sem("acc_zeroed")
        ones_ready = sem("ones_ready")
        idx_ready = sem("idx_ready")
        gathered = [sem(f"gathered{b}") for b in range(RING)]
        ticks = {eng: sem(f"ticks_{name}")
                 for name, eng in (("act", nc.scalar), ("dve", nc.vector), ("pool", nc.gpsimd))}
        onehot_ready = sem("onehot_ready")
        summed = sem("summed")
        drained = sem("drained")
        selfT_ready = sem("selfT_ready")
        self_done = sem("self_done")
        self_evac = sem("self_evac")
        bias_ready = sem("bias_ready")
        deg_step = sem("deg_step")
        ffn_weights = sem("ffn_weights")
        x_reloaded = sem("x_reloaded")
        bout_in = sem("bout_in")
        x_used = sem("x_used")
        x2_ready = sem("x2_ready")
        rh_done = sem("rh_done")
        rh_ready = sem("rh_ready")
        lg_done = sem("lg_done")
        lg_evac = sem("lg_evac")
        soft_in = sem("soft_in")
        soft_exp = sem("soft_exp")
        f_stored = sem("f_stored")
        f_free = sem("f_free")
        e_consts = sem("e_consts")
        ecnt_ready = sem("ecnt_ready")
        experts_counted = sem("experts_counted")
        e_sizes = sem("e_sizes")
        ebase_sum = sem("ebase_sum")
        item_ready = sem("item_ready")
        item_valued = sem("item_valued")
        item_used = sem("item_used")
        tables_ready = sem("tables_ready")
        rows_copied = sem("rows_copied")
        items_copied = sem("items_copied")
        fx_done = sem("fx_done")
        fx_ready = sem("fx_ready")
        words_ready = sem("words_ready")
        h1_done = sem("h1_done")
        h1_ready = sem("h1_ready")
        h2_done = sem("h2_done")
        h2_ready = sem("h2_ready")
        y_done = sem("y_done")
        y_ready = sem("y_ready")
        y_scattered = [sem(f"y_scattered{h}") for h in range(2)]
        y_free = [sem(f"y_free{h}") for h in range(2)]
        pairs_loaded = [sem(f"pairs_loaded{b}") for b in range(PBUFS)]
        first_added = sem("first_added")
        body_done = sem("body_done")
        out_stored = sem("out_stored")

        CREDIT = 1
        credited = (pos_added, f_free, y_free[0], y_free[1], x_used, t_done, t_evac, h_kept,
                    g_free, self_done, lg_done, g_evac,
                    m_evac, self_evac, rh_ready, lg_evac, first_added, body_done)

        N_CONSTS = 10
        FFN_LOADS = 5 * EXPERTS + 1 + 4
        SPLIT = ((0, CUT), (CUT, SLOTS))
        block = ctx.enter_context(nc.Block())

        def go(eng, semaphore, value):
            eng.wait_ge(semaphore, value)
            eng.sem_inc(ticks[eng], 1)

        def after(eng, semaphore, value):
            if not isinstance(value, int) or value > 0:
                eng.wait_ge(semaphore, value)

        @block.sync
        def _(sp):
            sp.dma_start(edge_t, tgt.rearrange("(p c) -> p c", p=P)).then_inc(edges_in, 16)
            sp.dma_start(edge_s, gat.rearrange("(p c) -> p c", p=P)).then_inc(edges_in, 16)
            for i in range(BODIES):
                sp.dma_start(acc3[:, i * BODY:(i + 1) * BODY, 0:C],
                             x_tiles[:, i * BODY:(i + 1) * BODY, :]).then_inc(x_loaded, 16)
            sp.dma_start(win3, w_in.rearrange("(k p) c -> p k c", p=P)).then_inc(weights_in, 16)
            wg4 = wg[:, :].rearrange("p (l k c) -> p l k c", k=KC, c=C)
            ws4 = ws[:, :].rearrange("p (l k c) -> p l k c", k=KC, c=C)
            for l in range(LAYERS):
                sp.dma_start(wg4[:, l], w_agg[l].rearrange("(k p) c -> p k c", p=P))\
                    .then_inc(weights_in, 16)
                sp.dma_start(ws4[:, l], w_self[l].rearrange("(k p) c -> p k c", p=P))\
                    .then_inc(weights_in, 16)
            sp.dma_start(wg4[:, LAYERS], w_out.rearrange("(k p) c -> p k c", p=P))\
                .then_inc(weights_in, 16)
            with nc.allow_non_contiguous_dma(reason="biases, one per partition"):
                sp.dma_start(bias_in[:, :], b_in.rearrange("(k p) -> p k", p=P))\
                    .then_inc(weights_in, 16)
                sp.dma_start(bias_hid[:, :], b_hid.rearrange("l (k p) -> p (l k)", p=P))\
                    .then_inc(weights_in, 16)

            def store_g(i, n):
                sp.wait_ge(g_evac, CREDIT + NPAIR * n + NPAIR)
                sp.dma_start(g_tiles[:, bass.ds(i * BODY, BODY), :], g3).then_inc(g_stored, 16)
                sp.wait_ge(g_stored, n * 16 + 16)
                sp.sem_inc(g_free, 1)

            sp.wait_ge(consts, 7)
            by_slot = rec_dram[0:P * SLOTS, :].rearrange("(p c) a -> p (c a)", p=P)
            sp.dma_start(by_slot, clear).then_inc(table_cleared, 16)
            with sp.Fori(0, BODIES) as i:
                store_g(i, i)
            for h in range(2):
                sp.wait_ge(scattered[h], 16 * SC_HALF * SORT_STEPS)
            sp.wait_ge(sc_filled, 2 * SORT_STEPS)
            sp.dma_start(scattered_recs, by_slot).then_inc(table_in, 16)
            with sp.Fori(0, LAYERS - 1) as l:
                with sp.Fori(0, BODIES) as i:
                    store_g(i, l * BODIES + i + BODIES)

            def load_x(i):
                sp.dma_start(x_in[:, :].rearrange("p (t c) -> p t c", c=C),
                             x_tiles[:, bass.ds(i * BODY, BODY), :]).then_inc(x_reloaded, 16)

            sp.wait_ge(self_done, CREDIT + LAYERS * STEPS)
            sp.wait_ge(drained, LAYERS * SLOTS + 4)
            load_x(0)
            sp.dma_start(bout_t, b_out.unsqueeze(0).to_broadcast([P, C])).then_inc(bout_in, 16)
            for w, src in enumerate((e_w1, e_w2, e_w3)):
                for e in range(EXPERTS):
                    sp.dma_start(ex3[:, e, w * KC * C:(w + 1) * KC * C]
                                 .rearrange("p (k c) -> p k c", k=KC),
                                 src[e].rearrange("(k p) c -> p k c", p=P)).then_inc(ffn_weights, 16)
            with nc.allow_non_contiguous_dma(reason="biases, one per partition"):
                for w, b in enumerate((e_b1, e_b2)):
                    at = 3 * KC * C + w * KC
                    for e in range(EXPERTS):
                        sp.dma_start(ex3[:, e, at:at + KC], b[e].rearrange("(k p) -> p k", p=P))\
                            .then_inc(ffn_weights, 16)
            sp.dma_start(ex3[:, :, WEXP - C:WEXP], e_b3.unsqueeze(0).to_broadcast([P, EXPERTS, C]))\
                .then_inc(ffn_weights, 16)
            sp.dma_start(rw1, r_w1.rearrange("(k p) c -> p k c", p=P)).then_inc(ffn_weights, 16)
            with nc.allow_non_contiguous_dma(reason="a bias, one per partition"):
                sp.dma_start(rb1, r_b1.rearrange("(p a) -> p a", a=1)).then_inc(ffn_weights, 16)
            sp.dma_start(rw2, r_w2).then_inc(ffn_weights, 16)
            sp.dma_start(rb2, r_b2.unsqueeze(0).to_broadcast([P, EXPERTS])).then_inc(ffn_weights, 16)
            with sp.Fori(0, BODIES - 1) as i:
                sp.wait_ge(x_used, CREDIT + i + 1)
                load_x(i + 1)

            def store_features(i, ring):
                sp.wait_ge(u_ready, (i + (LAYERS + 1) * BODIES) * BODY + BODY)
                sp.dma_start(f_tiles[:, bass.ds(i * BODY, BODY), :], ring).then_inc(f_stored, 16)
                sp.wait_ge(f_stored, i * 16 + 16)
                sp.sem_inc(f_free, 1)

            store_features(0, f_rings[0])
            with sp.Fori(0, BODIES // 2) as j:
                for r in range(2):
                    store_features(j * 2 + r + 1, f_rings[1 - r])

            with sp.Fori(0, ESTEPS) as i:
                for h in range(2):
                    sp.wait_ge(y_scattered[h], i * (16 * EHALF) + 16 * EHALF)
                    sp.sem_inc(y_free[h], 1)

            def load_pairs(i, b):
                for k in range(TOP_K):
                    sp.dma_start(pairs_in[:, b, k], y_tiles[:, k, i * BODY:(i + 1) * BODY, :])\
                        .then_inc(pairs_loaded[b], 16)

            sp.wait_ge(y_ready, ETILES)
            for i in range(BODIES):
                if i >= PBUFS:
                    sp.wait_ge(body_done, CREDIT + i - PBUFS + 1)
                load_pairs(i, i % PBUFS)
            sp.wait_ge(out_stored, 16 * BODIES)

        @block.gpsimd
        def _(pool):
            pool.iota(iota_f[:, :], [[1, P]], base=0, channel_multiplier=0,
                      allow_small_or_imprecise_dtypes=True).then_inc(consts, 1)
            pool.iota(iota_h, [[1, PW]], base=0, channel_multiplier=0,
                      allow_small_or_imprecise_dtypes=True).then_inc(consts, 1)
            pool.memset(zeros[:, :], 0.0).then_inc(consts, 1)
            pool.memset(eps_t[:, :], EPS).then_inc(consts, 1)
            pool.memset(ones, 1.0).then_inc(consts, 1)
            pool.memset(ident[:, :], 0.0).then_inc(consts, 1)
            pool.memset(clear, 0).then_inc(consts, 1)
            pool.wait_ge(consts, 7)
            pool.affine_select(out=ident[:, :], in_=ident[:, :], compare_op=ALU.not_equal, fill=1.0,
                               base=0, pattern=[[-1, P]], channel_multiplier=1).then_inc(consts, 1)
            pool.affine_select(out=lower, in_=ones, compare_op=ALU.is_gt, fill=0.0,
                               base=0, pattern=[[1, P]], channel_multiplier=-1).then_inc(consts, 1)
            pool.affine_select(out=lower_eq, in_=ones[:, 0:NT], compare_op=ALU.is_ge, fill=0.0,
                               base=0, pattern=[[1, NT]], channel_multiplier=-1).then_inc(consts, 1)

            def zero_sums(i, n):
                pool.wait_ge(u_ready, n * BODY + BODY)
                pool.tensor_copy(acc[:, bass.ds(i * (BODY * AW), BODY * AW)],
                                 zeros[:, 0:1].to_broadcast([P, BODY * AW])).then_inc(acc_zeroed, 1)

            with pool.Fori(0, BODIES) as i:
                for b in range(BODY):
                    pool.wait_ge(cum_ready, i * BODY + b + 1)
                    cum = cums[cum_of(b)]
                    pool.tensor_tensor(cum, cum, masks[mask_of(b)], ALU.mult).then_inc(msk_ready, 1)

            pool.iota(sc_pad, [[1, SC_COLS]], base=P * SLOTS + PE_COLS, channel_multiplier=COLS)\
                .then_inc(sc_base, 1)
            pool.wait_ge(table_cleared, 16)
            with pool.Fori(0, SORT_STEPS) as i:
                for b in range(SC_RING):
                    h = b // SC_HALF
                    if b % SC_HALF == 0:
                        go(pool, sc_filled, i * 2 + (h + 1))
                    pool.indirect_dma_start(
                        rec_dram, bass.IndirectOffsetOnAxis(ap=slot_ring[:, b:b + 1], axis=0),
                        rec_ring[:, b:b + 1], None).then_inc(scattered[h], 16)

            pool.wait_ge(slots_ready, 1)
            def gather_layer(l):
                go(pool, g_stored, l * (16 * BODIES) + 16 * BODIES)
                pool.memset(gath3[:, :, C:AW], 1.0).then_inc(ones_ready, 1)
                go(pool, ones_ready, l + 1)
                with pool.Fori(0, STEPS) as i:
                    n = l * STEPS + i
                    for b in range(RING):
                        if b == 0:
                            pool.wait_ge(idx_ready, n * 2 + 1)
                        if b == HALF:
                            pool.wait_ge(idx_ready, n * 2 + 2)
                        go(pool, summed, n * RING + (b + 1))
                        pool.indirect_dma_start(
                            gath3[:, b, 0:C], None, g_dram,
                            bass.IndirectOffsetOnAxis(ap=idx_ring[:, b:b + 1], axis=0))\
                            .then_inc(gathered[b], 16)

            def finish_layer(l):
                with pool.Fori(0, BODIES) as i:
                    zero_sums(i, l * BODIES + i + BODIES)

            with pool.Fori(0, LAYERS - 1) as l:
                gather_layer(l)
                finish_layer(l)
            gather_layer(LAYERS - 1)

            pool.wait_ge(g_evac, CREDIT + NPAIR * BODIES * (LAYERS + 1))
            pool.memset(e_ones, 1.0).then_inc(e_consts, 1)
            pool.iota(item_no, [[P, ITEMS]], base=1, channel_multiplier=1,
                      allow_small_or_imprecise_dtypes=True).then_inc(e_consts, 1)
            pool.iota(pad_i, [[P, ETILES]], base=ROWS, channel_multiplier=1).then_inc(e_consts, 1)
            pool.wait_ge(e_consts, 3)
            pool.affine_select(out=e_lower, in_=e_ones, compare_op=ALU.is_gt, fill=0.0,
                               base=0, pattern=[[1, P]], channel_multiplier=-1).then_inc(e_consts, 1)
            pool.affine_select(out=e_lower_eq, in_=e_ones[:, 0:EXPERTS], compare_op=ALU.is_ge,
                               fill=0.0, base=0, pattern=[[1, EXPERTS]],
                               channel_multiplier=-1).then_inc(e_consts, 1)

            with pool.Fori(0, ITEMS // EROW // 2) as i:
                for r in range(2):
                    pool.wait_ge(item_ready, (i * 2 + r) * 2 + 1)
                    pool.tensor_tensor(item_hi[r], item_hi[r],
                                       item_no[:, bass.ds((i * 2 + r) * EROW, EROW)].unsqueeze(2)
                                       .to_broadcast([P, EROW, ETILES]), ALU.mult)\
                        .then_inc(item_valued, 1)

            def gather_tile(b):
                pool.indirect_dma_start(
                    f_in[b], None, f_dram,
                    bass.IndirectOffsetOnAxis(ap=node_ring[:, b:b + 1], axis=0))\
                    .then_inc(gathered[b], 16)

            def copy_rows(i):
                for b in range(UNROLL):
                    go(pool, gathered[b], (i + LAYERS * STEPS) * 16)
                pool.tensor_copy(node_ring, node_i[:, bass.ds(i * UNROLL, UNROLL)])\
                    .then_inc(rows_copied, 1)
                go(pool, rows_copied, i + 1)

            def copy_items(i):
                if not isinstance(i, int):
                    for h in range(2):
                        go(pool, y_scattered[h], i * (16 * EHALF))
                pool.tensor_copy(item_ring, item_i[:, bass.ds(i * UNROLL, UNROLL)])\
                    .then_inc(items_copied, 1)
                go(pool, items_copied, i + 1)

            def scatter_tile(i, b):
                go(pool, y_ready, i * UNROLL + (b + 1))
                pool.indirect_dma_start(
                    y_dram, bass.IndirectOffsetOnAxis(ap=item_ring[:, b:b + 1], axis=0),
                    y_out[b], None).then_inc(y_scattered[b // EHALF], 16)

            def expert_step(i):
                copy_rows(i + 1)
                copy_items(i)
                for b in range(UNROLL):
                    go(pool, fx_done, i * UNROLL + (b + 1))
                    gather_tile(b)
                    scatter_tile(i, b)

            pool.wait_ge(f_stored, 16 * BODIES)
            pool.wait_ge(tables_ready, 1)
            copy_rows(0)
            for b in range(UNROLL):
                gather_tile(b)
            expert_step(0)
            with pool.Fori(0, ESTEPS - 2) as i:
                expert_step(i + 1)
            pool.wait_ge(items_copied, ESTEPS - 1)
            for h in range(2):
                pool.wait_ge(y_scattered[h], (ESTEPS - 1) * (16 * EHALF))
            pool.tensor_copy(item_ring, item_i[:, ETILES - UNROLL:]).then_inc(items_copied, 1)
            pool.wait_ge(items_copied, ESTEPS)
            for b in range(UNROLL):
                scatter_tile(ESTEPS - 1, b)

        @block.scalar
        def _(act):
            act.wait_ge(consts, N_CONSTS)
            act.wait_ge(var_ready, 1)
            act.activation(rstd[:, :], mv3[:, :, 1], ACT.Sqrt, bias=eps_t[:, 0:1])\
                .then_inc(std_ready, 1)
            act.wait_ge(weights_in, 16 * (2 + 2 * LAYERS + 2))

            def evac_g(n):
                act.wait_ge(g_free, CREDIT + n)
                for q, (a, z) in enumerate(PAIRS):
                    act.wait_ge(g_done, NPAIR * n + (q + 1))
                    act.copy(g_ring[:, a * C:z * C], banks[G_BANK[q]][:, 0:(z - a) * C])\
                        .then_inc(g_evac, 1)

            def keep_h(i, n, ready):
                go(act, ready, CREDIT + NPAIR * n + NPAIR)
                act.copy(hT_all[:, bass.ds(i * (BODY * C), BODY * C)], hT_ring).then_inc(h_kept, 1)

            def by_tile(bank, n):
                return bank[:, 0:n * C].rearrange("p (t k c) -> p t k c", k=KC, c=P)

            act.wait_ge(stats_ready, 1)
            def normal_rows(i):
                for b in range(BODY):
                    act.activation(u3[:, b], acc[:, bass.ds(i * (BODY * AW) + b * AW, C)],
                                   ACT.Identity, bias=nmr[:, bass.ds(i * BODY + b, 1)],
                                   scale=rstd[:, bass.ds(i * BODY + b, 1)]).then_inc(u_ready, 1)

            def input_layer(i):
                for q, (a, z) in enumerate(PAIRS):
                    act.wait_ge(t_done, CREDIT + i * NPAIR + (q + 1))
                    act.copy(xT_ring[:, a * C:z * C], banks[IN_BANK[q]][:, 0:(z - a) * C])\
                        .then_inc(t_evac, 1)
                act.wait_ge(h_kept, CREDIT + i)
                for q, (a, z) in enumerate(PAIRS):
                    act.wait_ge(m_done, i * NPAIR + (q + 1))
                    for k in range(KC):
                        ins = act.activation(hr4[:, a:z, k], by_tile(banks[M_BANK[q]], z - a)[:, :, k],
                                             ACT.Identity, bias=bias_in[:, k:k + 1])
                    ins.then_inc(m_evac, 1)
                keep_h(i, i, m_evac)

            normal_rows(0)
            with act.Fori(0, BODIES - 1) as i:
                input_layer(i)
                normal_rows(i + 1)
                evac_g(i)
            input_layer(BODIES - 1)
            evac_g(BODIES - 1)

            act.copy(acc[:, :], zeros[:, 0:1].to_broadcast([P, NT * AW])).then_inc(acc_zeroed, BODIES)

            def fill_half(h, step):
                ring = slice(h * SC_HALF, (h + 1) * SC_HALF)
                at = bass.ds(step * SC_RING + h * SC_HALF, SC_HALF)
                act.copy(slot_ring[:, ring], sc_slot[:, at])
                act.copy(rec_ring[:, ring], sc_rec[:, at]).then_inc(sc_filled, 1)

            act.wait_ge(sc_tables, 1)
            for h in range(2):
                fill_half(h, 0)
            with act.Fori(0, SORT_STEPS - 1) as i:
                for h in range(2):
                    go(act, scattered[h], (i + 1) * (16 * SC_HALF))
                    fill_half(h, i + 1)

            act.wait_ge(slots_ready, 1)
            def gather_layer(l):
                act.wait_ge(h_kept, CREDIT + l * BODIES + BODIES)
                with act.Fori(0, STEPS) as i:
                    n = l * STEPS + i
                    act.wait_ge(summed, n * RING + HALF)
                    act.copy(idx_ring[:, 0:HALF], slot_src[:, bass.ds(i * RING, HALF)])\
                        .then_inc(idx_ready, 1)
                    act.wait_ge(self_done, CREDIT + n)
                    act.copy(hT_self, hT_all[:, bass.ds(i * C, C)]).then_inc(selfT_ready, 1)
                    act.wait_ge(summed, n * RING + RING)
                    act.copy(idx_ring[:, HALF:RING],
                             slot_src[:, bass.ds(i * RING + HALF, RING - HALF)])\
                        .then_inc(idx_ready, 1)
                    act.wait_ge(self_done, CREDIT + n + 1)
                    act.copy(selfp[:, bass.ds(i * C, C)], banks[5][:, 0:C]).then_inc(self_evac, 1)

            def layer_bias(l):
                act.copy(bias_now[:, :], bias_hid[:, bass.ds(l * KC, KC)]).then_inc(bias_ready, 1)
                go(act, bias_ready, l + 1)

            def relu_out(n):
                for q, (a, z) in enumerate(PAIRS):
                    act.wait_ge(t_done, CREDIT + n * NPAIR + (q + 1))
                    for k in range(KC):
                        ins = act.activation(hr4[:, a:z, k],
                                             by_tile(banks[T_BANK[q]], z - a)[:, :, k],
                                             ACT.Relu, bias=bias_now[:, k:k + 1])
                    ins.then_inc(t_evac, 1)

            def finish_layer(l):
                layer_bias(l)
                with act.Fori(0, BODIES) as i:
                    n = l * BODIES + i + BODIES
                    act.wait_ge(h_kept, CREDIT + n)
                    relu_out(n)
                    keep_h(i, n, t_evac)

            with act.Fori(0, LAYERS - 1) as l:
                gather_layer(l)
                finish_layer(l)
            gather_layer(LAYERS - 1)
            act.wait_ge(h_kept, CREDIT + LAYERS * BODIES)
            layer_bias(LAYERS - 1)
            with act.Fori(0, BODIES) as i:
                relu_out(i + LAYERS * BODIES)

            act.wait_ge(var_ready, 2)
            act.activation(rstd[:, :], mv3[:, :, 1], ACT.Sqrt, bias=eps_t[:, 0:1])\
                .then_inc(std_ready, 1)
            act.wait_ge(ffn_weights, 16 * FFN_LOADS)
            fT3 = fT_ring.rearrange("p (k n) -> p k n", k=KC)
            def features_in(i):
                n = i + (LAYERS + 1) * BODIES
                for q, (a, z) in enumerate(PAIRS):
                    act.wait_ge(t_done, CREDIT + n * NPAIR + (q + 1))
                    act.copy(fT3[:, :, a * P:z * P],
                             banks[T_BANK[q]][:, 0:(z - a) * C].rearrange("p (k n) -> p k n", k=KC))\
                        .then_inc(t_evac, 1)

            def router_hidden(i):
                act.wait_ge(lg_done, CREDIT + i)
                for h in range(2):
                    act.wait_ge(rh_done, i * 2 + (h + 1))
                    act.activation(rhT[:, h * FH:(h + 1) * FH], banks[5 + h][:, 0:FH], ACT.Relu,
                                   bias=rb1).then_inc(rh_ready, 1)
            features_in(0)
            with act.Fori(0, BODIES - 1) as i:
                router_hidden(i)
                features_in(i + 1)
            router_hidden(BODIES - 1)
            for k in range(2):
                act.wait_ge(soft_in, k + 1)
                act.activation(gates, gates, ACT.Exp).then_inc(soft_exp, 1)

            def features_out(n, b):
                after(act, fx_done, n + 1)
                after(act, h1_done, n - 1)
                act.copy(fT[b % 2], banks[b % 2][:, 0:C]).then_inc(fx_ready, 1)

            def hidden_out(n, b, w, dst, done, ready, used):
                after(act, done, n + 1)
                after(act, used, n - 1)
                for m in range(KC):
                    at = 3 * KC * C + w * KC + m
                    ins = act.activation(dst[b % 2][:, m * P:(m + 1) * P],
                                         banks[2 + 2 * w + b % 2][:, m * P:(m + 1) * P], ACT.Relu,
                                         bias=wbuf[b % WBUFS][:, at:at + 1])
                ins.then_inc(ready, 1)

            def act_slot(n, b, first=0, last=WBUFS):
                if first <= 0 < last:
                    features_out(n, b)
                if first <= 1 < last:
                    hidden_out(n - 1, b - 1, 0, h1T, h1_done, h1_ready, h2_done)
                if first <= 2 < last:
                    hidden_out(n - 2, b - 2, 1, h2T, h2_done, h2_ready, y_done)

            for b in range(UNROLL):
                act_slot(b, b, last=b + 1)
            with act.Fori(0, ESTEPS - 1) as i:
                for b in range(UNROLL):
                    act_slot((i + 1) * UNROLL + b, b)
            for b in range(2):
                act_slot(ETILES + b, b, first=b + 1)

            for i in range(BODIES):
                act.wait_ge(body_done, CREDIT + i + 1)
                act.dma_start(out_tiles[:, i * BODY:(i + 1) * BODY, :],
                              x2_all[:, i * BODY:(i + 1) * BODY, :]).then_inc(out_stored, 16)

        @block.tensor
        def _(pe):
            pe.wait_ge(consts, N_CONSTS)
            pe.sem_inc(summed, RING)
            for semaphore in credited:
                pe.sem_inc(semaphore, CREDIT)

            pe.wait_ge(cnt_ready, NT)
            pe.matmul(banks[0][0:NT, 0:1], cnt[:, :], ones[:, 0:1], start=True, stop=True)\
                .then_inc(runs_counted, 1)
            pe.wait_ge(run_sizes, 1)
            pe.matmul(banks[1][:, 0:NT], run_wide, lower[0:NT, 0:NT], start=True, stop=False)
            pe.matmul(banks[1][:, 0:NT], lower, cnt[:, :], start=False, stop=True)
            pe.matmul(banks[2][0:NT, 0:1], lower_eq[0:NT, 0:NT], run_tiles[:, :],
                      start=True, stop=True).then_inc(base_sum, 1)

            def transposes(n, t_bank=T_BANK):
                for q, (a, z) in enumerate(PAIRS):
                    pe.wait_ge(u_ready, n * BODY + z)
                    pe.wait_ge(t_evac, CREDIT + t_freed(n, q, t_bank))
                    for t in range(a, z):
                        for k in range(KC):
                            at = ((t - a) * KC + k) * P
                            ins = pe.transpose(banks[t_bank[q]][:, at:at + P],
                                               u3[:, t, k * P:(k + 1) * P], ident[:, :])
                    ins.then_inc(t_done, 1)

            def g_products(n, w, ready):
                for q, (a, z) in enumerate(PAIRS):
                    pe.wait_ge(ready, CREDIT + n * NPAIR + (q + 1))
                    pe.wait_ge(g_evac, CREDIT + n * NPAIR + (1 if q == 3 else 0))
                    for t in range(a, z):
                        for k in range(KC):
                            ins = pe.matmul(banks[G_BANK[q]][:, (t - a) * C:(t - a + 1) * C],
                                            hr4[:, t, k], wg[:, bass.ds(w * (KC * C) + k * C, C)],
                                            start=(k == 0), stop=(k == KC - 1))
                    ins.then_inc(g_done, 1)

            def with_zeros(bank, width, opens):
                return pe.matmul(banks[bank][:, 0:width], ident[:, :],
                                 zeros[:, :].to_broadcast([P, width]), start=opens,
                                 stop=not opens, skip_group_check=True)

            pe.wait_ge(weights_in, 16 * (2 + 2 * LAYERS + 2))
            with pe.Fori(0, BODIES) as i:
                transposes(i, IN_BANK)
                for q, (a, z) in enumerate(PAIRS):
                    pe.wait_ge(t_evac, CREDIT + i * NPAIR + (q + 1))
                    pe.wait_ge(m_evac, CREDIT + i * NPAIR + (1 if q == 3 else 0))
                    for t in range(a, z):
                        for m in range(KC):
                            at = ((t - a) * KC + m) * P
                            for k in range(KC):
                                ins = pe.matmul(banks[M_BANK[q]][:, at:at + P],
                                                win3[:, k, m * P:(m + 1) * P], xr4[:, t, k],
                                                start=(k == 0), stop=(k == KC - 1))
                    ins.then_inc(m_done, 1)
                g_products(i, 0, m_evac)

            pe.wait_ge(g_evac, CREDIT + NPAIR * BODIES)
            for part in range(2):
                for k, (a, z) in enumerate(SPLIT):
                    with_zeros(2 * part + k, z - a, True)
            pe.sem_inc(p_used, PERM)
            with pe.Fori(0, PE_COLS // PERM) as i:
                for b in range(PERM):
                    pe.wait_ge(p_ready, i * PERM + (b + 2))
                    for part in range(2):
                        for k, (a, z) in enumerate(SPLIT):
                            ins = pe.matmul(banks[2 * part + k][:, 0:z - a], p_lo[:, b, part],
                                            p_hi[:, b, a:z], start=False, stop=False,
                                            skip_group_check=True)
                    ins.then_inc(p_used, 1)
            for part in range(2):
                for k, (a, z) in enumerate(SPLIT):
                    ins = with_zeros(2 * part + k, z - a, False)
            ins.then_inc(p_used, 1)
            pe.wait_ge(past_ready, 1)
            for k, (a, z) in enumerate(SPLIT):
                ins = pe.matmul(banks[6 + k][:, 0:z - a], ones[0:NT, :], past[0:NT, a:z],
                                start=True, stop=True)
            ins.then_inc(node_sum, 1)

            def gather_layer(l):
                with pe.Fori(0, STEPS) as i:
                    n = l * STEPS + i
                    for b in range(RING):
                        pe.wait_ge(gathered[b], n * 16 + 16)
                        if b == 0:
                            pe.wait_ge(onehot_ready, n * 2 + 1)
                        if b == HALF:
                            pe.wait_ge(onehot_ready, n * 2 + 2)
                        pe.wait_ge(drained, n * RING + (b + 1))
                        pe.matmul(banks[bank_of(b)][:, 0:AW], onehot3[:, b], gath3[:, b],
                                  start=True, stop=True).then_inc(summed, 1)
                        if b == RING // 2:
                            pe.wait_ge(selfT_ready, n + 1)
                            pe.wait_ge(self_evac, CREDIT + n)
                            for k in range(KC):
                                ins = pe.matmul(banks[5][:, 0:C], hs3[:, k],
                                                ws[:, bass.ds(l * (KC * C) + k * C, C)],
                                                start=(k == 0), stop=(k == KC - 1))
                            ins.then_inc(self_done, 1)

            def finish_layer(l):
                with pe.Fori(0, BODIES) as i:
                    n = l * BODIES + i + BODIES
                    transposes(n)
                    g_products(n, l + 1, t_evac)

            with pe.Fori(0, LAYERS - 1) as l:
                gather_layer(l)
                finish_layer(l)
            gather_layer(LAYERS - 1)
            finish_layer(LAYERS - 1)

            pe.wait_ge(ffn_weights, 16 * FFN_LOADS)
            pe.wait_ge(g_evac, CREDIT + NPAIR * BODIES * (LAYERS + 1))
            def turn_features(i, ring):
                n = i + (LAYERS + 1) * BODIES
                for q, (a, z) in enumerate(PAIRS):
                    pe.wait_ge(u_ready, n * BODY + z)
                    pe.wait_ge(t_evac, CREDIT + t_freed(n, q))
                    for t in range(a, z):
                        for k in range(KC):
                            at = (k * (z - a) + t - a) * P
                            ins = pe.transpose(banks[T_BANK[q]][:, at:at + P],
                                               ring[:, t, k * P:(k + 1) * P], ident[:, :])
                    ins.then_inc(t_done, 1)

            def router_products(i):
                pe.wait_ge(t_evac, CREDIT + (i + (LAYERS + 1) * BODIES) * NPAIR + NPAIR)
                pe.wait_ge(rh_ready, CREDIT + i * 2)
                for h in range(2):
                    for k in range(KC):
                        ins = pe.matmul(banks[5 + h][:, 0:FH], rw1[:, k],
                                        fT_ring[:, k * 2 * FH + h * FH:k * 2 * FH + (h + 1) * FH],
                                        start=(k == 0), stop=(k == KC - 1))
                    ins.then_inc(rh_done, 1)

            def logit_products(i):
                pe.wait_ge(rh_ready, CREDIT + i * 2 + 2)
                pe.wait_ge(lg_evac, CREDIT + i)
                for t in range(BODY):
                    ins = pe.matmul(banks[7][:, t * EXPERTS:(t + 1) * EXPERTS],
                                    rhT[:, t * P:(t + 1) * P], rw2, start=True, stop=True)
                ins.then_inc(lg_done, 1)

            turn_features(0, f_rings[0])
            with pe.Fori(0, BODIES // 2) as j:
                for r in range(2):
                    router_products(j * 2 + r)
                    turn_features(j * 2 + r + 1, f_rings[1 - r])
                    logit_products(j * 2 + r)
            router_products(BODIES - 1)
            logit_products(BODIES - 1)

            pe.wait_ge(e_consts, 5)
            pe.wait_ge(ecnt_ready, 1)
            pe.matmul(banks[0][0:EXPERTS, 0:1], ecnt, e_ones[:, 0:1], start=True, stop=True)\
                .then_inc(experts_counted, 1)
            pe.wait_ge(e_sizes, 1)
            pe.matmul(banks[1][:, 0:EXPERTS], e_wide, e_lower[0:EXPERTS, 0:EXPERTS],
                      start=True, stop=False)
            pe.matmul(banks[1][:, 0:EXPERTS], e_lower, ecnt, start=False, stop=True)
            pe.matmul(banks[2][0:EXPERTS, 0:1], e_lower_eq[0:EXPERTS, 0:EXPERTS],
                      run_tiles[0:EXPERTS, :], start=True, stop=True).then_inc(ebase_sum, 1)
            pe.matmul(banks[3][:, 0:ETILES], ident[:, :], zeros[:, :].to_broadcast([P, ETILES]),
                      start=True, stop=False, skip_group_check=True)
            pe.sem_inc(item_used, 2 * EROW)
            with pe.Fori(0, ITEMS // EROW // 2) as i:
                for r in range(2):
                    pe.wait_ge(item_ready, (i * 2 + r) * 2 + 2)
                    pe.wait_ge(item_valued, i * 2 + (r + 1))
                    for b in range(EROW):
                        pe.matmul(banks[3][:, 0:ETILES], item_lo[r][:, b], item_hi[r][:, b],
                                  start=False, stop=False, skip_group_check=True)\
                            .then_inc(item_used, 1)
            pe.matmul(banks[3][:, 0:ETILES], ident[:, :], zeros[:, :].to_broadcast([P, ETILES]),
                      start=False, stop=True, skip_group_check=True)
            pe.matmul(banks[4][:, 0:ETILES], e_ones[0:EXPERTS, :], e_past, start=True, stop=True)\
                .then_inc(item_used, 1)

            def turn(n, b, step):
                pe.wait_ge(gathered[b], (step + LAYERS * STEPS + 1) * 16)
                after(pe, fx_ready, n - 1)
                for k in range(KC):
                    ins = pe.transpose(banks[b % 2][:, k * P:(k + 1) * P],
                                       f_in[b][:, k * P:(k + 1) * P], ident[:, :])
                ins.then_inc(fx_done, 1)

            def hidden(n, b, w, src, src_ready, done, bank_read):
                after(pe, src_ready, n + 1)
                if w == 0:
                    after(pe, words_ready, n + 1)
                after(pe, bank_read, n - 1)
                for m in range(KC):
                    for k in range(KC):
                        at = w * KC * C + k * C + m * P
                        ins = pe.matmul(banks[2 + 2 * w + b % 2][:, m * P:(m + 1) * P],
                                        wbuf[b % WBUFS][:, at:at + P],
                                        src[b % 2][:, k * P:(k + 1) * P],
                                        start=(k == 0), stop=(k == KC - 1))
                ins.then_inc(done, 1)

            def rows_out(n, b):
                after(pe, h2_ready, n + 1)
                after(pe, y_ready, n - 1)
                for k in range(KC):
                    at = 2 * KC * C + k * C
                    ins = pe.matmul(banks[6 + b % 2][:, 0:C], h2T[b % 2][:, k * P:(k + 1) * P],
                                    wbuf[b % WBUFS][:, at:at + C], start=(k == 0), stop=(k == KC - 1))
                ins.then_inc(y_done, 1)

            def pe_slot(n, b, step, first=0, last=WBUFS):
                if first <= 0 < last:
                    turn(n, b, step)
                if first <= 1 < last:
                    hidden(n - 1, b - 1, 0, fT, fx_ready, h1_done, h1_ready)
                if first <= 2 < last:
                    hidden(n - 2, b - 2, 1, h1T, h1_ready, h2_done, h2_ready)
                if first <= 3 < last:
                    rows_out(n - 3, b - 3)

            pe.wait_ge(tables_ready, 1)
            for b in range(UNROLL):
                pe_slot(b, b, 0, last=b + 1)
            with pe.Fori(0, ESTEPS - 1) as i:
                for b in range(UNROLL):
                    pe_slot((i + 1) * UNROLL + b, b, i + 1)
            for b in range(3):
                pe_slot(ETILES + b, b, 0, first=b + 1)

        @block.vector
        def _(dve):
            steps = [0]

            def link(ins):
                steps[0] += 1
                ins.then_inc(dve_step, 1)
                dve.wait_ge(dve_step, steps[0])

            dve.wait_ge(edges_in, 32)
            link(nc.vector.tensor_scalar(tile_i, edge_t, 7, None, ALU.arith_shift_right))
            link(nc.vector.tensor_copy(tile_h, tile_i))
            for b in range(NT):
                if b >= len(masks):
                    dve.wait_ge(cnt_ready, b - len(masks) + 1)
                nc.vector.tensor_scalar(masks[b % len(masks)], tile_h, float(b), 0.0,
                                        ALU.is_equal, ALU.add, accum_out=cnt[:, b:b + 1])\
                    .then_inc(cnt_ready, 1)
            link(nc.vector.tensor_scalar(tile_i, edge_s, 3, None, ALU.arith_shift_right))
            link(nc.vector.tensor_copy(part_a, tile_i))
            link(nc.vector.tensor_scalar(temp_i, edge_s, 7, 7, ALU.bitwise_and,
                                         ALU.logical_shift_left))
            link(nc.vector.tensor_scalar(edge_t, edge_t, P - 1, None, ALU.bitwise_and))
            link(nc.vector.tensor_tensor(temp_i, temp_i, edge_t, ALU.add))
            link(nc.vector.tensor_scalar(part_b, temp_i, 1.0, None, ALU.add))

            dve.wait_ge(runs_counted, 1)
            link(nc.vector.tensor_scalar(run_i[:, :], banks[0][0:NT, 0:1], float(P - 1), None, ALU.add))
            link(nc.vector.tensor_scalar(run_j[:, :], run_i[:, :], 7, None, ALU.arith_shift_right))
            link(nc.vector.tensor_copy(run_tiles[:, :], run_j[:, :]))
            dve.wait_ge(consts, N_CONSTS)
            nc.vector.tensor_scalar(run_wide, ones[0:NT, :], run_tiles[:, 0:1], float(P),
                                    ALU.mult, ALU.mult).then_inc(run_sizes, 1)
            dve.wait_ge(base_sum, 1)
            link(nc.vector.tensor_copy(base[:, :], banks[1][:, 0:NT]))
            link(nc.vector.tensor_copy(run_end[:, :], banks[2][0:NT, 0:1]))

            def row_stats(rows):
                for t in range(NT):
                    ins = nc.vector.bn_stats(stats[:, t * 6:(t + 1) * 6], rows(t))
                link(ins)
                row_spreads(stats)

            def row_spreads(stats):
                for t in range(NT):
                    ins = nc.vector.bn_aggr(mv[:, 2 * t:2 * t + 2], stats[:, t * 6:(t + 1) * 6])
                ins.then_inc(var_ready, 1)

            def row_scales(n):
                dve.wait_ge(std_ready, n)
                link(nc.vector.reciprocal(rstd[:, :], rstd[:, :]))
                return nc.vector.scalar_tensor_tensor(nmr[:, :], mv3[:, :, 0], -1.0, rstd[:, :],
                                                      ALU.mult, ALU.mult)

            dve.wait_ge(x_loaded, 16 * BODIES)
            row_stats(lambda t: acc3[:, t, 0:C])
            row_scales(1).then_inc(stats_ready, 1)

            link(nc.vector.memset(pos_sum, 0.0))
            link(nc.vector.memset(cums[2], 0.0))
            dve.sem_inc(msk_ready, 1)

            def make_mask(i, b):
                nc.vector.tensor_scalar(masks[mask_of(b % BODY)], tile_h,
                                        iota_f[:, bass.ds(i * BODY + b, 1)], None,
                                        ALU.is_equal).then_inc(mask_ready, 1)

            def add_counts(b):
                return nc.vector.tensor_tensor(pos_sum, pos_sum, cums[cum_of(b)], ALU.add)

            make_mask(0, 0)
            with dve.Fori(0, BODIES) as i:
                for b in range(BODY):
                    n = i * BODY + b
                    make_mask(i, b + 1)
                    go(dve, pos_added, CREDIT + n)
                    dve.wait_ge(mask_ready, n + 1)
                    mask = masks[mask_of(b)]
                    nc.vector.tensor_tensor_scan(cums[cum_of(b)], mask, mask,
                                                 base[:, bass.ds(i * BODY + b, 1)],
                                                 ALU.add, ALU.bypass).then_inc(cum_ready, 1)
                    dve.wait_ge(msk_ready, n + 1)
                    add_counts((b - 1) % BODY).then_inc(pos_added, 1)

            dve.wait_ge(pos_added, CREDIT + NT)
            dve.wait_ge(msk_ready, NT + 1)
            link(add_counts(BODY - 1))
            dve.wait_ge(m_done, NPAIR * BODIES)
            slot_i, temp_j = (cums[r].bitcast(I32) for r in range(2))
            link(nc.vector.tensor_scalar(slot_i, pos_sum, -1.0, None, ALU.add))
            link(nc.vector.tensor_scalar(temp_j, slot_i, 7, None, ALU.arith_shift_right))
            link(nc.vector.tensor_copy(pos_hi, temp_j))
            link(nc.vector.tensor_scalar(temp_j, slot_i, P - 1, None, ALU.bitwise_and))
            link(nc.vector.tensor_copy(pos_lo, temp_j))
            tail = slice(PE_COLS, COLS)
            link(nc.vector.tensor_scalar(sc_rec, part_a[:, tail], 1024.0, None, ALU.mult))
            link(nc.vector.tensor_tensor(sc_rec, sc_rec, part_b[:, tail], ALU.add))
            link(nc.vector.tensor_scalar(sc_slot, pos_lo[:, tail], float(SLOTS), None, ALU.mult))
            link(nc.vector.tensor_tensor(sc_slot, sc_slot, pos_hi[:, tail], ALU.add))
            link(nc.vector.tensor_scalar(sc_temp, pos_hi[:, tail], 0.0, None, ALU.is_lt))
            dve.wait_ge(sc_base, 1)
            link(nc.vector.tensor_tensor(sc_pad, sc_pad, sc_slot, ALU.subtract))
            link(nc.vector.tensor_tensor(sc_pad, sc_pad, sc_temp, ALU.mult))
            nc.vector.tensor_tensor(sc_slot, sc_slot, sc_pad, ALU.add).then_inc(sc_tables, 1)
            dve.sem_inc(p_ready, 1)
            with dve.Fori(0, PE_COLS // PERM) as i:
                for b in range(PERM):
                    dve.wait_ge(p_used, i * PERM + (b + 1))
                    at = bass.ds(i * PERM + b, 1)
                    for part, value in enumerate((part_a, part_b)):
                        nc.vector.tensor_scalar(p_lo[:, b, part], iota_h[:, 0:P], pos_lo[:, at],
                                                value[:, at], ALU.is_equal, ALU.mult)
                    nc.vector.tensor_scalar(p_hi[:, b], iota_h, pos_hi[:, at], None,
                                            ALU.is_equal).then_inc(p_ready, 1)

            nc.vector.tensor_scalar(past[0:NT, :], iota_h[0:NT, 0:SLOTS], run_end[:, 0:1], None,
                                    ALU.is_ge).then_inc(past_ready, 1)
            dve.wait_ge(p_used, PE_COLS + PERM + 1)
            for k, (a, z) in enumerate(SPLIT):
                link(nc.vector.tensor_scalar(dec_a[:, a:z], banks[k][:, 0:z - a], 1024.0, None,
                                             ALU.mult))
                link(nc.vector.tensor_tensor(dec_a[:, a:z], dec_a[:, a:z], banks[2 + k][:, 0:z - a],
                                             ALU.add))
            dve.wait_ge(table_in, 16)
            link(nc.vector.tensor_tensor(dec_a, dec_a, scattered_recs, ALU.add))
            link(nc.vector.tensor_scalar(dec_bi, dec_a, -1.0, None, ALU.add))
            link(nc.vector.tensor_scalar(dec_ci, dec_bi, 7, None, ALU.arith_shift_right))
            link(nc.vector.tensor_scalar(slot_src, dec_ci, 0.0, None, ALU.max))
            link(nc.vector.tensor_scalar(dec_d, dec_bi, 0.0, 1000.0, ALU.is_lt, ALU.mult))
            link(nc.vector.tensor_scalar(dec_ci, dec_bi, P - 1, None, ALU.bitwise_and))
            link(nc.vector.tensor_tensor(slot_tgt, dec_d, dec_ci, ALU.add))
            dve.wait_ge(node_sum, 1)
            for k, (a, z) in enumerate(SPLIT):
                link(nc.vector.tensor_scalar(slot_node[:, a:z], banks[6 + k][0:1, 0:z - a],
                                             float(NT - 1), None, ALU.min))
            dve.sem_inc(drained, 4)
            dve.sem_inc(slots_ready, 1)

            def gather_layer(l):
                dve.wait_ge(acc_zeroed, l * BODIES + BODIES)
                dve.wait_ge(h_kept, CREDIT + l * BODIES + BODIES)
                go(dve, g_evac, CREDIT + l * (BODIES * NPAIR) + BODIES * NPAIR)
                with dve.Fori(0, STEPS) as i:
                    n = l * STEPS + i
                    _, nodes = nc.values_load_multi_w_load_instructions(
                        slot_node[:, bass.ds(i * RING, RING)], engines=(mybir.EngineType.DVE,),
                        min_val=0, max_val=NT - 1,
                        skip_runtime_bounds_check_because="the table was cut to this range")
                    for a, z in HALVES:
                        dve.wait_ge(summed, n * RING + z)
                        nc.vector.tensor_tensor(
                            onehot3[:, a:z],
                            iota_f[:, :].unsqueeze(1).to_broadcast([P, z - a, P]),
                            slot_tgt[:, bass.ds(i * RING + a, z - a)].unsqueeze(2)
                            .to_broadcast([P, z - a, P]), ALU.is_equal).then_inc(onehot_ready, 1)
                    for b in range(RING):
                        dve.wait_ge(drained, n * RING + (b + 4))
                        dve.wait_ge(summed, n * RING + (b + 1 + RING))
                        row = bass.ds(nodes[b] * AW, AW)
                        nc.vector.tensor_tensor(acc[:, row], acc[:, row],
                                                banks[bank_of(b)][:, 0:AW], ALU.add)\
                            .then_inc(drained, 1)
                dve.wait_ge(drained, l * SLOTS + (SLOTS + 4))
                dve.wait_ge(self_evac, CREDIT + l * STEPS + STEPS)
                nc.vector.tensor_scalar(rdeg[:, :], acc3[:, :, C], 1.0, None, ALU.max)\
                    .then_inc(deg_step, 1)
                dve.wait_ge(deg_step, l * 2 + 1)
                nc.vector.reciprocal(rdeg[:, :], rdeg[:, :]).then_inc(deg_step, 1)
                go(dve, deg_step, l * 2 + 2)

            def u_rows(i, n):
                dve.wait_ge(t_done, CREDIT + n * NPAIR)
                for b in range(BODY):
                    nc.vector.scalar_tensor_tensor(
                        u3[:, b], acc[:, bass.ds(i * (BODY * AW) + b * AW, C)],
                        rdeg[:, bass.ds(i * BODY + b, 1)],
                        selfp[:, bass.ds(i * (BODY * C) + b * C, C)],
                        ALU.mult, ALU.add).then_inc(u_ready, 1)

            def g_rows(n):
                dve.wait_ge(g_free, CREDIT + n)
                for q, (a, z) in enumerate(PAIRS):
                    dve.wait_ge(g_done, NPAIR * n + (q + 1))
                    nc.vector.tensor_copy(g_ring[:, a * C:z * C], banks[G_BANK[q]][:, 0:(z - a) * C])\
                        .then_inc(g_evac, 1)

            def finish_layer(l):
                first = l * BODIES + BODIES
                u_rows(0, first)
                with dve.Fori(0, BODIES - 1) as i:
                    u_rows(i + 1, first + i + 1)
                    g_rows(first + i)
                g_rows(first + BODIES - 1)

            with dve.Fori(0, LAYERS - 1) as l:
                gather_layer(l)
                finish_layer(l)
            gather_layer(LAYERS - 1)

            def x2_rows(i):
                n = i + LAYERS * BODIES
                dve.wait_ge(x_reloaded, i * 16 + 16)
                for q, (a, z) in enumerate(PAIRS):
                    dve.wait_ge(g_done, NPAIR * n + (q + 1))
                    nc.vector.tensor_tensor(selfp[:, bass.ds(i * (BODY * C) + a * C, (z - a) * C)],
                                            x_in[:, a * C:z * C], banks[G_BANK[q]][:, 0:(z - a) * C],
                                            ALU.add).then_inc(g_evac, 1)
                here = x2_all[:, bass.ds(i * BODY, BODY), :]
                dve.wait_ge(g_evac, CREDIT + n * NPAIR + NPAIR)
                nc.vector.tensor_tensor(here, here,
                                        bout_t.unsqueeze(1).to_broadcast([P, BODY, C]), ALU.add)\
                    .then_inc(x_used, 1)
                go(dve, x_used, CREDIT + i + 1)
                for b in range(BODY):
                    ins = nc.vector.bn_stats(e_stats[:, bass.ds(i * (BODY * 6) + b * 6, 6)],
                                             selfp[:, bass.ds(i * (BODY * C) + b * C, C)])
                ins.then_inc(x2_ready, 1)

            dve.wait_ge(bout_in, 16)
            u_rows(0, LAYERS * BODIES)
            with dve.Fori(0, BODIES - 1) as i:
                u_rows(i + 1, i + 1 + LAYERS * BODIES)
                x2_rows(i)
            x2_rows(BODIES - 1)
            dve.wait_ge(x2_ready, BODIES)
            row_spreads(e_stats)
            dve.wait_ge(ffn_weights, 16 * FFN_LOADS)
            link(row_scales(2))
            def feature_rows(i, ring, before):
                n = i + (LAYERS + 1) * BODIES
                dve.wait_ge(t_done, CREDIT + (n + 1 - before) * NPAIR)
                go(dve, f_free, CREDIT + i + 1 - before)
                for b in range(BODY):
                    nc.vector.tensor_scalar(ring[:, b], selfp[:, bass.ds(i * (BODY * C) + b * C, C)],
                                            rstd[:, bass.ds(i * BODY + b, 1)],
                                            nmr[:, bass.ds(i * BODY + b, 1)],
                                            ALU.mult, ALU.add).then_inc(u_ready, 1)

            def logits_in(i):
                dve.wait_ge(lg_done, CREDIT + i + 1)
                nc.vector.tensor_tensor(lg3[:, bass.ds(i * BODY, BODY), :],
                                        banks[7][:, 0:BODY * EXPERTS]
                                        .rearrange("p (t e) -> p t e", e=EXPERTS),
                                        rb2.unsqueeze(1).to_broadcast([P, BODY, EXPERTS]),
                                        ALU.add).then_inc(lg_evac, 1)

            feature_rows(0, f_rings[0], 1)
            with dve.Fori(0, BODIES // 2) as j:
                for r in range(2):
                    feature_rows(j * 2 + r + 1, f_rings[1 - r], 2)
                    logits_in(j * 2 + r)
            logits_in(BODIES - 1)

            wide = top3.to_broadcast([P, NT, EXPERTS])
            dve.wait_ge(lg_evac, CREDIT + BODIES)
            link(nc.vector.tensor_reduce(topv, lg3, AX.X, ALU.max))
            nc.vector.tensor_tensor(gt3, lg3, wide, ALU.subtract).then_inc(soft_in, 1)
            dve.wait_ge(soft_exp, 1)
            link(nc.vector.tensor_reduce(topv, gt3, AX.X, ALU.add))
            link(nc.vector.reciprocal(topv, topv))
            link(nc.vector.tensor_tensor(gt3, gt3, wide, ALU.mult))
            link(nc.vector.memset(rank, 0.0))
            for o in range(EXPERTS):
                if o > 0:
                    link(nc.vector.tensor_tensor(bt3[:, :, 0:o],
                                                 gt3[:, :, o:o + 1].to_broadcast([P, NT, o]),
                                                 gt3[:, :, 0:o], ALU.is_gt))
                    link(nc.vector.tensor_tensor(rk3[:, :, 0:o], rk3[:, :, 0:o], bt3[:, :, 0:o],
                                                 ALU.add))
                if o < EXPERTS - 1:
                    r = EXPERTS - 1 - o
                    link(nc.vector.tensor_tensor(bt3[:, :, o + 1:],
                                                 gt3[:, :, o:o + 1].to_broadcast([P, NT, r]),
                                                 gt3[:, :, o + 1:], ALU.is_ge))
                    link(nc.vector.tensor_tensor(rk3[:, :, o + 1:], rk3[:, :, o + 1:],
                                                 bt3[:, :, o + 1:], ALU.add))
            by_expert = rk3.rearrange("p t e -> p e t")
            for k in range(TOP_K):
                link(nc.vector.tensor_scalar(ch3[:, :, k * NT:(k + 1) * NT], by_expert, float(k), None,
                                             ALU.is_equal))
            nc.vector.tensor_reduce(ecnt, ch3, AX.X, ALU.add).then_inc(ecnt_ready, 1)
            dve.wait_ge(experts_counted, 1)
            link(nc.vector.tensor_scalar(run_i[0:EXPERTS, :], banks[0][0:EXPERTS, 0:1], float(P - 1),
                                         None, ALU.add))
            link(nc.vector.tensor_scalar(run_j[0:EXPERTS, :], run_i[0:EXPERTS, :], 7, None,
                                         ALU.arith_shift_right))
            link(nc.vector.tensor_copy(run_tiles[0:EXPERTS, :], run_j[0:EXPERTS, :]))
            nc.vector.tensor_scalar(e_wide, e_ones[0:EXPERTS, :], run_tiles[0:EXPERTS, 0:1], float(P),
                                    ALU.mult, ALU.mult).then_inc(e_sizes, 1)
            dve.wait_ge(ebase_sum, 1)
            link(nc.vector.tensor_copy(ebase, banks[1][:, 0:EXPERTS]))
            link(nc.vector.tensor_copy(run_end[0:EXPERTS, :], banks[2][0:EXPERTS, 0:1]))
            for e in range(EXPERTS):
                ins = nc.vector.tensor_tensor_scan(ra3[:, e], ch3[:, e], ch3[:, e], ebase[:, e:e + 1],
                                                   ALU.add, ALU.bypass)
            link(ins)
            link(nc.vector.tensor_tensor(ranked, ranked, chosen, ALU.mult))
            link(nc.vector.tensor_reduce(eslot_lo, ra3.rearrange("p e j -> p j e"), AX.X, ALU.add))
            link(nc.vector.tensor_scalar(eslot_i, eslot_lo, -1.0, None, ALU.add))
            link(nc.vector.tensor_scalar(etemp_i, eslot_i, 7, None, ALU.arith_shift_right))
            link(nc.vector.tensor_copy(eslot_hi, etemp_i))
            link(nc.vector.tensor_scalar(etemp_i, eslot_i, P - 1, None, ALU.bitwise_and))
            link(nc.vector.tensor_copy(eslot_lo, etemp_i))
            link(nc.vector.tensor_scalar(e_past, iota_f[0:EXPERTS, 0:ETILES],
                                         run_end[0:EXPERTS, 0:1], None, ALU.is_ge))
            with dve.Fori(0, ITEMS // EROW // 2) as i:
                for r in range(2):
                    dve.wait_ge(item_used, (i * 2 + r) * EROW + EROW)
                    at = bass.ds((i * 2 + r) * EROW, EROW)
                    for onehots, slots, width in ((item_hi[r], eslot_hi, ETILES),
                                                  (item_lo[r], eslot_lo, P)):
                        nc.vector.tensor_tensor(
                            onehots, iota_f[:, 0:width].unsqueeze(1).to_broadcast([P, EROW, width]),
                            slots[:, at].unsqueeze(2).to_broadcast([P, EROW, width]),
                            ALU.is_equal).then_inc(item_ready, 1)
            dve.wait_ge(item_used, ITEMS + 2 * EROW + 1)
            link(nc.vector.tensor_scalar(item_i, banks[3][:, 0:ETILES], -1.0, None, ALU.add))
            link(nc.vector.tensor_scalar(etest_i, item_i, float(NT * P), float(-NT * P),
                                         ALU.is_ge, ALU.mult))
            link(nc.vector.tensor_tensor(node_i, item_i, etest_i, ALU.add))
            link(nc.vector.tensor_scalar(node_i, node_i, 0.0, None, ALU.max))
            link(nc.vector.tensor_scalar(etest_i, item_i, 0.0, None, ALU.is_lt))
            link(nc.vector.tensor_scalar(pad_i, pad_i, 1.0, None, ALU.add))
            link(nc.vector.tensor_tensor(pad_i, pad_i, etest_i, ALU.mult))
            link(nc.vector.tensor_tensor(item_i, item_i, pad_i, ALU.add))
            link(nc.vector.tensor_scalar(tile_expert, banks[4][0:1, 0:ETILES], float(EXPERTS - 1),
                                         None, ALU.min))
            dve.sem_inc(tables_ready, 1)

            link(nc.vector.tensor_scalar(rank, rank, float(TOP_K), None, ALU.is_lt))
            link(nc.vector.tensor_reduce(topv, gt3, AX.X, ALU.max))
            nc.vector.tensor_tensor(gt3, gt3, wide, ALU.subtract).then_inc(soft_in, 1)
            dve.wait_ge(soft_exp, 2)
            link(nc.vector.tensor_tensor(gates, gates, rank, ALU.mult))
            link(nc.vector.tensor_reduce(topv, gt3, AX.X, ALU.add))
            link(nc.vector.reciprocal(topv, topv))
            link(nc.vector.tensor_tensor(gt3, gt3, wide, ALU.mult))

            for k in range(TOP_K):
                picked = ch3[:, :, k * NT:(k + 1) * NT].rearrange("p e t -> p t e")
                link(nc.vector.tensor_tensor(bt3, gt3, picked, ALU.mult))
                link(nc.vector.tensor_reduce(gate[k], bt3, AX.X, ALU.add))

            def words_in(n, b, expert):
                after(dve, y_done, n - 3)
                after(dve, y_ready, n - 3)
                nc.vector.tensor_copy(wbuf[b % WBUFS], experts[:, bass.ds(expert * WEXP, WEXP)])\
                    .then_inc(words_ready, 1)

            def rows_in(n, b, step):
                after(dve, y_done, n + 1)
                dve.wait_ge(y_free[b // EHALF], CREDIT + step)
                nc.vector.tensor_tensor(y_out[b], banks[6 + b % 2][:, 0:C],
                                        wbuf[b % WBUFS][:, WEXP - C:WEXP], ALU.add)\
                    .then_inc(y_ready, 1)

            def load_experts(step):
                _, which = nc.values_load_multi_w_load_instructions(
                    tile_expert[:, bass.ds(step * UNROLL, UNROLL)],
                    engines=(mybir.EngineType.DVE,), min_val=0, max_val=EXPERTS - 1,
                    skip_runtime_bounds_check_because="the table was cut to this range")
                return which

            which = load_experts(0)
            for b in range(UNROLL):
                words_in(b, b, which[b])
                if b >= 3:
                    rows_in(b - 3, b - 3, 0)
            with dve.Fori(0, ESTEPS - 1) as i:
                which = load_experts(i + 1)
                for b in range(UNROLL):
                    words_in((i + 1) * UNROLL + b, b, which[b])
                    rows_in((i + 1) * UNROLL + b - 3, (b - 3) % UNROLL, i + 1 if b >= 3 else i)
            for b in range(3):
                rows_in(ETILES + b - 3, UNROLL + b - 3, ESTEPS - 1)

            for i in range(BODIES):
                dve.wait_ge(pairs_loaded[i % PBUFS], 16 * TOP_K * (i // PBUFS + 1))
                for k in range(TOP_K):
                    for t in range(i * BODY, (i + 1) * BODY):
                        ins = nc.vector.scalar_tensor_tensor(
                            x2_all[:, t], pairs_in[:, i % PBUFS, k, t - i * BODY], gate[k][:, t:t + 1],
                            x2_all[:, t], ALU.mult, ALU.add)
                    ins.then_inc(first_added if k == 0 else body_done, 1)
                    if k == 0:
                        dve.wait_ge(first_added, CREDIT + i + 1)


def kernel(x, src, dst, L0_gnn_W_in, L0_gnn_b_in, L0_gnn_W_agg, L0_gnn_W_self, L0_gnn_b_hid,
           L0_gnn_W_out, L0_gnn_b_out, L0_ffn_router_w1, L0_ffn_router_b1, L0_ffn_router_w2,
           L0_ffn_router_b2, L0_ffn_expert_w1, L0_ffn_expert_b1, L0_ffn_expert_w2,
           L0_ffn_expert_b2, L0_ffn_expert_w3, L0_ffn_expert_b3):
    import numpy as np
    import concourse.bacc as bacc
    from concourse.bass_utils import run_bass_kernel_spmd

    def padded(a, rows, fill):
        a = np.asarray(a)
        out = np.full((rows,) + a.shape[1:], fill, a.dtype)
        out[:a.shape[0]] = a
        return out

    arrays = {
        "in_x": padded(x, NT * P, 0),
        "in_tgt": padded(src, P * COLS, -1),
        "in_gat": padded(dst, P * COLS, 0),
    }
    for name, a in (("w_in", L0_gnn_W_in), ("b_in", L0_gnn_b_in), ("w_agg", L0_gnn_W_agg),
                    ("w_self", L0_gnn_W_self), ("b_hid", L0_gnn_b_hid), ("w_out", L0_gnn_W_out),
                    ("b_out", L0_gnn_b_out), ("r_w1", L0_ffn_router_w1),
                    ("r_b1", L0_ffn_router_b1), ("r_w2", L0_ffn_router_w2),
                    ("r_b2", L0_ffn_router_b2), ("e_w1", L0_ffn_expert_w1),
                    ("e_b1", L0_ffn_expert_b1), ("e_w2", L0_ffn_expert_w2),
                    ("e_b2", L0_ffn_expert_b2), ("e_w3", L0_ffn_expert_w3),
                    ("e_b3", L0_ffn_expert_b3)):
        arrays["in_" + name] = np.ascontiguousarray(np.asarray(a))

    nc = bacc.Bacc("TRN2", target_bir_lowering=False, num_devices=1)
    args = [nc.dram_tensor(n, a.shape, mybir.dt.from_np(a.dtype), kind="ExternalInput").ap()
            for n, a in arrays.items()]
    out = nc.dram_tensor("out_rows", (NT * P, C), F32, kind="ExternalOutput").ap()
    gnn_moe(nc, *args, out)
    r = run_bass_kernel_spmd(nc, [arrays], core_ids=[0])
    return r.results[0]["out_rows"][:NODES]
```
